# Optimizing a Trainium2 kernel written in Bass

```python
import numpy as np
import jax
import jax.numpy as jnp

def _softmax(x, axis=-1):
    return jax.nn.softmax(x, axis=axis)

def _gelu(x):
    return jax.nn.gelu(x, approximate=True)

def _silu(x):
    return jax.nn.silu(x)

def _sigmoid(x):
    return jax.nn.sigmoid(x)

def _layernorm(x, axis=-1, eps=1e-05):
    m = jnp.mean(x, axis=axis, keepdims=True)
    v = jnp.var(x, axis=axis, keepdims=True)
    return (x - m) / jnp.sqrt(v + eps)

def _scatter_add(tgt, idx, src, axis=0):
    return tgt.at[idx].add(src)

def _segment_sum(src, seg, n):
    return jax.ops.segment_sum(src, seg, n)
kernel_name = 'mk_seq_preln_d2_jaxref_r8_21b268'

def setup_inputs(seed: int=0):
    np.random.seed(seed)
    _w = jnp.asarray

    def _L0_attn_setup():
        import jax, jax.numpy as jnp
        import numpy as np
        B, T, D, S = (4, 256, 128, 64)
        EPS = 1e-08
        key = jax.random.key(seed)
        ks = jax.random.split(key, 6)
        return {'token_embeddings': jax.random.normal(ks[0], (B, T, D), dtype=jnp.float32), 'splat_positions': jax.random.normal(ks[1], (S, D), dtype=jnp.float32), 'splat_log_scales': jax.random.uniform(ks[2], (S,), dtype=jnp.float32), 'splat_amplitudes': jax.random.uniform(ks[3], (S,), dtype=jnp.float32), 'Wv': jax.random.normal(ks[4], (D, D), dtype=jnp.float32) / np.sqrt(D).astype(np.float32), 'Wo': jax.random.normal(ks[5], (D, D), dtype=jnp.float32) / np.sqrt(D).astype(np.float32)}
    _L0_attn_in = _L0_attn_setup()

    def _L0_ffn_setup():
        import jax, jax.numpy as jnp
        import numpy as np
        LN_EPS = 0.001
        EPS = 1e-05
        QB = 128.0

        def ste_round(x):
            return x + jax.lax.stop_gradient(jnp.round(x) - x)
        key = jax.random.key(seed)
        k1, k2 = jax.random.split(key)
        x = jax.random.normal(k1, (4, 1024, 128), dtype=jnp.float32)
        weight = jax.random.normal(k2, (128, 128), dtype=jnp.float32) * 0.02
        ln_gamma = jnp.ones((128,), dtype=jnp.float32)
        ln_beta = jnp.zeros((128,), dtype=jnp.float32)
        return {'x': x, 'weight': weight, 'ln_gamma': ln_gamma, 'ln_beta': ln_beta}
    _L0_ffn_in = _L0_ffn_setup()

    def _L1_attn_setup():
        import jax, jax.numpy as jnp
        import numpy as np
        B, S, E = (4, 256, 128)
        H, KVH = (16, 4)
        D = E // H
        QL, KVL = (64, 32)
        ROPE_BASE = 10000.0

        def _rope(x):
            d = x.shape[-1]
            inv_freq = 1.0 / ROPE_BASE ** (jnp.arange(0, d, 2, dtype=jnp.float32) / d)
            t = jnp.arange(x.shape[1], dtype=jnp.float32)
            freqs = jnp.outer(t, inv_freq)
            cos = jnp.cos(freqs)[None, :, None, :].astype(x.dtype)
            sin = jnp.sin(freqs)[None, :, None, :].astype(x.dtype)
            x1, x2 = (x[..., ::2], x[..., 1::2])
            r1 = x1 * cos - x2 * sin
            r2 = x1 * sin + x2 * cos
            return jnp.stack([r1, r2], axis=-1).reshape(x.shape)
        key = jax.random.key(seed)
        ks = jax.random.split(key, 7)
        s = 0.02
        return {'x': jax.random.normal(ks[0], (B, S, E), dtype=jnp.float32), 'Wqa': jax.random.normal(ks[1], (E, QL), dtype=jnp.float32) * s, 'Wqb': jax.random.normal(ks[2], (QL, E), dtype=jnp.float32) * s, 'Wkva': jax.random.normal(ks[3], (E, KVL), dtype=jnp.float32) * s, 'Wkvb': jax.random.normal(ks[4], (KVL, KVH * D * 2), dtype=jnp.float32) * s, 'Wout': jax.random.normal(ks[5], (E, E), dtype=jnp.float32) * s, 'bout': jax.random.normal(ks[6], (E,), dtype=jnp.float32) * s}
    _L1_attn_in = _L1_attn_setup()

    def _L1_ffn_setup():
        import jax, jax.numpy as jnp
        import numpy as np
        E = 16
        H = 128
        F = 256
        TOP_K = 1
        B, S = (2, 128)
        key = jax.random.key(seed)
        ks = jax.random.split(key, 7)
        s = 0.02
        return {'hidden_states': jax.random.normal(ks[0], (B, S, H), jnp.float32), 'w_router': jax.random.normal(ks[1], (E, H), jnp.float32) * s, 'gate_up_proj': jax.random.normal(ks[2], (E, H, 2 * F), jnp.float32) * s, 'down_proj': jax.random.normal(ks[3], (E, F, H), jnp.float32) * s, 'w_gate': jax.random.normal(ks[4], (F, H), jnp.float32) * s, 'w_up': jax.random.normal(ks[5], (F, H), jnp.float32) * s, 'w_down': jax.random.normal(ks[6], (H, F), jnp.float32) * s}
    _L1_ffn_in = _L1_ffn_setup()
    _d = {'L0_attn_token_embeddings': _L0_attn_in['token_embeddings'], 'L0_attn_splat_positions': _L0_attn_in['splat_positions'], 'L0_attn_splat_log_scales': _L0_attn_in['splat_log_scales'], 'L0_attn_splat_amplitudes': _L0_attn_in['splat_amplitudes'], 'L0_attn_Wv': _L0_attn_in['Wv'], 'L0_attn_Wo': _L0_attn_in['Wo'], 'L0_ffn_weight': _L0_ffn_in['weight'], 'L0_ffn_ln_gamma': _L0_ffn_in['ln_gamma'], 'L0_ffn_ln_beta': _L0_ffn_in['ln_beta'], 'L1_attn_Wqa': _L1_attn_in['Wqa'], 'L1_attn_Wqb': _L1_attn_in['Wqb'], 'L1_attn_Wkva': _L1_attn_in['Wkva'], 'L1_attn_Wkvb': _L1_attn_in['Wkvb'], 'L1_attn_Wout': _L1_attn_in['Wout'], 'L1_attn_bout': _L1_attn_in['bout'], 'L1_ffn_w_router': _L1_ffn_in['w_router'], 'L1_ffn_gate_up_proj': _L1_ffn_in['gate_up_proj'], 'L1_ffn_down_proj': _L1_ffn_in['down_proj'], 'L1_ffn_w_gate': _L1_ffn_in['w_gate'], 'L1_ffn_w_up': _L1_ffn_in['w_up'], 'L1_ffn_w_down': _L1_ffn_in['w_down']}
    _x0 = _d['L0_attn_token_embeddings']
    _d['L0_attn_token_embeddings'] = jax.random.normal(jax.random.fold_in(jax.random.key(seed), 1), (8, 512, 128), dtype=_x0.dtype)
    del _x0
    return _d

def reference(L0_attn_token_embeddings, L0_attn_splat_positions, L0_attn_splat_log_scales, L0_attn_splat_amplitudes, L0_attn_Wv, L0_attn_Wo, L0_ffn_weight, L0_ffn_ln_gamma, L0_ffn_ln_beta, L1_attn_Wqa, L1_attn_Wqb, L1_attn_Wkva, L1_attn_Wkvb, L1_attn_Wout, L1_attn_bout, L1_ffn_w_router, L1_ffn_gate_up_proj, L1_ffn_down_proj, L1_ffn_w_gate, L1_ffn_w_up, L1_ffn_w_down):

    def _L0_attn_ref(token_embeddings, splat_positions, splat_log_scales, splat_amplitudes, Wv, Wo):
        import jax, jax.numpy as jnp
        import numpy as np
        B, T, D, S = (4, 256, 128, 64)
        EPS = 1e-08
        x = token_embeddings
        p = splat_positions
        x2 = jnp.sum(x * x, axis=-1, keepdims=True)
        p2 = jnp.sum(p * p, axis=-1)
        xp = jnp.einsum('btd,sd->bts', x, p)
        d2 = jnp.maximum(x2 + p2[None, None, :] - 2.0 * xp, 0.0)
        scales = jnp.exp(splat_log_scales)
        gauss = splat_amplitudes * jnp.exp(-0.5 * d2 / (scales * scales))
        attn = jnp.einsum('bis,bjs->bij', gauss, gauss)
        attn = attn / (jnp.sum(attn, axis=-1, keepdims=True) + EPS)
        v = jnp.einsum('btd,de->bte', x, Wv)
        out = jnp.einsum('bij,bjd->bid', attn, v)
        return jnp.einsum('btd,de->bte', out, Wo)

    def _L0_ffn_ref(x, weight, ln_gamma, ln_beta):
        import jax, jax.numpy as jnp
        import numpy as np
        LN_EPS = 0.001
        EPS = 1e-05
        QB = 128.0

        def ste_round(x):
            return x + jax.lax.stop_gradient(jnp.round(x) - x)
        mu = jnp.mean(x, axis=-1, keepdims=True)
        var = jnp.var(x, axis=-1, keepdims=True)
        xn = (x - mu) * jax.lax.rsqrt(var + LN_EPS) * ln_gamma + ln_beta
        beta = jnp.mean(jnp.abs(weight))
        w_q = jnp.clip(ste_round(weight / (beta + EPS)), -1.0, 1.0)
        gamma = jnp.max(jnp.abs(xn))
        xq = jnp.clip(xn * QB / gamma, -QB + EPS, QB - EPS)
        y = jnp.einsum('bsd,du->bsu', xq, w_q)
        return y * (gamma * beta / QB)

    def _L1_attn_ref(x, Wqa, Wqb, Wkva, Wkvb, Wout, bout):
        import jax, jax.numpy as jnp
        import numpy as np
        B, S, E = (4, 256, 128)
        H, KVH = (16, 4)
        D = E // H
        QL, KVL = (64, 32)
        ROPE_BASE = 10000.0

        def _rope(x):
            d = x.shape[-1]
            inv_freq = 1.0 / ROPE_BASE ** (jnp.arange(0, d, 2, dtype=jnp.float32) / d)
            t = jnp.arange(x.shape[1], dtype=jnp.float32)
            freqs = jnp.outer(t, inv_freq)
            cos = jnp.cos(freqs)[None, :, None, :].astype(x.dtype)
            sin = jnp.sin(freqs)[None, :, None, :].astype(x.dtype)
            x1, x2 = (x[..., ::2], x[..., 1::2])
            r1 = x1 * cos - x2 * sin
            r2 = x1 * sin + x2 * cos
            return jnp.stack([r1, r2], axis=-1).reshape(x.shape)
        b, s, _ = x.shape
        scale = D ** (-0.5)
        q = (x @ Wqa @ Wqb).reshape(b, s, H, D)
        kv = (x @ Wkva @ Wkvb).reshape(b, s, KVH, D, 2)
        k, v = (kv[..., 0], kv[..., 1])
        q = _rope(q)
        k = _rope(k)
        g = H // KVH
        k = jnp.repeat(k, g, axis=2)
        v = jnp.repeat(v, g, axis=2)
        scores = jnp.einsum('bqhd,bkhd->bhqk', q, k) * scale
        causal = jnp.triu(jnp.ones((s, s), dtype=bool), k=1)
        scores = jnp.where(causal[None, None], -jnp.inf, scores)
        w = jax.nn.softmax(scores, axis=-1)
        out = jnp.einsum('bhqk,bkhd->bqhd', w, v).reshape(b, s, E)
        return out @ Wout + bout

    def _L1_ffn_ref(hidden_states, w_router, gate_up_proj, down_proj, w_gate, w_up, w_down):
        import jax, jax.numpy as jnp
        import numpy as np
        E = 16
        H = 128
        F = 256
        TOP_K = 1
        B, S = (2, 128)
        b, s, h = hidden_states.shape
        x = hidden_states.reshape(-1, h)
        logits = x @ w_router.T
        _, top_idx = jax.lax.top_k(logits, TOP_K)
        mask = jax.nn.one_hot(top_idx, E, dtype=logits.dtype).sum(axis=1)
        scores = jax.nn.sigmoid(logits) * mask
        masked_inputs = scores.T[:, :, None] * x[None, :, :]
        gate_up = jnp.einsum('eth,ehf->etf', masked_inputs, gate_up_proj)
        gate, up = jnp.split(gate_up, 2, axis=-1)
        expert_out = jnp.einsum('etf,efh->eth', up * jax.nn.silu(gate), down_proj)
        shared = jax.nn.silu(x @ w_gate.T) * (x @ w_up.T) @ w_down.T
        out = shared + expert_out.sum(axis=0)
        return out.reshape(b, s, h)
    x = L0_attn_token_embeddings
    x = x + _L0_attn_ref(_layernorm(x, axis=-1), L0_attn_splat_positions, L0_attn_splat_log_scales, L0_attn_splat_amplitudes, L0_attn_Wv, L0_attn_Wo)
    x = x + _L0_ffn_ref(_layernorm(x, axis=-1), L0_ffn_weight, L0_ffn_ln_gamma, L0_ffn_ln_beta)
    x = x + _L1_attn_ref(_layernorm(x, axis=-1), L1_attn_Wqa, L1_attn_Wqb, L1_attn_Wkva, L1_attn_Wkvb, L1_attn_Wout, L1_attn_bout)
    x = x + _L1_ffn_ref(_layernorm(x, axis=-1), L1_ffn_w_router, L1_ffn_gate_up_proj, L1_ffn_down_proj, L1_ffn_w_gate, L1_ffn_w_up, L1_ffn_w_down)
    return x

_drawn_inputs = setup_inputs


def setup_inputs(seed=0):
    import zlib

    import numpy as np

    out = dict(_drawn_inputs(seed))
    spreads = {'L0_ffn_ln_gamma': (1.0, 0.2), 'L0_ffn_ln_beta': (0.0, 0.522)}
    factors = {'L1_attn_Wqa': 8.0,
     'L1_attn_Wqb': 8.0,
     'L1_attn_Wkva': 8.0,
     'L1_attn_Wkvb': 8.0,
     'L1_attn_Wout': 8.0,
     'L1_attn_bout': 2.754,
     'L1_ffn_w_router': 8.0,
     'L1_ffn_gate_up_proj': 8.0,
     'L1_ffn_down_proj': 8.0,
     'L1_ffn_w_gate': 7.064,
     'L1_ffn_w_up': 7.027,
     'L1_ffn_w_down': 6.992}
    for name, (base, spread) in spreads.items():
        noise = np.random.default_rng([zlib.crc32(name.encode()), seed]).standard_normal(out[name].shape)
        drawn = base * np.exp(spread * noise) if base else spread * noise
        out[name] = jnp.asarray(drawn.astype(out[name].dtype))
    for name, factor in factors.items():
        out[name] = (out[name] * factor).astype(out[name].dtype)
    return out
```

```python
from contextlib import ExitStack

import numpy as np
import concourse.bass as bass
from concourse import mybir

F32, BF16 = mybir.dt.float32, mybir.dt.bfloat16
I32, U32 = mybir.dt.int32, mybir.dt.uint32
ALU = mybir.AluOpType
ACT = mybir.ActivationFunctionType
AX = mybir.AxisListType.X
REDUCE_ADD, REDUCE_MAX = bass.bass_isa.ReduceOp.add, bass.bass_isa.ReduceOp.max

P = 128
B, T = 8, 512
TILES = T // P
NSPLAT = 64
H, KVH, HD = 16, 4, 8
GRP = H // KVH
QC, KC = H * HD, KVH * HD
RC = QC + KC
NE, FE = 16, 256
LN_EPS, FFN_LN_EPS, EPS_BETA, EPS_SPLAT = 1e-5, 1e-3, 1e-5, 1e-8
QB = 128.0
MASKED = -1e30
CAP = B * T + P
ROW = 2 * P + 1
NOBODY = B * T
SLOTS = B * T // P + NE - 1
OUT_R = 4

MAX_UNITS = [(0, 0, 4), (1, 0, 2), (1, 2, 2)] + [(2, h, 1) for h in range(4)] + [(3, h, 1) for h in range(4)]
SCORE_UNITS = [(0, h, 1) for h in range(4)] + [(1, h, 1) for h in range(4)] + [(2, 0, 2), (2, 2, 2), (3, 0, 4)]
UNITS = len(SCORE_UNITS)
LAST_OF_TILE = [3, 7, 9, 10]
W_RING = 8
SC_BANKS = 3

PLAN = {
    (0, 3): [("AVT", -1)], (0, 1): [("CT", 0)], (0, 4): [("SPLITA", 1)], (0, 5): [("OT", -1)],
    (0, 7): [("SPLITB", 1), ("OUTP", -1)], (0, 10): [("T3", -1)],
    (1, 1): [("CT", 0)], (1, 2): [("ROUTER", -1)], (1, 3): [("AVT", 0)], (1, 5): [("GATE0", -1)],
    (1, 6): [("UP0", -1)], (1, 8): [("GATE1", -1)], (1, 9): [("UP1", -1)],
    (2, 0): [("RANK", -1)], (2, 1): [("CT", 0), ("DOWN", -1)], (2, 3): [("AVT", 0)],
    (2, 4): [("Y", 2)], (2, 10): [("T2", 2)],
    (3, 1): [("CT", 1)], (3, 3): [("AVT", 0)], (3, 4): [("QKV0", 2)], (3, 6): [("QKV1", 2)],
}
PRE_PIECES = ("Y", "T2", "QKV0", "QKV1", "SPLITA", "SPLITB", "CT")
CT_OF = {0: 1, 1: 2, 2: 3, 3: 0}


def plan(prev, nxt):
    out, n = {}, {"pre": 0, "post": 0}
    for kv in range(KVH):
        for u in range(UNITS):
            for name, off in PLAN.get((kv, u), ()):
                if (off < 0 and not prev) or (off > 0 and not nxt):
                    continue
                bank = "pre" if name in PRE_PIECES else "post"
                out.setdefault((kv, u), []).append((name, off, n[bank]))
                n[bank] += 1
    return out, n


PRE_USES, POST_USES = plan(True, True)[1]["pre"], plan(True, True)[1]["post"]
HEAD = [("Y", 0), ("T2", 0), ("QKV0", 0), ("QKV1", 0), ("SPLITA", 0), ("SPLITB", 0),
        ("Y", 1), ("T2", 1), ("QKV0", 1), ("QKV1", 1)]
HEAD_USES = len(HEAD) + 1
FIRST_POST = plan(False, True)[1]["post"]
TAIL = ["OT", "OUTP", "T3", "ROUTER", "GATE0", "UP0", "GATE1", "UP1", "RANK", "DOWN"]


def pre_use(b, n):
    return HEAD_USES + PRE_USES * b + n


def post_use(b, n):
    return n if isinstance(b, int) and b == 0 else FIRST_POST + POST_USES * (b - 1) + n


def bank_uses(name, b, kv=None):
    if isinstance(b, int) and (name, b) in HEAD:
        return HEAD.index((name, b)) + 1
    if name == "CT" and kv == 0 and isinstance(b, int) and b == 0:
        return HEAD_USES
    if name in TAIL and isinstance(b, int) and b == B - 1:
        return post_use(B, 0) + 1 + TAIL.index(name) + 1
    off = {0: 1, None: None}.get(kv, 0) if name == "CT" else next(o for v in PLAN.values() for p, o in v if p == name)
    body = b - off
    order, _ = plan(not isinstance(body, int) or body > 0, not isinstance(body, int) or body < B - 1)
    n = next(n for (slot, u), v in order.items() for p, o, n in v if p == name and (kv is None or CT_OF[slot] == kv))
    return (pre_use if name in PRE_PIECES else post_use)(body, n) + 1


def prior(u, ring):
    if u >= ring:
        return 0, u - ring
    return 1, max(v for v in range(UNITS) if v % ring == u)


def carve(region):
    at = 0

    def tile(shape):
        nonlocal at
        n = int(np.prod(shape[1:]))
        view = region[0:shape[0], at:at + n]
        at += n
        assert at <= region.shape[1], (at, region.shape)
        if len(shape) == 3:
            view = view.rearrange("p (a b) -> p a b", a=shape[1])
        elif len(shape) == 4:
            view = view.rearrange("p (a b c) -> p a b c", a=shape[1], b=shape[2])
        return view
    return tile


def build(nc, ins, out):
    ctx = ExitStack()
    with ctx:
        def sb(name, shape, dt=F32):
            return ctx.enter_context(nc.sbuf_tensor(name, shape, dt))

        def sem(name):
            return ctx.enter_context(nc.semaphore(name))

        x_d = ins["x"].rearrange("b (j p) f -> b p j f", p=P)
        out_rows = out.rearrange("b t f -> (b t) f")
        rows_d = nc.dram_tensor("expert_rows", [NE * CAP + SLOTS * P, ROW], F32, kind="Internal").ap()
        q_d = [nc.dram_tensor(f"q_parts{i}", [3, QC, T], BF16, kind="Internal").ap() for i in range(2)]
        k_d = [nc.dram_tensor(f"k_parts{i}", [KC, 3, T], BF16, kind="Internal").ap() for i in range(2)]
        c_d = [nc.dram_tensor(f"shift_parts{i}", [2, GRP, T], BF16, kind="Internal").ap() for i in range(2)]

        xres = sb("xres", [P, B + 1, TILES, P])
        zt = sb("zt", [P, B + 1, T])
        gate_up = sb("gate_up", [P, NE, 2 * FE])
        down = zt[:, 0:B].rearrange("p b t -> p (b t)").rearrange("p (e c f) -> p e c f", e=NE, c=FE // P)
        stage = sb("stage", [P, 4500])
        splat_tile, mixer_tile, expert_tile = carve(stage), carve(stage), carve(stage)
        turned = sb("turned", [P, 2800])
        setup_tile, output_tile = carve(turned), carve(turned)
        two = range(2)
        ident, identb = sb("ident", [P, P]), sb("identb", [P, P], BF16)
        causal = sb("causal", [P, P], BF16)
        before = sb("before", [P, P], BF16)
        onesb, ones = sb("onesb", [P, P], BF16), sb("ones", [P, P])
        half = sb("half", [P, TILES])
        eps_ln, eps_ffn = sb("eps_ln", [P, TILES]), sb("eps_ffn", [P, TILES])
        seen = sb("seen", [P, P])
        idle, idle_pool = sb("idle", [P, 2]), sb("idle_pool", [P, 3])
        w_in = {n: setup_tile(s) for n, s in {
            "p": [NSPLAT, P], "wv": [P, P], "wo": [P, P], "wffn": [P, P], "wqa": [P, 64], "wqb": [64, P],
            "wkva": [P, 32], "wkvb": [32, 2 * KC], "router": [NE, P],
            "wg": [P, 2, P], "wu": [P, 2, P], "wd": [P, FE]}.items()} | {
            "wout": sb("w_wout", [P, P]), "bout": sb("w_bout", [1, P])}
        logs, amp = sb("logs", [NSPLAT, 1]), sb("amp", [NSPLAT, 1])
        gamma_c, beta_c = sb("gamma_c", [P, 1]), sb("beta_c", [P, 1])
        rope_c, rope_s = sb("rope_c", [P, TILES, RC]), sb("rope_s", [P, TILES, RC])
        small = sb("small", [P, 16])
        splat_t = sb("splat_t", [P, NSPLAT])
        scaled_p = setup_tile([NSPLAT, P])
        squares = setup_tile([NSPLAT, P])
        diag_a, diag_p = sb("diag_a", [NSPLAT, NSPLAT]), sb("diag_p", [NSPLAT, NSPLAT])
        a_rows = sb("a_rows", [P, NSPLAT])
        wvt, wvo = setup_tile([P, P]), sb("wvo", [P, P])
        wqat, wkvat = setup_tile([64, P]), setup_tile([32, P])
        wqkv = sb("wqkv", [P, RC + KC])
        router_t = sb("router_t", [P, NE])
        gate_t, up_t = sb("gate_t", [P, FE]), sb("up_t", [P, FE])
        down_t = sb("down_t", [P, 2, P])
        wq_pos, wq_neg, wq = setup_tile([P, P]), setup_tile([P, P]), sb("wq", [P, P])
        bout_rows = sb("bout_rows", [P, P])
        e_base = sb("e_base", [P, NE])
        e_start = sb("e_start", [P, NE])
        priority = sb("priority", [P, NE])
        token_no = sb("token_no", [P, B, TILES], I32)

        a_st = [sb(f"a_st{i}", [P, TILES, 6]) for i in two]
        a_mv = [sb(f"a_mv{i}", [P, TILES, 2]) for i in two]
        a_rs = [sb(f"a_rs{i}", [P, 6, TILES]) for i in two]
        a_xn = [splat_tile([P, TILES, P]) for i in two]
        a_xt = [splat_tile([P, T]) for i in two]
        a_d2 = [splat_tile([P, TILES, NSPLAT]) for i in two]
        a_e = [splat_tile([P, TILES, NSPLAT]) for i in two]
        a_gt = [splat_tile([P, NSPLAT]) for i in two]
        a_et = [splat_tile([NSPLAT, T]) for i in two]
        a_m = [splat_tile([NSPLAT, P + 1]) for i in two]
        a_den = [sb(f"a_den{i}", [P, 2, TILES]) for i in two]
        zmax = sb("zmax", [P, B])
        zlim = sb("zlim", [P, 4])

        zc = sb("zc", [P, T])
        st2, mv2, rs2 = sb("st2", [P, TILES, 6]), sb("mv2", [P, TILES, 2]), sb("rs2", [P, 2, TILES])
        xn2, xt2 = sb("xn2", [P, TILES, P]), sb("xt2", [P, T])
        rot_c, rot_s = sb("rot_c", [P, 2, RC]), sb("rot_s", [P, 2, RC])
        rot, rest = sb("rot", [P, 2, RC]), sb("rest", [P, 2, RC])
        parts = sb("parts", [P, TILES, RC, 3], BF16)
        qt = sb("qt", [P, 3, T], BF16)
        kt = sb("kt", [3 * KC, T], BF16)
        q8 = [sb(f"q8_{i}", [P, H, T], BF16) for i in two]
        k8 = [sb(f"k8_{i}", [P, KVH, T], BF16) for i in two]
        vv = [sb(f"vv{i}", [P, TILES, KVH, 32]) for i in two]
        v_next = sb("v_next", [P, TILES, KC])
        negmax = [sb(f"negmax{i}", [P, TILES, GRP]) for i in two]
        shift = [sb(f"shift{i}", [P, TILES, 2, GRP], BF16) for i in two]
        shift_t = [sb(f"shift_t{i}", [2 * GRP, T], BF16) for i in two]
        w_ring = [mixer_tile([P, T]) for i in range(W_RING)]
        av_sb = [output_tile([P, T]) for i in two]
        rden = sb("rden", [P, TILES, GRP])
        o_tok = [output_tile([P, TILES, P]) for i in two]
        o_t = output_tile([P, T])
        st3, mv3, rs3 = sb("st3", [P, TILES, 6]), sb("mv3", [P, TILES, 2]), sb("rs3", [P, 2, TILES])
        xn3, xt3 = sb("xn3", [P, TILES, P]), sb("xt3", [P, T])
        lmax, score = sb("lmax", [P, TILES]), sb("score", [P, 2, TILES])
        top, pri, onehot_f = sb("top", [P, TILES, NE]), sb("pri", [P, TILES]), sb("onehot_f", [P, TILES, NE])
        onehot = sb("onehot", [P, TILES, NE], BF16)
        place, place_s = sb("place", [P, TILES, NE]), sb("place_s", [P, TILES])
        place_i = [sb(f"place_i{i}", [P, TILES], U32) for i in two]
        th, sg = sb("th", [P, T]), sb("sg", [P, T])
        hid = sb("hid", [P, 2, T])
        rows = [sb(f"rows{i}", [P, TILES, ROW]) for i in two]

        pad_rows = sb("pad_rows", [P, ROW])
        steps = sb("steps", [P, NE, B * T // P])
        cnt, full = sb("cnt", [P, NE]), expert_tile([P, NE, B * T // P])
        ntile, ends = sb("ntile", [P, NE]), sb("ends", [P, NE])
        slot_no = sb("slot_no", [P, 1])
        ended, s_tmp = sb("ended", [P, NE]), sb("s_tmp", [P, NE])
        s_val = sb("s_val", [P, 6])
        s_tab, s_row = sb("s_tab", [P, 2]), sb("s_row", [2, P], I32)
        base_i = sb("base_i", [1, NE], I32)
        slot = [expert_tile([P, ROW]) for i in range(OUT_R)]
        d_xt = [expert_tile([P, P]) for i in two]
        d_th = [expert_tile([P, FE]) for i in two]
        d_h = [expert_tile([P, FE]) for i in two]
        d_ht = [expert_tile([P, FE]) for i in two]
        d_out = [expert_tile([P, P]) for i in range(OUT_R)]

        bank = [ctx.enter_context(nc.psum_tensor(f"bank{i}", [P, T], F32)) for i in range(8)]
        MAXB, SCB, AVB, PREB, POSTB = bank[0:2], bank[2:5], bank[5], bank[6], bank[7]

        names = """w_p w_small w_ffn w_attn w_moe w_rope w_experts
            const_pool const_dve ident_ready s_dve s_act s_pe1 s_copy1 s_pe2 s_copy2 beta_part beta_sum wq_ready
            x_loaded0 x_loaded1
            a_stats a_rstd a_xn a_xt_ps a_xt a_d2_ps a_d2 a_e a_gt_ps a_et_ps a_gt a_et a_m_ps a_m a_o_ps a_den a_x1
            a_stats2 a_rstd2 a_zn a_zt_ps a_zt a_zmax zlim_part zlim_all zlim
            pre_full pre_free post_full post_free
            zclip x2 xbias rstd2 xn2_ready rope_mul v_ready rope_add part_hi rest_lo part_mid part_lo
            parts_stored0 parts_stored1 parts_loaded0 parts_loaded1
            max_ps max_done shift_split shift_stored0 shift_stored1 shift_loaded0 shift_loaded1
            score_ps exp_done masked av_ps av_copied o_rden stats3 rstd3 xn3_ready
            route score_tanh expert_in tanh_g place_ready numbered
            rows_sent0 rows_sent1 pads_sent table table_ps table_ready
            slot_in0 slot_in1 slot_in2 slot_in3 d_xt_ps d_xt_ready d_gu_ps d_tanh d_sg d_hid d_ht_ps d_ht_ready d_dn_ps
            d_out_ready scatter_turn out_sent0 out_sent1 out_sent2 out_sent3""".split()
        s = {n: sem(n) for n in names}

        block = ctx.enter_context(nc.Block())

        @block.sync
        def _(sp):
            load = lambda dst, src, sm: sp.dma_start(dst, src).then_inc(s[sm], 16)
            for i in range(2):
                load(xres[:, i], x_d[i], f"x_loaded{i}")
            load(w_in["p"][:], ins["p"], "w_p")
            with nc.allow_non_contiguous_dma(reason="columns of one value for each partition"):
                load(logs[:], ins["logs"].rearrange("(p a) -> p a", a=1), "w_small")
                load(amp[:], ins["amp"].rearrange("(p a) -> p a", a=1), "w_small")
                load(gamma_c[:], ins["gamma"].rearrange("(p a) -> p a", a=1), "w_small")
                load(beta_c[:], ins["beta"].rearrange("(p a) -> p a", a=1), "w_small")
            for n in ("wv", "wo"):
                load(w_in[n][:], ins[n], "w_attn")
            load(w_in["wffn"][:], ins["wffn"], "w_ffn")
            for n in ("wqa", "wqb", "wkva", "wkvb", "wout"):
                load(w_in[n][:], ins[n], "w_attn")
            load(w_in["bout"][:], ins["bout"].rearrange("(a f) -> a f", a=1), "w_attn")
            load(w_in["router"][:], ins["router"], "w_moe")
            load(w_in["wg"][:], ins["wg"].rearrange("(c p) f -> p c f", p=P), "w_moe")
            load(w_in["wu"][:], ins["wu"].rearrange("(c p) f -> p c f", p=P), "w_moe")
            load(w_in["wd"][:], ins["wd"], "w_moe")
            with sp.Fori(0, B // 2 - 1) as i:
                for par in two:
                    sp.wait_ge(s[f"x_loaded{par}"], i * 16 + 16)
                    sp.dma_start(xres[:, bass.ds(i * 2 + 2 + par, 1)].rearrange("p a j f -> p (a j) f"),
                                 x_d[bass.ds(i * 2 + 2 + par, 1)].rearrange("a p j f -> (a p) j f"))\
                      .then_inc(s[f"x_loaded{par}"], 16)
            load(rope_c[:], ins["rope_c"], "w_rope")
            load(rope_s[:], ins["rope_s"], "w_rope")
            load(gate_up[:], ins["gate_up"].rearrange("e p f -> p e f"), "w_experts")

            def parts_round_trip(b, par, past):
                sp.wait_ge(s["pre_free"], bank_uses("SPLITB", b))
                st, ld = s[f"parts_stored{par}"], s[f"parts_loaded{par}"]
                sp.wait_ge(ld, 12 * 16 * past)
                sp.dma_start(q_d[par].rearrange("c p t -> p c t"), qt[:]).then_inc(st, 16)
                sp.dma_start(k_d[par].rearrange("c p t -> (c p) t"), kt[:]).then_inc(st, 16)
                if not isinstance(b, int) or b >= 2:
                    sp.wait_ge(s["score_ps"], KVH * UNITS * (b - 1))
                sp.wait_ge(st, 32 * past + 32)
                for g, (qp, kp) in enumerate(((0, 0), (1, 0), (2, 0), (0, 1), (1, 1), (0, 2))):
                    r = slice(HD * g, HD * g + HD)
                    sp.dma_start(q8[par][r], q_d[par][qp].rearrange("(h d) t -> d h t", d=HD)).then_inc(ld, 16)
                    sp.dma_start(k8[par][r], k_d[par][:, kp].rearrange("(h d) t -> d h t", d=HD)).then_inc(ld, 16)

            def shift_round_trip(b, par, kv, groups):
                g = kv % 2
                sp.wait_ge(s["pre_free"], bank_uses("CT", b, kv))
                st, ld = s[f"shift_stored{g}"], s[f"shift_loaded{g}"]
                sp.wait_ge(ld, 16 * groups)
                sp.dma_start(c_d[g].rearrange("c h t -> (c h) t"), shift_t[g][:]).then_inc(st, 16)
                sp.wait_ge(st, 16 * groups + 16)
                if kv == 0 and not (isinstance(b, int) and b < 2):
                    sp.wait_ge(s["score_ps"], KVH * UNITS * (b - 1))
                sp.dma_start(q8[par][64:66, GRP * kv:GRP * kv + GRP, :], c_d[g]).then_inc(ld, 16)

            parts_round_trip(0, 0, 0)
            shift_round_trip(0, 0, 0, 0)

            def body(b, par, past, nxt=True):
                shift_round_trip(b, par, 1, 2 * b)
                if nxt:
                    parts_round_trip(b + 1, 1 - par, past + par)
                shift_round_trip(b, par, 2, 2 * b + 1)
                shift_round_trip(b, par, 3, 2 * b + 1)
                if nxt:
                    shift_round_trip(b + 1, 1 - par, 0, 2 * b + 2)

            body(0, 0, 0)
            with sp.Fori(0, B // 2 - 1) as i:
                body(i * 2 + 1, 1, i)
                body(i * 2 + 2, 0, i + 1)
            body(B - 1, 1, B // 2 - 1, nxt=False)

            sp.wait_ge(s["x2"], 8 * B)
            sp.dma_start(down[:], ins["down"].rearrange("e (c p) f -> p e c f", p=P)).then_inc(s["w_experts"], 16)

            sp.wait_ge(s["table"], 1)
            for i in two:
                sp.wait_ge(s[f"rows_sent{i}"], 16 * TILES * B // 2)
            for e in range(NE):
                end = sp.value_load(base_i[0:1, e:e + 1], min_val=0, max_val=NE * CAP)
                sp.dma_start(rows_d[bass.ds(end, P), :], pad_rows[:]).then_inc(s["pads_sent"], 16)
            with sp.Fori(0, SLOTS) as i:
                sp.dma_start(rows_d[bass.ds(i * P + NE * CAP, P), :], pad_rows[:]).then_inc(s["pads_sent"], 16)
            sp.wait_ge(s["pads_sent"], 16 * (NE + SLOTS))
            sp.wait_ge(s["table_ready"], 1)

            def load_slot(n, r, past, waits=True):
                at = sp.value_load(s_row[0:1, bass.ds(n, 1)], min_val=0, max_val=NE * CAP + (SLOTS - 1) * P)
                if waits:
                    sp.wait_ge(s[f"out_sent{r}"], 16 * past)
                sp.dma_start(slot[r][:], rows_d[bass.ds(at, P), :]).then_inc(s[f"slot_in{r}"], 16)

            for n in range(OUT_R):
                load_slot(n, n, 0, waits=False)
            with sp.Fori(1, SLOTS // OUT_R) as i:
                for r in range(OUT_R):
                    load_slot(i * OUT_R + r, r, i)
            for n in range(SLOTS // OUT_R * OUT_R, SLOTS):
                load_slot(n, n % OUT_R, n // OUT_R)
            for r in range(OUT_R):
                sp.wait_ge(s[f"out_sent{r}"], 16 * len(range(r, SLOTS, OUT_R)))

        @block.gpsimd
        def _(pool):
            g = nc.gpsimd
            g.memset(ident[:], 0.0).then_inc(s["const_pool"], 1)
            g.memset(identb[:], 0.0).then_inc(s["const_pool"], 1)
            g.memset(causal[:], 0.0).then_inc(s["const_pool"], 1)
            g.memset(before[:], 0.0).then_inc(s["const_pool"], 1)
            g.memset(half[:], -0.5).then_inc(s["const_pool"], 1)
            g.memset(seen[:], 1.0).then_inc(s["const_pool"], 1)
            g.memset(eps_ln[:], LN_EPS).then_inc(s["const_pool"], 1)
            g.memset(eps_ffn[:], FFN_LN_EPS).then_inc(s["const_pool"], 1)
            g.memset(idle_pool[:], 0.0).then_inc(s["const_pool"], 1)
            pool.wait_ge(s["const_pool"], 9)
            for m, op, fill, cm, step in ((ident, ALU.not_equal, 1.0, 1, -1), (identb, ALU.not_equal, 1.0, 1, -1),
                                          (causal, ALU.is_ge, MASKED, 1, -1), (before, ALU.is_ge, 1.0, 1, -1)):
                g.affine_select(out=m[:], in_=m[:], compare_op=op, fill=fill, base=0, pattern=[[step, P]],
                                channel_multiplier=cm).then_inc(s["ident_ready"], 1)
            g.affine_select(out=seen[:], in_=seen[:], compare_op=ALU.is_ge, fill=0.0, base=0, pattern=[[1, P]],
                            channel_multiplier=-1).then_inc(s["ident_ready"], 1)
            g.iota(token_no[:], pattern=[[T, B], [P, TILES]], base=0, channel_multiplier=1).then_inc(s["const_pool"], 1)
            g.iota(full[:].bitcast(I32), pattern=[[0, NE], [P, B * T // P]], base=0, channel_multiplier=0).then_inc(s["const_pool"], 1)
            g.iota(s_tmp[:].bitcast(I32), pattern=[[CAP, NE]], base=0, channel_multiplier=0).then_inc(s["const_pool"], 1)
            g.iota(ended[:].bitcast(I32), pattern=[[-1, NE]], base=NE, channel_multiplier=0).then_inc(s["const_pool"], 1)
            g.iota(s_val[:, 0:1].bitcast(I32), pattern=[[0, 1]], base=0, channel_multiplier=1).then_inc(s["const_pool"], 1)
            g.memset(pad_rows[:], 0.0).then_inc(s["const_pool"], 1)
            g.iota(s_val[:, 1:2].bitcast(I32), pattern=[[0, 1]], base=NOBODY, channel_multiplier=0).then_inc(s["const_pool"], 1)
            pool.wait_ge(s["beta_part"], 1)
            g.partition_all_reduce(small[:, 9:10], small[:, 8:9], P, REDUCE_ADD).then_inc(s["beta_sum"], 1)

            def root(dst, src, eps, tmp, sm, at):
                g.tensor_tensor(tmp, src, eps, ALU.add).then_inc(s[sm], 1)
                pool.wait_ge(s[sm], at + 1)
                g.tensor_tensor(dst, tmp, half[:, 0:TILES], ALU.pow).then_inc(s[sm], 1)

            with pool.Fori(0, B // 2) as i:
                for par in two:
                    b = i * 2 + par
                    rs, mv = a_rs[par], a_mv[par]
                    pool.wait_ge(s["a_stats"], 8 * b + 8)
                    root(rs[:, 1], mv[:, :, 1], eps_ln[:], rs[:, 0], "a_rstd", 4 * b)
                    pool.wait_ge(s["a_rstd"], 4 * b + 2)
                    g.tensor_tensor(rs[:, 2], rs[:, 1], rs[:, 1], ALU.mult).then_inc(s["a_rstd"], 1)
                    pool.wait_ge(s["a_rstd"], 4 * b + 3)
                    g.tensor_tensor(rs[:, 3], rs[:, 2], mv[:, :, 1], ALU.mult).then_inc(s["a_rstd"], 1)
                for par in two:
                    b = i * 2 + par
                    rs, mv = a_rs[par], a_mv[par]
                    pool.wait_ge(s["a_stats2"], 8 * b + 8)
                    root(rs[:, 1], mv[:, :, 1], eps_ln[:], rs[:, 0], "a_rstd2", 7 * b)
                    pool.wait_ge(s["a_rstd2"], 7 * b + 2)
                    g.tensor_tensor(rs[:, 2], rs[:, 1], rs[:, 1], ALU.mult).then_inc(s["a_rstd2"], 1)
                    pool.wait_ge(s["a_rstd2"], 7 * b + 3)
                    g.tensor_tensor(rs[:, 3], rs[:, 2], mv[:, :, 1], ALU.mult).then_inc(s["a_rstd2"], 1)
                    pool.wait_ge(s["a_rstd2"], 7 * b + 4)
                    root(rs[:, 4], rs[:, 3], eps_ffn[:], rs[:, 0], "a_rstd2", 7 * b + 4)
                    pool.wait_ge(s["a_rstd2"], 7 * b + 6)
                    g.tensor_tensor(rs[:, 5], rs[:, 4], rs[:, 1], ALU.mult).then_inc(s["a_rstd2"], 1)
            pool.wait_ge(s["zlim_part"], 1)
            g.partition_all_reduce(zlim[:, 1:2], zlim[:, 0:1], P, REDUCE_MAX).then_inc(s["zlim_all"], 1)

            def y(b, par):
                pool.wait_ge(s["x2"], 8 * b + 8)
                root(rs2[:, 1], mv2[:, :, 1], eps_ln[:], rs2[:, 0], "rstd2", 2 * b)
                pool.wait_ge(s["xn2_ready"], 4 * b + 4)
                xb = xres[:, b] if isinstance(b, int) else xres[:, bass.ds(b, 1)].rearrange("p a j f -> p (a j) f")
                g.tensor_tensor(xb, xb, bout_rows[:].unsqueeze(1).to_broadcast([P, TILES, P]), ALU.add)\
                 .then_inc(s["xbias"], 1)

            def split(b, par, hf):
                n = 2 * b + hf
                pool.wait_ge(s["rope_mul"], 3 * n + 3)
                g.tensor_tensor(rot[:], rot_c[:], rot_s[:], ALU.add).then_inc(s["rope_add"], 1)
                pool.wait_ge(s["part_hi"], n + 1)
                g.tensor_tensor(rest[:], rot[:], parts[:, 2 * hf:2 * hf + 2, :, 0], ALU.subtract).then_inc(s["rest_lo"], 1)
                pool.wait_ge(s["part_mid"], n + 1)
                g.tensor_tensor(parts[:, 2 * hf:2 * hf + 2, :, 2], rest[:], parts[:, 2 * hf:2 * hf + 2, :, 1], ALU.subtract)\
                 .then_inc(s["part_lo"], 1)

            def outp(b, par):
                pool.wait_ge(s["stats3"], 8 * b + 8)
                root(rs3[:, 1], mv3[:, :, 1], eps_ln[:], rs3[:, 0], "rstd3", 2 * b)

            def down_scatter(b, par):
                pool.wait_ge(s["post_free"], bank_uses("DOWN", b))
                pool.wait_ge(s["expert_in"], 4 * b + 4)
                pool.wait_ge(s["numbered"], b + 1)
                pool.wait_ge(s["place_ready"], 5 * b + 5)
                g.tensor_tensor(idle_pool[:, 0:1], idle_pool[:, 1:2], idle_pool[:, 1:2], ALU.add)
                for j in range(TILES):
                    g.indirect_dma_start(rows_d, bass.IndirectOffsetOnAxis(place_i[par][:, j:j + 1], 0), rows[par][:, j, :],
                                         None, bounds_check=NE * CAP - 1, oob_is_err=False)\
                     .then_inc(s[f"rows_sent{par}"], 16)

            def select(b, kv, u):
                ktile, h0, nh = SCORE_UNITS[u]
                pool.wait_ge(s["exp_done"], KVH * UNITS * b + UNITS * kv + u + 1)
                n = T - P * ktile
                blk = w_ring[u % W_RING][:, 0:nh * n].rearrange("p (h n) -> p h n", h=nh)[:, :, 0:P]
                g.tensor_tensor(blk, blk, seen[:].unsqueeze(1).to_broadcast([P, nh, P]), ALU.mult).then_inc(s["masked"], 1)

            for b in two:
                y(b, b)
                split(b, b, 0) if b == 0 else None
                split(b, b, 1) if b == 0 else None
            split(1, 1, 0)
            split(1, 1, 1)

            def body(b, par, prev=True, nxt=True):
                order, _ = plan(prev, nxt)
                for kv in range(KVH):
                    for u in range(UNITS):
                        for name, off, _ in order.get((kv, u), ()):
                            if name == "OUTP":
                                outp(b - 1, 1 - par)
                            elif name == "Y":
                                y(b + 2, par)
                            elif name == "DOWN":
                                down_scatter(b - 1, 1 - par)
                            elif name in ("QKV0", "QKV1"):
                                split(b + 2, par, int(name[3]))
                        select(b, kv, u)

            body(0, 0, prev=False)
            with pool.Fori(0, B // 2 - 1) as i:
                body(i * 2 + 1, 1)
                body(i * 2 + 2, 0)
            body(B - 1, 1, nxt=False)
            outp(B - 1, 1)
            down_scatter(B - 1, 1)

            def scatter(n, r, past):
                pool.wait_ge(s["d_out_ready"], n + 1)
                pool.wait_ge(s["scatter_turn"], n)
                g.tensor_tensor(idle_pool[:, 2:3], idle_pool[:, 1:2], idle_pool[:, 1:2], ALU.add).then_inc(s["scatter_turn"], 1)
                g.indirect_dma_start(out_rows, bass.IndirectOffsetOnAxis(slot[r][:, 2 * P:ROW].bitcast(U32), 0), d_out[r][:],
                                     None, bounds_check=B * T - 1, oob_is_err=False).then_inc(s[f"out_sent{r}"], 16)

            with pool.Fori(0, SLOTS // OUT_R) as i:
                for r in range(OUT_R):
                    scatter(i * OUT_R + r, r, i)
            for n in range(SLOTS // OUT_R * OUT_R, SLOTS):
                scatter(n, n % OUT_R, n // OUT_R)

        @block.scalar
        def _(act):
            a = nc.scalar
            act.wait_ge(s["w_small"], 64)
            act.wait_ge(s["const_dve"], 12)
            a.activation(small[0:NSPLAT, 0:1], logs[:], ACT.Exp, scale=-2.0).then_inc(s["s_act"], 1)
            act.wait_ge(s["s_pe1"], 11)
            for dst, src in ((wvt[:], bank[0][:, 0:128]), (splat_t[:], bank[0][:, 128:192]),
                             (wqat[:], bank[0][0:64, 192:320]), (wkvat[:], bank[0][0:32, 320:448]),
                             (router_t[:], bank[0][:, 448:464]), (gate_t[:], bank[1][:, 0:256]),
                             (up_t[:], bank[1][:, 256:512]), (down_t[:], bank[2][:, 0:256].rearrange("p (c f) -> p c f", c=2))):
                a.copy(dst, src).then_inc(s["s_copy1"], 1)
            act.wait_ge(s["s_pe2"], 6)
            for dst, src in ((wvo[:], bank[3][:, 0:128]), (wqkv[:], bank[3][:, 128:320]), (a_rows[:], bank[3][:, 320:384]),
                             (bout_rows[:], bank[3][:, 384:512])):
                a.copy(dst, src).then_inc(s["s_copy2"], 1)

            with act.Fori(0, B // 2) as i:
                for par in two:
                    b = i * 2 + par
                    act.wait_ge(s["a_xt_ps"], b + 1)
                    a.copy(a_xt[par][:], bank[4 * par][:]).then_inc(s["a_xt"], 1)
                for par in two:
                    b = i * 2 + par
                    act.wait_ge(s["a_d2"], 5 * b + 5)
                    a.activation(a_e[par][:], a_d2[par][:], ACT.Exp).then_inc(s["a_e"], 1)
                for par in two:
                    b = i * 2 + par
                    act.wait_ge(s["a_gt_ps"], b + 1)
                    a.copy(a_gt[par][:], bank[4 * par + 2][:, 0:NSPLAT]).then_inc(s["a_gt"], 1)
                    act.wait_ge(s["a_et_ps"], b + 1)
                    a.copy(a_et[par][:], bank[4 * par + 3][0:NSPLAT, :]).then_inc(s["a_et"], 1)
                for par in two:
                    b = i * 2 + par
                    act.wait_ge(s["a_zt_ps"], b + 1)
                    a.activation(zt[:, bass.ds(b, 1)].rearrange("p a t -> p (a t)"), bank[4 * par + 2][:], ACT.Identity,
                                 bias=beta_c[:, 0:1], scale=gamma_c[:, 0:1]).then_inc(s["a_zt"], 1)

            def t2(b, n):
                act.wait_ge(s["pre_full"], n + 1)
                a.copy(xt2[:], PREB[:]).then_inc(s["pre_free"], 1)

            def split(b, hf):
                k = 2 * b + hf
                act.wait_ge(s["rope_add"], k + 1)
                if hf == 0:
                    if not isinstance(b, int) or b > 0:
                        act.wait_ge(s["pre_full"], bank_uses("SPLITB", b - 1))
                a.copy(parts[:, 2 * hf:2 * hf + 2, :, 0], rot[:]).then_inc(s["part_hi"], 1)
                act.wait_ge(s["rest_lo"], k + 1)
                a.copy(parts[:, 2 * hf:2 * hf + 2, :, 1], rest[:]).then_inc(s["part_mid"], 1)

            def split_a(b, n, par, past):
                act.wait_ge(s["pre_full"], n + 1)
                if not isinstance(b, int) or b > 0:
                    act.wait_ge(s[f"parts_stored{1 - par}"], 32 * (past + par))
                a.copy(qt[:, 0:2], PREB[:].bitcast(BF16).rearrange("p (c t) -> p c t", c=2)).then_inc(s["pre_free"], 1)

            def split_b(b, n):
                act.wait_ge(s["pre_full"], n + 1)
                both = PREB[:].bitcast(BF16)
                a.copy(qt[:, 2], both[:, 0:T])
                a.copy(kt[:], both[0:3 * KC, T:2 * T]).then_inc(s["pre_free"], 1)

            def ct(gb, kv, n, groups):
                act.wait_ge(s["pre_full"], n + 1)
                act.wait_ge(s[f"shift_stored{kv % 2}"], 16 * groups)
                a.copy(shift_t[kv % 2][:], PREB[:].bitcast(BF16)[0:2 * GRP, 0:T]).then_inc(s["pre_free"], 1)

            def ot(b, n):
                act.wait_ge(s["post_full"], n + 1)
                a.copy(o_t[:], POSTB[:]).then_inc(s["post_free"], 1)

            def t3(b, n):
                act.wait_ge(s["post_full"], n + 1)
                a.copy(xt3[:], POSTB[:]).then_inc(s["post_free"], 1)

            def router(b):
                act.wait_ge(s["route"], 5 * b + 1)
                a.activation(score[:, 0], lmax[:], ACT.Tanh, scale=0.5).then_inc(s["score_tanh"], 1)

            def gate(b, n, hf):
                act.wait_ge(s["post_full"], n + 1)
                a.activation(th[:], POSTB[:], ACT.Tanh, scale=0.5).then_inc(s["tanh_g"], 1)

            def av_copy(b, kv):
                g = KVH * b + kv
                act.wait_ge(s["av_ps"], 4 * g + 4)
                a.copy(av_sb[kv % 2][:], AVB[:]).then_inc(s["av_copied"], 1)

            def exp(b, kv, u):
                ktile, h0, nh = SCORE_UNITS[u]
                g = KVH * b + kv
                act.wait_ge(s["score_ps"], UNITS * g + u + 1)
                back, v = prior(u, W_RING)
                if not (isinstance(b, int) and b == 0 and kv == 0) or back == 0:
                    done = next(k for k, last in enumerate(LAST_OF_TILE) if v <= last) + 1
                    act.wait_ge(s["av_ps"], 4 * (g - back) + done)
                cols = nh * (T - P * ktile)
                a.activation(w_ring[u % W_RING][:, 0:cols], SCB[u % SC_BANKS][:, 0:cols], ACT.Exp).then_inc(s["exp_done"], 1)

            for n, (name, b) in enumerate(HEAD):
                if name == "T2":
                    t2(b, n)
                elif name in ("QKV0", "QKV1"):
                    split(b, int(name[3]))
                elif name == "SPLITA":
                    split_a(b, n, b % 2, 0)
                elif name == "SPLITB":
                    split_b(b, n)
            ct(0, 0, HEAD_USES - 1, 0)

            def body(b, par, past, prev=True, nxt=True):
                order, _ = plan(prev, nxt)
                for kv in range(KVH):
                    for u in range(UNITS):
                        for name, off, n in order.get((kv, u), ()):
                            pre, post = pre_use(b, n), post_use(b, n)
                            if name == "T2":
                                t2(b + 2, pre)
                            elif name in ("QKV0", "QKV1"):
                                split(b + 2, int(name[3]))
                            elif name == "SPLITA":
                                split_a(b + 1, pre, 1 - par, past + par)
                            elif name == "SPLITB":
                                split_b(b + 1, pre)
                            elif name == "CT":
                                c = CT_OF[kv]
                                ct(b + off, c, pre, 2 * (b + off) + c // 2)
                            elif name == "OT":
                                ot(b - 1, post)
                            elif name == "T3":
                                t3(b - 1, post)
                            elif name == "ROUTER":
                                router(b - 1)
                            elif name in ("GATE0", "GATE1"):
                                gate(b - 1, post, int(name[4]))
                        exp(b, kv, u)
                        if u == 2 and (prev or kv):
                            av_copy(*((b, kv - 1) if kv else (b - 1, KVH - 1)))

            body(0, 0, 0, prev=False)
            with act.Fori(0, B // 2 - 1) as i:
                body(i * 2 + 1, 1, i)
                body(i * 2 + 2, 0, i + 1)
            body(B - 1, 1, B // 2 - 1, nxt=False)
            av_copy(B - 1, KVH - 1)
            last = post_use(B, 0) + 1
            for n, name in enumerate(TAIL):
                if name == "OT":
                    ot(B - 1, last + n)
                elif name == "T3":
                    t3(B - 1, last + n)
                elif name == "ROUTER":
                    router(B - 1)
                elif name in ("GATE0", "GATE1"):
                    gate(B - 1, last + n, int(name[4]))

            def d_xt_copy(n, r):
                act.wait_ge(s["d_xt_ps"], n + 1)
                a.copy(d_xt[r % 2][:], bank[r % 2][:, 0:P]).then_inc(s["d_xt_ready"], 1)

            def d_step(n, r, first=False, last=False):
                act.wait_ge(s["d_gu_ps"], n + 1)
                if not first:
                    act.wait_ge(s["d_hid"], n - 1 if isinstance(n, int) and n < 2 else n - 1)
                a.activation(d_th[r % 2][:], bank[2 + r % 2][:, 0:FE], ACT.Tanh, scale=0.5).then_inc(s["d_tanh"], 1)
                if not last:
                    d_xt_copy(n + 1, r + 1)
                if not first:
                    act.wait_ge(s["d_ht_ps"], n)
                    a.copy(d_ht[(r + 1) % 2][:], bank[4 + (r + 1) % 2][:, 0:FE]).then_inc(s["d_ht_ready"], 1)

            d_xt_copy(0, 0)
            d_step(0, 0, first=True)
            loops = (SLOTS - 2) // OUT_R
            with act.Fori(0, loops) as i:
                for r in range(OUT_R):
                    d_step(i * OUT_R + 1 + r, (1 + r) % OUT_R)
            for n in range(1 + loops * OUT_R, SLOTS):
                d_step(n, n % OUT_R, last=n == SLOTS - 1)
            act.wait_ge(s["d_ht_ps"], SLOTS)
            a.copy(d_ht[(SLOTS - 1) % 2][:], bank[4 + (SLOTS - 1) % 2][:, 0:FE]).then_inc(s["d_ht_ready"], 1)

        @block.vector
        def _(dve):
            v = nc.vector
            v.memset(ones[:], 1.0).then_inc(s["const_dve"], 1)
            v.memset(onesb[:], 1.0).then_inc(s["const_dve"], 1)
            for i in two:
                v.memset(q8[i][:], 0.0).then_inc(s["const_dve"], 1)
                v.memset(k8[i][:], 0.0).then_inc(s["const_dve"], 1)
                v.memset(vv[i][:], 0.0).then_inc(s["const_dve"], 1)
            v.memset(xres[:, B], 1.0).then_inc(s["const_dve"], 1)
            v.memset(zt[:, B], 0.0).then_inc(s["const_dve"], 1)
            v.memset(small[:], 0.0).then_inc(s["const_dve"], 1)
            v.memset(idle[:], 0.0).then_inc(s["const_dve"], 1)
            dve.wait_ge(s["const_dve"], 12)
            for i in two:
                v.memset(k8[i][64:66], 1.0).then_inc(s["const_dve"], 1)
                v.memset(vv[i][:, :, :, HD:HD + 1], 1.0).then_inc(s["const_dve"], 1)

            small_s = lambda c: small[0:NSPLAT, c:c + 1]
            dve.wait_ge(s["s_act"], 1)
            dve.wait_ge(s["w_p"], 16)
            dve.wait_ge(s["w_small"], 64)
            dve.wait_ge(s["ident_ready"], 5)
            v.tensor_tensor(squares[:], w_in["p"][:], w_in["p"][:], ALU.mult).then_inc(s["s_dve"], 1)
            v.tensor_scalar(small_s(1), small_s(0), -0.5, None, ALU.mult).then_inc(s["s_dve"], 1)
            v.tensor_scalar(small_s(2), small_s(0), -0.5 * P, None, ALU.mult).then_inc(s["s_dve"], 1)
            v.tensor_tensor(small_s(4), amp[:], amp[:], ALU.mult).then_inc(s["s_dve"], 1)
            dve.wait_ge(s["s_dve"], 4)
            v.tensor_reduce(small_s(3), squares[:], AX, ALU.add).then_inc(s["s_dve"], 1)
            v.tensor_scalar(scaled_p[:], w_in["p"][:], small_s(1), -2.0, ALU.mult, ALU.mult).then_inc(s["s_dve"], 1)
            v.tensor_scalar(diag_a[:], ident[0:NSPLAT, 0:NSPLAT], small_s(2), None, ALU.mult).then_inc(s["s_dve"], 1)
            dve.wait_ge(s["s_dve"], 7)
            v.tensor_scalar(diag_p[:], ident[0:NSPLAT, 0:NSPLAT], small_s(3), small_s(1), ALU.mult, ALU.mult)\
             .then_inc(s["s_dve"], 1)

            dve.wait_ge(s["w_ffn"], 16)
            v.tensor_reduce(small[:, 8:9], w_in["wffn"][:], AX, ALU.add, apply_absolute_value=True).then_inc(s["beta_part"], 1)
            dve.wait_ge(s["beta_sum"], 1)
            v.tensor_scalar(small[:, 10:11], small[:, 9:10], 1.0 / (P * P), EPS_BETA, ALU.mult, ALU.add).then_inc(s["wq_ready"], 1)
            v.tensor_scalar(small[:, 5:6], small[:, 9:10], 1.0 / (P * P), None, ALU.mult).then_inc(s["wq_ready"], 1)
            dve.wait_ge(s["wq_ready"], 2)
            v.reciprocal(small[:, 7:8], small[:, 10:11]).then_inc(s["wq_ready"], 1)
            dve.wait_ge(s["wq_ready"], 3)
            v.tensor_scalar(wq_pos[:], w_in["wffn"][:], small[:, 7:8], 0.5, ALU.mult, ALU.is_gt).then_inc(s["wq_ready"], 1)
            v.tensor_scalar(wq_neg[:], w_in["wffn"][:], small[:, 7:8], -0.5, ALU.mult, ALU.is_lt).then_inc(s["wq_ready"], 1)
            dve.wait_ge(s["wq_ready"], 5)
            v.tensor_tensor(wq[:], wq_pos[:], wq_neg[:], ALU.subtract).then_inc(s["wq_ready"], 1)

            dve.wait_ge(s["const_pool"], 16)
            v.tensor_copy(steps[:], full[:].bitcast(I32)).then_inc(s["s_dve"], 1)
            v.tensor_copy(e_start[:], s_tmp[:].bitcast(I32)).then_inc(s["s_dve"], 1)
            v.tensor_copy(priority[:], ended[:].bitcast(I32)).then_inc(s["s_dve"], 1)
            v.tensor_copy(slot_no[:], s_val[:, 0:1].bitcast(I32)).then_inc(s["s_dve"], 1)
            v.tensor_copy(pad_rows[:, 2 * P:ROW].bitcast(I32), s_val[:, 1:2].bitcast(I32)).then_inc(s["s_dve"], 1)
            dve.wait_ge(s["s_dve"], 13)
            v.tensor_copy(e_base[:], e_start[:]).then_inc(s["s_dve"], 1)

            def statistics(src, st, mv, sm, at):
                for j in range(TILES):
                    v.bn_stats(st[:, j], src(j)).then_inc(s[sm], 1)
                dve.wait_ge(s[sm], at + TILES)
                v.tensor_copy(idle[:, 0:1], idle[:, 1:2])
                for j in range(TILES):
                    v.bn_aggr(mv[:, j], st[:, j]).then_inc(s[sm], 1)

            def normalise(dst, src, mv, rstd, sm):
                for j in range(TILES):
                    v.tensor_scalar(dst[:, j], src(j), mv[:, j, 0:1], rstd[:, j:j + 1], ALU.subtract, ALU.mult)\
                     .then_inc(s[sm], 1)

            def res(b):
                if isinstance(b, int):
                    return lambda j: xres[:, b, j]
                return lambda j: xres[:, bass.ds(b, 1), j].rearrange("p a f -> p (a f)")

            with dve.Fori(0, B // 2) as i:
                for par in two:
                    b = i * 2 + par
                    dve.wait_ge(s[f"x_loaded{par}"], i * 16 + 16)
                    statistics(res(b), a_st[par], a_mv[par], "a_stats", 8 * b)
                for par in two:
                    b = i * 2 + par
                    dve.wait_ge(s["a_rstd"], 4 * b + 4)
                    normalise(a_xn[par], res(b), a_mv[par], a_rs[par][:, 1], "a_xn")
                for par in two:
                    b = i * 2 + par
                    dve.wait_ge(s["a_d2_ps"], b + 1)
                    if True:
                        dve.wait_ge(s["s_copy2"], 4)
                    for j in range(TILES):
                        c = slice(NSPLAT * j, NSPLAT * j + NSPLAT)
                        v.scalar_tensor_tensor(a_d2[par][:, j], a_rows[:], a_rs[par][:, 3, j:j + 1], bank[4 * par + 1][:, c],
                                               ALU.mult, ALU.add).then_inc(s["a_d2"], 1)
                    dve.wait_ge(s["a_d2"], 5 * b + 4)
                    v.tensor_scalar(a_d2[par][:], a_d2[par][:], 0.0, None, ALU.min).then_inc(s["a_d2"], 1)
                for par in two:
                    b = i * 2 + par
                    dve.wait_ge(s["a_gt_ps"], b + 1)
                    dve.wait_ge(s["a_gt"], b + 1)
                    v.tensor_scalar(a_m[par][:, P:P + 1], bank[4 * par + 2][0:NSPLAT, NSPLAT:NSPLAT + 1], small_s(4), None,
                                    ALU.mult).then_inc(s["a_m"], 1)
                    dve.wait_ge(s["a_m_ps"], b + 1)
                    v.tensor_scalar(a_m[par][:, 0:P], bank[4 * par + 1][0:NSPLAT, 0:P], small_s(4), None, ALU.mult)\
                     .then_inc(s["a_m"], 1)
                for par in two:
                    b = i * 2 + par
                    den = a_den[par]
                    for h in two:
                        dve.wait_ge(s["a_o_ps"], 2 * b + h + 1)
                        o = bank[4 * par + 3 * h][:, 0:2 * (P + 1)].rearrange("p (j f) -> p j f", j=2)
                        v.tensor_scalar(den[:, 0, 2 * h:2 * h + 2], o[:, :, P], EPS_SPLAT, None, ALU.add).then_inc(s["a_den"], 1)
                        dve.wait_ge(s["a_den"], 4 * b + 2 * h + 1)
                        v.reciprocal(den[:, 1, 2 * h:2 * h + 2], den[:, 0, 2 * h:2 * h + 2]).then_inc(s["a_den"], 1)
                        dve.wait_ge(s["a_den"], 4 * b + 2 * h + 2)
                        for j in two:
                            xb = res(b)(2 * h + j)
                            v.scalar_tensor_tensor(xb, o[:, j, 0:P], den[:, 1, 2 * h + j:2 * h + j + 1], xb, ALU.mult, ALU.add)\
                             .then_inc(s["a_x1"], 1)
                    dve.wait_ge(s["a_x1"], 4 * b + 4)
                    v.tensor_copy(idle[:, 0:1], idle[:, 1:2])
                    statistics(res(b), a_st[par], a_mv[par], "a_stats2", 8 * b)
                for par in two:
                    b = i * 2 + par
                    dve.wait_ge(s["a_rstd2"], 7 * b + 7)
                    normalise(a_xn[par], res(b), a_mv[par], a_rs[par][:, 5], "a_zn")
                for par in two:
                    b = i * 2 + par
                    dve.wait_ge(s["a_zt"], b + 1)
                    v.tensor_reduce(zmax[:, bass.ds(b, 1)], zt[:, bass.ds(b, 1)].rearrange("p a t -> p (a t)"), AX, ALU.max,
                                    apply_absolute_value=True).then_inc(s["a_zmax"], 1)
            dve.wait_ge(s["a_zmax"], B)
            v.tensor_reduce(zlim[:, 0:1], zmax[:], AX, ALU.max).then_inc(s["zlim_part"], 1)
            dve.wait_ge(s["zlim_all"], 1)
            lim = float(np.float32(QB - EPS_BETA)) / QB
            v.tensor_scalar(zlim[:, 2:3], zlim[:, 1:2], lim, None, ALU.mult).then_inc(s["zlim"], 1)
            v.tensor_scalar(zlim[:, 3:4], zlim[:, 1:2], -lim, None, ALU.mult).then_inc(s["zlim"], 1)
            dve.wait_ge(s["zlim"], 2)

            def clip(b):
                if not isinstance(b, int) or b > 0:
                    dve.wait_ge(s["x2"], 8 * b - 7)
                z = zt[:, b] if isinstance(b, int) else zt[:, bass.ds(b, 1)].rearrange("p a t -> p (a t)")
                v.tensor_scalar(zc[:], z, zlim[:, 2:3], zlim[:, 3:4], ALU.min, ALU.max).then_inc(s["zclip"], 1)

            def y(b, n):
                dve.wait_ge(s["pre_full"], n + 1)
                xb = xres[:, b] if isinstance(b, int) else xres[:, bass.ds(b, 1)].rearrange("p a j f -> p (a j) f")
                v.scalar_tensor_tensor(xb, PREB[:].rearrange("p (j f) -> p j f", j=TILES), small[:, 5:6], xb, ALU.mult, ALU.add)\
                 .then_inc(s["pre_free"], 1)
                dve.wait_ge(s["pre_free"], n + 1)
                v.tensor_copy(idle[:, 0:1], idle[:, 1:2])
                statistics(res(b), st2, mv2, "x2", 8 * b)

            def norm2(b):
                dve.wait_ge(s["rstd2"], 2 * b + 2)
                normalise(xn2, res(b), mv2, rs2[:, 1], "xn2_ready")

            def qkv(b, par, n, hf):
                k = 2 * b + hf
                dve.wait_ge(s["pre_full"], n + 1)
                tiles = slice(2 * hf, 2 * hf + 2)
                o = PREB[:, 0:2 * (RC + KC)].rearrange("p (j f) -> p j f", j=2)
                if not isinstance(k, int) or k > 0:
                    dve.wait_ge(s["rope_add"], k)
                v.tensor_tensor(rot_c[:], o[:, :, 0:RC], rope_c[:, tiles], ALU.mult).then_inc(s["rope_mul"], 1)
                for odd in two:
                    pair = lambda t, w: t.rearrange("p j (n two) -> p j n two", two=2)[:, :, :, w]
                    v.tensor_tensor(pair(rot_s[:], odd), pair(o[:, :, 0:RC], 1 - odd), pair(rope_s[:, tiles], odd), ALU.mult)\
                     .then_inc(s["rope_mul"], 1)
                v.tensor_copy(v_next[:, tiles], o[:, :, RC:RC + KC]).then_inc(s["pre_free"], 1)

            def values(b, par, n):
                dve.wait_ge(s["pre_free"], n)
                if not isinstance(b, int) or b >= 2:
                    dve.wait_ge(s["av_ps"], 4 * KVH * (b - 1))
                v.tensor_copy(vv[par][:, :, :, 0:HD], v_next[:].rearrange("p j (h d) -> p j h d", h=KVH)).then_inc(s["v_ready"], 1)

            def row_max(b, kv, u):
                qtile, h0, nh = MAX_UNITS[u]
                k = UNITS * (KVH * b + kv) + u
                n = P * (qtile + 1)
                dve.wait_ge(s["max_ps"], k + 1)
                v.tensor_reduce(negmax[kv % 2][:, qtile, h0:h0 + nh],
                                MAXB[(kv * UNITS + u) % 2][:, 0:nh * n].rearrange("p (h n) -> p h n", h=nh),
                                AX, ALU.max, negate=True).then_inc(s["max_done"], 1)

            def shift_parts(b, kv):
                g = KVH * b + kv
                dve.wait_ge(s["max_done"], UNITS * (g + 1))
                nm, sh = negmax[kv % 2], shift[kv % 2]
                v.tensor_copy(sh[:, :, 0], nm[:]).then_inc(s["shift_split"], 1)
                dve.wait_ge(s["shift_split"], 2 * g + 1)
                v.tensor_tensor(sh[:, :, 1], nm[:], sh[:, :, 0], ALU.subtract).then_inc(s["shift_split"], 1)

            def avt(b, par, kv, n):
                g = KVH * b + kv
                dve.wait_ge(s["post_full"], n + 1)
                o = POSTB[:].rearrange("p (j h c) -> p j h c", j=TILES, h=GRP)
                v.reciprocal(rden[:], o[:, :, :, HD]).then_inc(s["o_rden"], 1)
                dve.wait_ge(s["o_rden"], g + 1)
                v.tensor_tensor(o_tok[par][:, :, KC * kv:KC * kv + KC].rearrange("p j (h d) -> p j h d", h=GRP),
                                o[:, :, :, 0:HD], rden[:].unsqueeze(3).to_broadcast([P, TILES, GRP, HD]), ALU.mult)\
                 .then_inc(s["post_free"], 1)

            def outp(b, n):
                dve.wait_ge(s["post_full"], n + 1)
                dve.wait_ge(s["xbias"], b + 1)
                xb = xres[:, b] if isinstance(b, int) else xres[:, bass.ds(b, 1)].rearrange("p a j f -> p (a j) f")
                v.tensor_tensor(xb, POSTB[:].rearrange("p (j f) -> p j f", j=TILES), xb, ALU.add).then_inc(s["post_free"], 1)
                dve.wait_ge(s["post_free"], n + 1)
                v.tensor_copy(idle[:, 0:1], idle[:, 1:2])
                statistics(res(b), st3, mv3, "stats3", 8 * b)

            def norm3(b):
                dve.wait_ge(s["rstd3"], 2 * b + 2)
                normalise(xn3, res(b), mv3, rs3[:, 1], "xn3_ready")

            def router(b, par, past, n):
                dve.wait_ge(s["post_full"], n + 1)
                lg = POSTB[:, 0:TILES * NE].rearrange("p (j e) -> p j e", j=TILES)
                wide = lambda t: t.unsqueeze(2).to_broadcast([P, TILES, NE])
                v.tensor_reduce(lmax[:], lg, AX, ALU.max).then_inc(s["route"], 1)
                dve.wait_ge(s["route"], 5 * b + 1)
                v.tensor_tensor(top[:], lg, wide(lmax[:]), ALU.is_ge).then_inc(s["post_free"], 1)
                dve.wait_ge(s["post_free"], n + 1)
                v.tensor_tensor(top[:], top[:], priority[:].unsqueeze(1).to_broadcast([P, TILES, NE]), ALU.mult)\
                 .then_inc(s["route"], 1)
                dve.wait_ge(s["route"], 5 * b + 2)
                v.tensor_reduce(pri[:], top[:], AX, ALU.max).then_inc(s["route"], 1)
                dve.wait_ge(s["route"], 5 * b + 3)
                v.tensor_tensor(onehot[:], top[:], wide(pri[:]), ALU.is_equal).then_inc(s["route"], 1)
                dve.wait_ge(s["score_tanh"], b + 1)
                v.tensor_scalar(score[:, 1], score[:, 0], 0.5, 0.5, ALU.mult, ALU.add).then_inc(s["route"], 1)
                dve.wait_ge(s["route"], 5 * b + 5)
                dve.wait_ge(s[f"rows_sent{par}"], 16 * TILES * past)
                for j in range(TILES):
                    v.tensor_scalar(rows[par][:, j, 0:P], xn3[:, j], score[:, 1, j:j + 1], None, ALU.mult)\
                     .then_inc(s["expert_in"], 1)
                num = token_no[:, b] if isinstance(b, int) else token_no[:, bass.ds(b, 1)].rearrange("p a j -> p (a j)")
                v.tensor_copy(rows[par][:, :, 2 * P].bitcast(I32), num).then_inc(s["numbered"], 1)

            def gate(b, n, hf):
                dve.wait_ge(s["tanh_g"], 2 * b + hf + 1)
                v.scalar_tensor_tensor(sg[:], th[:], 1.0, POSTB[:], ALU.add, ALU.mult).then_inc(s["post_free"], 1)

            def up(b, n, hf):
                dve.wait_ge(s["post_full"], n + 1)
                v.tensor_tensor(hid[:, hf], sg[:], POSTB[:], ALU.mult).then_inc(s["post_free"], 1)

            def rank(b, par, past, n):
                dve.wait_ge(s["post_full"], n + 1)
                r = POSTB[:, 0:TILES * NE].rearrange("p (j e) -> p j e", j=TILES)
                v.tensor_tensor(place[:], r, e_base[:].unsqueeze(1).to_broadcast([P, TILES, NE]), ALU.add)\
                 .then_inc(s["place_ready"], 1)
                v.tensor_copy(onehot_f[:], onehot[:]).then_inc(s["place_ready"], 1)
                dve.wait_ge(s["place_ready"], 5 * b + 2)
                v.tensor_tensor(place[:], place[:], onehot_f[:], ALU.mult).then_inc(s["place_ready"], 1)
                v.tensor_tensor(e_base[:], POSTB[:, TILES * NE:(TILES + 1) * NE], e_base[:], ALU.add)\
                 .then_inc(s["post_free"], 1)
                dve.wait_ge(s["place_ready"], 5 * b + 3)
                v.tensor_reduce(place_s[:], place[:], AX, ALU.add).then_inc(s["place_ready"], 1)
                dve.wait_ge(s["place_ready"], 5 * b + 4)
                v.tensor_copy(place_i[par][:], place_s[:]).then_inc(s["place_ready"], 1)

            def carry(b, par, n):
                dve.wait_ge(s["post_full"], n + 1)
                xb = xres[:, b] if isinstance(b, int) else xres[:, bass.ds(b, 1)].rearrange("p a j f -> p (a j) f")
                v.scalar_tensor_tensor(rows[par][:, :, P:2 * P], POSTB[:].rearrange("p (j f) -> p j f", j=TILES), 0.5, xb,
                                       ALU.mult, ALU.add).then_inc(s["post_free"], 1)

            for n, (name, b) in enumerate(HEAD):
                if name == "Y":
                    clip(b)
                    y(b, n)
                    norm2(b)
                elif name in ("QKV0", "QKV1"):
                    qkv(b, b % 2, n, int(name[3]))
                    if (name, b) == ("QKV1", 0):
                        values(0, 0, n + 1)
            for kv in range(2):
                for u in range(UNITS):
                    row_max(0, kv, u)
                if kv == 0:
                    shift_parts(0, 0)

            def body(b, par, past, prev=True, nxt=True):
                order, _ = plan(prev, nxt)
                before_prev = past + par - 1 if not isinstance(past, int) or prev else 0
                for kv in range(KVH):
                    for u in range(UNITS):
                        m = (b, kv + 2) if kv < 2 else (b + 1, kv - 2)
                        if kv < 2 or nxt:
                            row_max(*m, u)
                        if u == 0 and (kv < 3 or nxt):
                            shift_parts(*((b, kv + 1) if kv < 3 else (b + 1, 0)))
                        for name, off, n in order.get((kv, u), ()):
                            pre, post = pre_use(b, n), post_use(b, n)
                            if name == "Y":
                                y(b + 2, pre)
                            elif name in ("QKV0", "QKV1"):
                                qkv(b + 2, par, pre, int(name[3]))
                            elif name == "AVT":
                                avt(*((b, par, kv - 1) if off == 0 else (b - 1, 1 - par, KVH - 1)), post)
                            elif name == "OUTP":
                                outp(b - 1, post)
                            elif name == "ROUTER":
                                router(b - 1, 1 - par, before_prev, post)
                            elif name in ("GATE0", "GATE1"):
                                gate(b - 1, post, int(name[4]))
                            elif name in ("UP0", "UP1"):
                                up(b - 1, post, int(name[2]))
                            elif name == "RANK":
                                rank(b - 1, 1 - par, before_prev, post)
                            elif name == "DOWN":
                                carry(b - 1, 1 - par, post)
                        if (kv, u) == (0, 9) and prev:
                            norm3(b - 1)
                        if (kv, u) == (0, 7) and nxt:
                            values(b + 1, 1 - par, bank_uses("QKV1", b + 1))
                        if (kv, u) == (2, 1) and nxt:
                            clip(b + 2)
                        if (kv, u) == (2, 8) and nxt:
                            norm2(b + 2)

            body(0, 0, 0, prev=False)
            with dve.Fori(0, B // 2 - 1) as i:
                body(i * 2 + 1, 1, i)
                body(i * 2 + 2, 0, i + 1)
            body(B - 1, 1, B // 2 - 1, nxt=False)
            last = post_use(B, 0)
            avt(B - 1, 1, KVH - 1, last)
            for n, name in enumerate(TAIL):
                n += last + 1
                if name == "OUTP":
                    outp(B - 1, n)
                    norm3(B - 1)
                elif name == "ROUTER":
                    router(B - 1, 1, B // 2 - 1, n)
                elif name in ("GATE0", "GATE1"):
                    gate(B - 1, n, int(name[4]))
                elif name in ("UP0", "UP1"):
                    up(B - 1, n, int(name[2]))
                elif name == "RANK":
                    rank(B - 1, 1, B // 2 - 1, n)
                    dve.wait_ge(s["post_free"], n + 1)
                    v.tensor_copy(base_i[:], e_base[0:1, :]).then_inc(s["table"], 1)
                    v.tensor_tensor(cnt[:], e_base[:], e_start[:], ALU.subtract).then_inc(s["table"], 1)
                    dve.wait_ge(s["table"], 2)
                    v.tensor_tensor(full[:], cnt[:].unsqueeze(2).to_broadcast([P, NE, B * T // P]), steps[:], ALU.is_gt)\
                     .then_inc(s["table"], 1)
                    dve.wait_ge(s["table"], 3)
                    v.tensor_reduce(ntile[:], full[:], AX, ALU.add).then_inc(s["table"], 1)
                    dve.wait_ge(s["table"], 4)
                    v.tensor_tensor_scan(ends[:], ones[:, 0:NE], ntile[:], 0.0, ALU.mult, ALU.add).then_inc(s["table"], 1)
                    dve.wait_ge(s["table"], 5)
                    v.tensor_scalar(ended[:], ends[:], slot_no[:, 0:1], None, ALU.is_le).then_inc(s["table"], 1)
                    dve.wait_ge(s["table"], 6)
                    v.tensor_reduce(s_val[:, 0:1], ended[:], AX, ALU.add).then_inc(s["table"], 1)
                    v.tensor_tensor(s_tmp[:], ended[:], ntile[:], ALU.mult).then_inc(s["table"], 1)
                    dve.wait_ge(s["table"], 8)
                    v.tensor_reduce(s_val[:, 1:2], s_tmp[:], AX, ALU.add).then_inc(s["table"], 1)
                    v.tensor_scalar(s_tab[:, 1:2], s_val[:, 0:1], float(NE - 1), None, ALU.min).then_inc(s["table"], 1)
                    dve.wait_ge(s["table"], 10)
                    v.tensor_tensor(s_val[:, 2:3], slot_no[:], s_val[:, 1:2], ALU.subtract).then_inc(s["table"], 1)
                    v.tensor_scalar(s_val[:, 3:4], s_val[:, 0:1], float(CAP), None, ALU.mult).then_inc(s["table"], 1)
                    dve.wait_ge(s["table"], 12)
                    v.scalar_tensor_tensor(s_tab[:, 0:1], s_val[:, 2:3], float(P), s_val[:, 3:4], ALU.mult, ALU.add)\
                     .then_inc(s["table"], 1)
                elif name == "DOWN":
                    carry(B - 1, 1, n)
            dve.wait_ge(s["table_ps"], 1)
            v.tensor_copy(s_row[:], bank[0][0:2, 0:P]).then_inc(s["table_ready"], 1)

            def d_step(n, r):
                p = r % 2
                dve.wait_ge(s["d_tanh"], n + 1)
                v.scalar_tensor_tensor(d_th[p][:], d_th[p][:], 1.0, bank[2 + p][:, 0:FE], ALU.add, ALU.mult)\
                 .then_inc(s["d_sg"], 1)
                dve.wait_ge(s["d_sg"], n + 1)
                if not isinstance(n, int) or n >= 2:
                    dve.wait_ge(s["d_ht_ps"], n - 1)
                v.tensor_tensor(d_h[p][:], d_th[p][:], bank[2 + p][:, FE:2 * FE], ALU.mult).then_inc(s["d_hid"], 1)

            def d_output(n, r, past):
                dve.wait_ge(s["d_dn_ps"], n + 1)
                dve.wait_ge(s[f"out_sent{r}"], 16 * past)
                dve.wait_ge(s[f"slot_in{r}"], 16 * past + 16)
                v.scalar_tensor_tensor(d_out[r][:], bank[6 + r % 2][:, 0:P], 0.5, slot[r][:, P:2 * P], ALU.mult, ALU.add)\
                 .then_inc(s["d_out_ready"], 1)

            d_step(0, 0)
            loops = (SLOTS - 2) // OUT_R
            with dve.Fori(0, loops) as i:
                for r in range(OUT_R):
                    d_step(i * OUT_R + 1 + r, (1 + r) % OUT_R)
                    d_output(i * OUT_R + r, r, i)
            for n in range(1 + loops * OUT_R, SLOTS + 1):
                if n < SLOTS:
                    d_step(n, n % OUT_R)
                d_output(n - 1, (n - 1) % OUT_R, (n - 1) // OUT_R)

        @block.tensor
        def _(pe):
            t = nc.tensor
            mm = lambda o, l, r, start=True, stop=True: t.matmul(o, l, r, start=start, stop=stop)
            pe.wait_ge(s["ident_ready"], 5)
            pe.wait_ge(s["w_attn"], 16 * 8)
            pe.wait_ge(s["s_dve"], 8)
            pe.wait_ge(s["w_moe"], 64)
            turn = lambda o, i: t.transpose(o, i, ident[0:i.shape[0], 0:i.shape[0]]).then_inc(s["s_pe1"], 1)
            turn(bank[0][:, 0:128], w_in["wv"][:])
            turn(bank[0][:, 128:192], scaled_p[:])
            turn(bank[0][0:64, 192:320], w_in["wqa"][:])
            turn(bank[0][0:32, 320:448], w_in["wkva"][:])
            turn(bank[0][:, 448:464], w_in["router"][:])
            for c in two:
                turn(bank[1][:, P * c:P * c + P], w_in["wg"][:, c])
                turn(bank[1][:, 256 + P * c:256 + P * c + P], w_in["wu"][:, c])
                turn(bank[2][:, P * c:P * c + P], w_in["wd"][:, P * c:P * c + P])
            pe.wait_ge(s["s_copy1"], 8)
            pe.wait_ge(s["const_dve"], 2)
            kv_cols = w_in["wkvb"][:].rearrange("p (n two) -> p n two", two=2)
            mm(bank[3][:, 0:128], wvt[:], w_in["wo"][:]).then_inc(s["s_pe2"], 1)
            mm(bank[3][:, 128:256], wqat[:], w_in["wqb"][:]).then_inc(s["s_pe2"], 1)
            mm(bank[3][:, 256:288], wkvat[:], kv_cols[:, :, 0]).then_inc(s["s_pe2"], 1)
            mm(bank[3][:, 288:320], wkvat[:], kv_cols[:, :, 1]).then_inc(s["s_pe2"], 1)
            mm(bank[3][:, 320:384], ones[0:NSPLAT, :], diag_a[:]).then_inc(s["s_pe2"], 1)
            mm(bank[3][:, 384:512], ones[0:1, :], w_in["bout"][:]).then_inc(s["s_pe2"], 1)
            pe.wait_ge(s["s_copy2"], 4)

            def turn_tiles(dst, src, idn=None):
                for j in range(TILES):
                    last = t.transpose(dst[:, P * j:P * j + P], src(j), ident[:])
                return last

            with pe.Fori(0, B // 2) as i:
                for par in two:
                    b = i * 2 + par
                    pe.wait_ge(s["a_xn"], 4 * b + 4)
                    pe.wait_ge(s["a_x1"], 4 * b - 4 if False else 4 * (i * 2))
                    turn_tiles(bank[4 * par], lambda j: a_xn[par][:, j]).then_inc(s["a_xt_ps"], 1)
                for par in two:
                    b = i * 2 + par
                    pe.wait_ge(s["a_xt"], b + 1)
                    pe.wait_ge(s["a_m"], 4 * i)
                    for j in range(TILES):
                        o = bank[4 * par + 1][:, NSPLAT * j:NSPLAT * j + NSPLAT]
                        mm(o, a_xt[par][:, P * j:P * j + P], splat_t[:], stop=False)
                        last = mm(o, ones[0:NSPLAT, :], diag_p[:], start=False)
                    last.then_inc(s["a_d2_ps"], 1)
                for par in two:
                    b = i * 2 + par
                    pe.wait_ge(s["a_e"], b + 1)
                    pe.wait_ge(s["a_zt"], 2 * i)
                    pe.wait_ge(s["a_x1"], 8 * i)
                    for j in range(TILES):
                        mm(bank[4 * par + 2][:, 0:NSPLAT], a_xn[par][:, j], a_e[par][:, j], j == 0, j == TILES - 1)
                    for j in range(TILES):
                        last = mm(bank[4 * par + 2][0:NSPLAT, NSPLAT:NSPLAT + 1], a_e[par][:, j], ones[:, 0:1], j == 0, j == TILES - 1)
                    last.then_inc(s["a_gt_ps"], 1)
                    for j in range(TILES):
                        last = t.transpose(bank[4 * par + 3][0:NSPLAT, P * j:P * j + P], a_e[par][:, j], ident[:])
                    last.then_inc(s["a_et_ps"], 1)
                for par in two:
                    b = i * 2 + par
                    pe.wait_ge(s["a_gt"], b + 1)
                    pe.wait_ge(s["a_d2"], 5 * b + 4)
                    mm(bank[4 * par + 1][0:NSPLAT, 0:P], a_gt[par][:], wvo[:]).then_inc(s["a_m_ps"], 1)
                for par in two:
                    b = i * 2 + par
                    pe.wait_ge(s["a_m"], 2 * b + 2)
                    pe.wait_ge(s["a_et"], b + 1)
                    for h in two:
                        for j in two:
                            tile = 2 * h + j
                            last = mm(bank[4 * par + 3 * h][:, (P + 1) * j:(P + 1) * (j + 1)], a_et[par][:, P * tile:P * tile + P], a_m[par][:])
                        last.then_inc(s["a_o_ps"], 1)
                for par in two:
                    b = i * 2 + par
                    pe.wait_ge(s["a_zn"], 4 * b + 4)
                    turn_tiles(bank[4 * par + 2], lambda j: a_xn[par][:, j]).then_inc(s["a_zt_ps"], 1)
            pe.wait_ge(s["a_zt"], B)
            pe.wait_ge(s["w_rope"], 32)

            def pre_bank(n):
                if not isinstance(n, int) or n > 0:
                    pe.wait_ge(s["pre_free"], n)

            def post_bank(n):
                if not isinstance(n, int) or n > 0:
                    pe.wait_ge(s["post_free"], n)

            def y(b, n):
                pre_bank(n)
                pe.wait_ge(s["zclip"], b + 1)
                for j in range(TILES):
                    last = mm(PREB[:, P * j:P * j + P], zc[:, P * j:P * j + P], wq[:])
                last.then_inc(s["pre_full"], 1)

            def t2(b, n):
                pre_bank(n)
                pe.wait_ge(s["xn2_ready"], 4 * b + 4)
                turn_tiles(PREB, lambda j: xn2[:, j]).then_inc(s["pre_full"], 1)

            def qkv(b, n, hf):
                pre_bank(n)
                for j in two:
                    c = P * (2 * hf + j)
                    last = mm(PREB[:, (RC + KC) * j:(RC + KC) * (j + 1)], xt2[:, c:c + P], wqkv[:])
                last.then_inc(s["pre_full"], 1)

            def split_a(b, n):
                pre_bank(n)
                pe.wait_ge(s["part_lo"], 2 * b + 2)
                both = PREB[:].bitcast(BF16)
                for c in two:
                    for j in range(TILES):
                        last = t.transpose(both[:, T * c + P * j:T * c + P * j + P], parts[:, j, 0:QC, c], identb[:])
                last.then_inc(s["pre_full"], 1)

            def split_b(b, n):
                pre_bank(n)
                both = PREB[:].bitcast(BF16)
                for j in range(TILES):
                    t.transpose(both[:, P * j:P * j + P], parts[:, j, 0:QC, 2], identb[:])
                for j in range(TILES):
                    last = t.transpose(both[0:3 * KC, T + P * j:T + P * j + P], parts[:, j, QC:RC].rearrange("p k c -> p (k c)"), identb[:])
                last.then_inc(s["pre_full"], 1)

            def ct(gb, kv, n):
                pre_bank(n)
                pe.wait_ge(s["shift_split"], 2 * (KVH * gb + kv) + 2)
                both = PREB[:].bitcast(BF16)
                for j in range(TILES):
                    last = t.transpose(both[0:2 * GRP, P * j:P * j + P], shift[kv % 2][:, j], identb[:])
                last.then_inc(s["pre_full"], 1)

            def avt(b, kv, n):
                post_bank(n)
                pe.wait_ge(s["av_copied"], KVH * b + kv + 1)
                turn_tiles(POSTB, lambda j: av_sb[kv % 2][:, P * j:P * j + P]).then_inc(s["post_full"], 1)

            def ot(b, par, n):
                post_bank(n)
                turn_tiles(POSTB, lambda j: o_tok[par][:, j]).then_inc(s["post_full"], 1)

            def outp(b, n):
                post_bank(n)
                for j in range(TILES):
                    last = mm(POSTB[:, P * j:P * j + P], o_t[:, P * j:P * j + P], w_in["wout"][:])
                last.then_inc(s["post_full"], 1)

            def t3(b, n):
                post_bank(n)
                pe.wait_ge(s["xn3_ready"], 4 * b + 4)
                turn_tiles(POSTB, lambda j: xn3[:, j]).then_inc(s["post_full"], 1)

            def router(b, n):
                post_bank(n)
                for j in range(TILES):
                    last = mm(POSTB[:, NE * j:NE * j + NE], xt3[:, P * j:P * j + P], router_t[:])
                last.then_inc(s["post_full"], 1)

            def inner(b, n, w, hf):
                post_bank(n)
                mm(POSTB[:], w[:, P * hf:P * hf + P], xt3[:]).then_inc(s["post_full"], 1)

            def rank(b, n):
                post_bank(n)
                pe.wait_ge(s["route"], 5 * b + 4)
                for j in range(TILES):
                    o = POSTB[:, NE * j:NE * j + NE]
                    for k in range(j):
                        mm(o, onesb[:], onehot[:, k], k == 0, False)
                    mm(o, before[:], onehot[:, j], j == 0, True)
                for k in range(TILES):
                    last = mm(POSTB[:, TILES * NE:(TILES + 1) * NE], onesb[:], onehot[:, k], k == 0, k == TILES - 1)
                last.then_inc(s["post_full"], 1)

            def down_shared(b, n):
                post_bank(n)
                for j in range(TILES):
                    for c in two:
                        last = mm(POSTB[:, P * j:P * j + P], hid[:, c, P * j:P * j + P], down_t[:, c], c == 0, c == 1)
                last.then_inc(s["post_full"], 1)

            def max_unit(b, par, past, kv, u):
                qtile, h0, nh = MAX_UNITS[u]
                k = UNITS * (KVH * b + kv) + u
                if kv == 0 and u == 0:
                    pe.wait_ge(s[f"parts_loaded{par}"], 12 * 16 * past + 12 * 16)
                if not isinstance(k, int) or k >= 2:
                    pe.wait_ge(s["max_done"], k - 1)
                n = P * (qtile + 1)
                o = MAXB[(kv * UNITS + u) % 2]
                for h in range(nh):
                    q = q8[par][0:64, GRP * kv + h0 + h, P * qtile:P * qtile + P]
                    mm(o[:, n * h:n * h + n], q, k8[par][0:64, kv, 0:n], True, False)
                    last = mm(o[:, n * h + n - P:n * h + n], identb[:], causal[:], False, True)
                last.then_inc(s["max_ps"], 1)

            def score_unit(b, par, past, kv, u):
                ktile, h0, nh = SCORE_UNITS[u]
                g = KVH * b + kv
                if u == 0:
                    pe.wait_ge(s[f"shift_loaded{kv % 2}"], 16 * (2 * b + kv // 2) + 16)
                back, was = prior(u, SC_BANKS)
                if not (isinstance(b, int) and b == 0 and kv == 0) or back == 0:
                    pe.wait_ge(s["exp_done"], UNITS * (g - back) + was + 1)
                n = T - P * ktile
                for h in range(nh):
                    last = mm(SCB[u % SC_BANKS][:, n * h:n * h + n], k8[par][:, kv, P * ktile:P * ktile + P],
                              q8[par][:, GRP * kv + h0 + h, P * ktile:T])
                last.then_inc(s["score_ps"], 1)

            def av(b, par, kv, ktile):
                g = KVH * b + kv
                pe.wait_ge(s["masked"], UNITS * g + LAST_OF_TILE[ktile] + 1)
                if ktile == 0:
                    if kv == 0:
                        pe.wait_ge(s["v_ready"], b + 1)
                    if not (isinstance(b, int) and b == 0 and kv == 0):
                        pe.wait_ge(s["av_copied"], g)
                n = T - P * ktile
                for u, (kt_, h0, nh) in enumerate(SCORE_UNITS):
                    if kt_ != ktile:
                        continue
                    for h in range(nh):
                        c = 32 * (h0 + h)
                        last = t.matmul(AVB[c:c + 32, P * ktile:T], vv[par][:, ktile, kv], w_ring[u % W_RING][:, n * h:n * h + n],
                                        start=ktile == 0, stop=ktile == TILES - 1)
                last.then_inc(s["av_ps"], 1)

            for n, (name, b) in enumerate(HEAD):
                {"Y": y, "T2": t2, "SPLITA": split_a, "SPLITB": split_b}[name](b, n) if name[0] != "Q" else qkv(b, n, int(name[3]))
            for kv in range(2):
                for u in range(UNITS):
                    max_unit(0, 0, 0, kv, u)
            ct(0, 0, HEAD_USES - 1)

            def body(b, par, past, prev=True, nxt=True):
                order, _ = plan(prev, nxt)
                for kv in range(KVH):
                    for u in range(UNITS):
                        for name, off, n in order.get((kv, u), ()):
                            pre, post = pre_use(b, n), post_use(b, n)
                            if name == "Y":
                                y(b + 2, pre)
                            elif name == "T2":
                                t2(b + 2, pre)
                            elif name in ("QKV0", "QKV1"):
                                qkv(b + 2, pre, int(name[3]))
                            elif name == "SPLITA":
                                split_a(b + 1, pre)
                            elif name == "SPLITB":
                                split_b(b + 1, pre)
                            elif name == "CT":
                                ct(b + off, CT_OF[kv], pre)
                            elif name == "AVT":
                                avt(*((b, kv - 1) if off == 0 else (b - 1, KVH - 1)), post)
                            elif name == "OT":
                                ot(b - 1, 1 - par, post)
                            elif name == "OUTP":
                                outp(b - 1, post)
                            elif name == "T3":
                                t3(b - 1, post)
                            elif name == "ROUTER":
                                router(b - 1, post)
                            elif name in ("GATE0", "GATE1"):
                                inner(b - 1, post, gate_t, int(name[4]))
                            elif name in ("UP0", "UP1"):
                                inner(b - 1, post, up_t, int(name[2]))
                            elif name == "RANK":
                                rank(b - 1, post)
                            elif name == "DOWN":
                                down_shared(b - 1, post)
                        if kv < 2:
                            max_unit(b, par, past, kv + 2, u)
                        elif nxt:
                            max_unit(b + 1, 1 - par, past + par, kv - 2, u)
                        score_unit(b, par, past, kv, u)
                        if u < 2 and (prev or kv):
                            av(*((b, par, kv - 1) if kv else (b - 1, 1 - par, KVH - 1)), u + 2)
                        if u == 5:
                            av(b, par, kv, 0)
                        if u == 9:
                            av(b, par, kv, 1)

            body(0, 0, 0, prev=False)
            with pe.Fori(0, B // 2 - 1) as i:
                body(i * 2 + 1, 1, i)
                body(i * 2 + 2, 0, i + 1)
            body(B - 1, 1, B // 2 - 1, nxt=False)
            av(B - 1, 1, KVH - 1, 2)
            av(B - 1, 1, KVH - 1, 3)
            last_post = post_use(B, 0)
            avt(B - 1, KVH - 1, last_post)
            for n, name in enumerate(TAIL):
                n += last_post + 1
                if name == "OT":
                    ot(B - 1, 1, n)
                elif name == "OUTP":
                    outp(B - 1, n)
                elif name == "T3":
                    t3(B - 1, n)
                elif name == "ROUTER":
                    router(B - 1, n)
                elif name in ("GATE0", "GATE1"):
                    inner(B - 1, n, gate_t, int(name[4]))
                elif name in ("UP0", "UP1"):
                    inner(B - 1, n, up_t, int(name[2]))
                elif name == "RANK":
                    rank(B - 1, n)
                elif name == "DOWN":
                    down_shared(B - 1, n)
            pe.wait_ge(s["table"], 13)
            t.transpose(bank[0][0:2, 0:P], s_tab[:], ident[:]).then_inc(s["table_ps"], 1)
            pe.wait_ge(s["table_ready"], 1)
            pe.wait_ge(s["post_free"], last_post + 1 + len(TAIL))
            pe.wait_ge(s["w_experts"], 32)

            def d_turn(n, r, past, waits=True):
                pe.wait_ge(s[f"slot_in{r % OUT_R}"], 16 * past + 16)
                if waits:
                    pe.wait_ge(s["d_xt_ready"], n - 1)
                t.transpose(bank[r % 2][:, 0:P], slot[r % OUT_R][:, 0:P], ident[:]).then_inc(s["d_xt_ps"], 1)

            def d_gate_up(n, r):
                e = pe.value_load(s_row[1:2, bass.ds(n, 1)], min_val=0, max_val=NE - 1)
                pe.wait_ge(s["d_xt_ready"], n + 1)
                if not isinstance(n, int) or n >= 2:
                    pe.wait_ge(s["d_hid"], n - 1)
                mm(bank[2 + r % 2][:], d_xt[r % 2][:], gate_up[:, bass.ds(e, 1)].rearrange("p a f -> p (a f)"))\
                  .then_inc(s["d_gu_ps"], 1)
                return e

            def d_down(n, r, e):
                pe.wait_ge(s["d_hid"], n + 1)
                if not isinstance(n, int) or n >= 2:
                    pe.wait_ge(s["d_ht_ready"], n - 1)
                for c in two:
                    last = t.transpose(bank[4 + r % 2][:, P * c:P * c + P], d_h[r % 2][:, P * c:P * c + P], ident[:])
                last.then_inc(s["d_ht_ps"], 1)
                pe.wait_ge(s["d_ht_ready"], n + 1)
                if not isinstance(n, int) or n >= 2:
                    pe.wait_ge(s["d_out_ready"], n - 1)
                for c in two:
                    last = mm(bank[6 + r % 2][:, 0:P], d_ht[r % 2][:, P * c:P * c + P],
                              down[:, bass.ds(e, 1), c].rearrange("p a f -> p (a f)"), c == 0, c == 1)
                last.then_inc(s["d_dn_ps"], 1)

            d_turn(0, 0, 0, waits=False)
            d_gate_up(0, 0)
            d_turn(1, 1, 0, waits=False)
            loops = (SLOTS - 2) // OUT_R

            def d_four(i):
                for r in range(OUT_R):
                    n = i * OUT_R + 1 + r
                    d_gate_up(n, 1 + r)
                    d_turn(n + 1, 2 + r, i + (2 + r) // OUT_R)
                    e = pe.value_load(s_row[1:2, bass.ds(i * OUT_R + r, 1)], min_val=0, max_val=NE - 1)
                    d_down(i * OUT_R + r, r, e)

            d_four(0)
            with pe.Fori(1, loops) as i:
                d_four(i)
            for n in range(1 + loops * OUT_R, SLOTS + 1):
                if n < SLOTS:
                    d_gate_up(n, n % OUT_R)
                if n + 1 < SLOTS:
                    d_turn(n + 1, (n + 1) % OUT_R, (n + 1) // OUT_R)
                e = pe.value_load(s_row[1:2, n - 1:n], min_val=0, max_val=NE - 1)
                d_down(n - 1, (n - 1) % OUT_R, e)


_NAMES = {"x": "L0_attn_token_embeddings", "p": "L0_attn_splat_positions", "logs": "L0_attn_splat_log_scales",
          "amp": "L0_attn_splat_amplitudes", "wv": "L0_attn_Wv", "wo": "L0_attn_Wo", "wffn": "L0_ffn_weight",
          "gamma": "L0_ffn_ln_gamma", "beta": "L0_ffn_ln_beta", "wqa": "L1_attn_Wqa", "wqb": "L1_attn_Wqb",
          "wkva": "L1_attn_Wkva", "wkvb": "L1_attn_Wkvb", "wout": "L1_attn_Wout", "bout": "L1_attn_bout",
          "router": "L1_ffn_w_router", "gate_up": "L1_ffn_gate_up_proj", "down": "L1_ffn_down_proj",
          "wg": "L1_ffn_w_gate", "wu": "L1_ffn_w_up", "wd": "L1_ffn_w_down"}


def rope_tables():
    inv = (1.0 / 10000.0 ** (np.arange(0, HD, 2, dtype=np.float32) / np.float32(HD))).astype(np.float32)
    ang = np.outer(np.arange(T, dtype=np.float32), inv).astype(np.float32)
    cos = np.repeat(np.cos(ang), 2, axis=1)
    sin = np.repeat(np.sin(ang), 2, axis=1) * np.tile([-1.0, 1.0], HD // 2)
    out = []
    for t in (cos, sin):
        full = np.concatenate([np.tile(t, (1, H)) * HD ** -0.5, np.tile(t, (1, KVH))], axis=1)
        out.append(np.ascontiguousarray(full.reshape(TILES, P, RC).transpose(1, 0, 2).astype(np.float32)))
    return out


def kernel(**inputs):
    import numpy as _np
    import concourse.bacc as _bacc
    from concourse.bass_utils import run_bass_kernel_spmd as _run

    nc = _bacc.Bacc("TRN2", target_bir_lowering=False, num_devices=1)
    rope_c, rope_s = rope_tables()
    arrays = {n: _np.ascontiguousarray(inputs[full]) for n, full in _NAMES.items()} | {"rope_c": rope_c, "rope_s": rope_s}
    ins = {n: nc.dram_tensor(f"in_{n}", a.shape, mybir.dt.from_np(a.dtype), kind="ExternalInput").ap()
           for n, a in arrays.items()}
    out = nc.dram_tensor("out_rows", (B, T, P), F32, kind="ExternalOutput").ap()
    build(nc, ins, out)
    r = _run(nc, [{f"in_{n}": a for n, a in arrays.items()}], core_ids=[0])
    return r.results[0]["out_rows"]
```

```python
from contextlib import ExitStack

import numpy as np
import concourse.bass as bass
from concourse import mybir

F32, BF16 = mybir.dt.float32, mybir.dt.bfloat16
I32, U32 = mybir.dt.int32, mybir.dt.uint32
ALU = mybir.AluOpType
ACT = mybir.ActivationFunctionType
AX = mybir.AxisListType.X
REDUCE_ADD, REDUCE_MAX = bass.bass_isa.ReduceOp.add, bass.bass_isa.ReduceOp.max

P = 128
B, T = 8, 512
TILES = T // P
NSPLAT = 64
H, KVH, HD = 16, 4, 8
GRP = H // KVH
QC, KC = H * HD, KVH * HD
RC = QC + KC
NE, FE = 16, 256
LN_EPS, FFN_LN_EPS, EPS_BETA, EPS_SPLAT = 1e-5, 1e-3, 1e-5, 1e-8
QB = 128.0
MASKED = -1e30
CAP = B * T + P
ROW = 2 * P + 1
NOBODY = B * T
SLOTS = B * T // P + NE - 1
OUT_R = 8
FULL = (SLOTS - 2) // OUT_R
LANES, ROUNDS = 4, B // 4

MAX_UNITS = [(0, 0, 4), (1, 0, 2), (1, 2, 2)] + [(2, h, 1) for h in range(4)] + [(3, h, 1) for h in range(4)]
SCORE_UNITS = [(0, h, 1) for h in range(4)] + [(1, h, 1) for h in range(4)] + [(2, 0, 2), (2, 2, 2), (3, 0, 4)]
UNITS = len(SCORE_UNITS)
LAST_OF_TILE = [3, 7, 9, 10]
W_RING = UNITS
AV_AT = {8: (0, 0), 0: (1, 1), 2: (1, 2), 3: (1, 3)}
AV_COPY_AT, NORM3_AT, CLIP_AT, NORM2_AT, VALUES_AT = 4, (1, 3), (1, 6), (2, 2), (0, 9)
SC_BANKS = 3

PLAN = {
    (0, 3): [("CT", 0)], (0, 5): [("SPLITA", 1)], (0, 6): [("AVT", -1)], (0, 7): [("SPLITB", 1)], (0, 8): [("OT", -1)],
    (0, 10): [("OUTP", -1)],
    (1, 3): [("CT", 0)], (1, 5): [("T3", -1)], (1, 7): [("ROUTER", -1)], (1, 8): [("Y", 2)], (1, 9): [("AVT", 0)],
    (2, 0): [("GATE0", -1)], (2, 1): [("UP0", -1)], (2, 3): [("CT", 0), ("GATE1", -1)], (2, 4): [("UP1", -1)],
    (2, 6): [("T2", 2)], (2, 7): [("AVT", 0)], (2, 9): [("QKV0", 2)], (2, 10): [("RANK", -1)],
    (3, 1): [("QKV1", 2)], (3, 2): [("DOWN", -1)], (3, 3): [("CT", 1)], (3, 7): [("AVT", 0)],
}
DVE_STEPS = {n: [(n, 0)] for n in ("Y", "QKV0", "QKV1", "AVT", "OUTP", "UP0", "UP1", "RANK", "DOWN")} | {
    "GATE0": [("GATE0", 1)], "GATE1": [("GATE1", 1)], "ROUTER": [("ROUTER", 0), ("EXPERT_IN", 2)]}
ACT_STEPS = {n: [(n, 0)] for n in ("T2", "SPLITA", "SPLITB", "CT", "OT", "T3", "GATE0", "GATE1")} | {
    "ROUTER": [("ROUTER", 1)], "QKV0": [("HIGH", 2), ("MID", 4)], "QKV1": [("HIGH", 2), ("MID", 4)]}
POOL_STEPS = {"Y": [("ROOT2", 2), ("XBIAS", 7)], "OUTP": [("ROOT3", 3)], "DOWN": [(f"SCATTER{j}", j + 1) for j in range(TILES)],
              "QKV0": [("ADD", 1), ("REST", 3), ("LOW", 5)], "QKV1": [("ADD", 1), ("REST", 3), ("LOW", 5)]}
PRE_PIECES = ("Y", "T2", "QKV0", "QKV1", "SPLITA", "SPLITB", "CT", "UP0", "UP1")
CT_OF = {0: 1, 1: 2, 2: 3, 3: 0}


def plan(prev, nxt):
    out, n = {}, {"pre": 0, "post": 0}
    for kv in range(KVH):
        for u in range(UNITS):
            for name, off in PLAN.get((kv, u), ()):
                if (off < 0 and not prev) or (off > 0 and not nxt):
                    continue
                bank = "pre" if name in PRE_PIECES else "post"
                out.setdefault((kv, u), []).append((name, off, n[bank]))
                n[bank] += 1
    return out, n


def steps_of(order, steps):
    out = {}
    for (kv, u), pieces in order.items():
        for name, off, n in pieces:
            for step, delay in steps.get(name, ()):
                out.setdefault(divmod(kv * UNITS + u + delay, UNITS), []).append((step, name, off, n))
    return out


PRE_USES, POST_USES = plan(True, True)[1]["pre"], plan(True, True)[1]["post"]
HEAD = [("Y", 0), ("T2", 0), ("QKV0", 0), ("QKV1", 0), ("SPLITA", 0), ("SPLITB", 0),
        ("Y", 1), ("T2", 1), ("QKV0", 1), ("QKV1", 1)]
HEAD_USES = len(HEAD) + 1
FIRST_PRE, FIRST_POST = plan(False, True)[1]["pre"], plan(False, True)[1]["post"]
TAIL = ["OT", "OUTP", "T3", "ROUTER", "RANK", "GATE0", "UP0", "GATE1", "UP1", "DOWN"]


def pre_use(b, n):
    return HEAD_USES + (n if isinstance(b, int) and b == 0 else FIRST_PRE + PRE_USES * (b - 1) + n)


def post_use(b, n):
    return n if isinstance(b, int) and b == 0 else FIRST_POST + POST_USES * (b - 1) + n


def bank_uses(name, b, kv=None):
    if isinstance(b, int) and (name, b) in HEAD:
        return HEAD.index((name, b)) + 1
    if name == "CT" and kv == 0 and isinstance(b, int) and b == 0:
        return HEAD_USES
    if name in TAIL and isinstance(b, int) and b == B - 1:
        return post_use(B, 0) + 1 + TAIL.index(name) + 1
    off = {0: 1, None: None}.get(kv, 0) if name == "CT" else next(o for v in PLAN.values() for p, o in v if p == name)
    body = b - off
    order, _ = plan(not isinstance(body, int) or body > 0, not isinstance(body, int) or body < B - 1)
    n = next(n for (slot, u), v in order.items() for p, o, n in v if p == name and (kv is None or CT_OF[slot] == kv))
    return (pre_use if name in PRE_PIECES else post_use)(body, n) + 1


def prior(u, ring):
    if u >= ring:
        return 0, u - ring
    return 1, max(v for v in range(UNITS) if v % ring == u)


def carve(region):
    at = 0

    def tile(shape):
        nonlocal at
        n = int(np.prod(shape[1:]))
        view = region[0:shape[0], at:at + n]
        at += n
        assert at <= region.shape[1], (at, region.shape)
        if len(shape) == 3:
            view = view.rearrange("p (a b) -> p a b", a=shape[1])
        elif len(shape) == 4:
            view = view.rearrange("p (a b c) -> p a b c", a=shape[1], b=shape[2])
        return view
    return tile


def build(nc, ins, out):
    ctx = ExitStack()
    with ctx:
        def sb(name, shape, dt=F32):
            return ctx.enter_context(nc.sbuf_tensor(name, shape, dt))

        def sem(name):
            return ctx.enter_context(nc.semaphore(name))

        x_d = ins["x"].rearrange("b (j p) f -> b p j f", p=P)
        out_rows = out.rearrange("b t f -> (b t) f")
        rows_d = nc.dram_tensor("expert_rows", [NE * CAP + P, ROW], F32, kind="Internal").ap()
        q_d = [nc.dram_tensor(f"q_parts{i}", [3, QC, T], BF16, kind="Internal").ap() for i in range(2)]
        k_d = [nc.dram_tensor(f"k_parts{i}", [KC, 3, T], BF16, kind="Internal").ap() for i in range(2)]
        c_d = [nc.dram_tensor(f"shift_parts{i}", [2, GRP, T], BF16, kind="Internal").ap() for i in range(2)]

        xres = sb("xres", [P, B + 1, TILES, P])
        zt = sb("zt", [P, B + 1, T])
        gate_up = sb("gate_up", [P, NE, 2 * FE])
        down = zt[:, 0:B].rearrange("p b t -> p (b t)").rearrange("p (e c f) -> p e c f", e=NE, c=FE // P)
        stage = sb("stage", [P, W_RING * T])
        splat_tile, mixer_tile, expert_tile = carve(stage), carve(stage), carve(stage)
        turned = sb("turned", [P, 2800])
        setup_tile, output_tile = carve(turned), carve(turned)
        two = range(2)
        ident, identb = sb("ident", [P, P]), sb("identb", [P, P], BF16)
        causal = sb("causal", [P, P], BF16)
        before = sb("before", [P, P], BF16)
        onesb, ones = sb("onesb", [P, P], BF16), sb("ones", [P, P])
        half = sb("half", [P, TILES])
        seen = sb("seen", [P, P])
        idle, idle_pool = sb("idle", [P, 2]), sb("idle_pool", [P, 3])
        w_in = {n: setup_tile(s) for n, s in {
            "p": [NSPLAT, P], "wv": [P, P], "wo": [P, P], "wffn": [P, P], "wqa": [P, 64], "wqb": [64, P],
            "wkva": [P, 32], "wkvb": [32, 2 * KC], "router": [NE, P],
            "wg": [P, 2, P], "wu": [P, 2, P], "wd": [P, FE]}.items()} | {
            "wout": sb("w_wout", [P, P]), "bout": sb("w_bout", [1, P])}
        logs, amp = sb("logs", [NSPLAT, 1]), sb("amp", [NSPLAT, 1])
        gamma_c, beta_c = sb("gamma_c", [P, 1]), sb("beta_c", [P, 1])
        rope_c, rope_s = sb("rope_c", [P, TILES, RC]), sb("rope_s", [P, TILES, RC])
        small = sb("small", [P, 16])
        splat_t = sb("splat_t", [P, NSPLAT])
        scaled_p = setup_tile([NSPLAT, P])
        squares = setup_tile([NSPLAT, P])
        diag_a, diag_p = sb("diag_a", [NSPLAT, NSPLAT]), sb("diag_p", [NSPLAT, NSPLAT])
        a_rows = sb("a_rows", [P, NSPLAT])
        wvt, wvo = setup_tile([P, P]), sb("wvo", [P, P])
        wqat, wkvat = setup_tile([64, P]), setup_tile([32, P])
        wqkv = sb("wqkv", [P, RC + KC])
        router_t = sb("router_t", [P, NE])
        gate_t, up_t = sb("gate_t", [P, FE]), sb("up_t", [P, FE])
        down_t = sb("down_t", [P, 2, P])
        wq_pos, wq_neg, wq = setup_tile([P, P]), setup_tile([P, P]), sb("wq", [P, P])
        bout_rows = sb("bout_rows", [P, P])
        e_base = sb("e_base", [P, NE])
        e_start = sb("e_start", [P, NE])
        priority = sb("priority", [P, NE])
        token_no = sb("token_no", [P, B, TILES], I32)

        lanes = range(LANES)
        a_st = [sb(f"a_st{i}", [P, TILES, 6]) for i in lanes]
        a_mv = [sb(f"a_mv{i}", [P, TILES, 2]) for i in lanes]
        a_rs = [sb(f"a_rs{i}", [P, 4, TILES]) for i in lanes]
        a_den = [sb(f"a_den{i}", [P, 2, TILES]) for i in lanes]
        zmax = sb("zmax", [P, B])
        zlim = sb("zlim", [P, 4])

        zc = sb("zc", [P, T])
        st2, mv2, rs2 = sb("st2", [P, TILES, 6]), sb("mv2", [P, TILES, 2]), sb("rs2", [P, 2, TILES])
        xn2, xt2 = sb("xn2", [P, TILES, P]), sb("xt2", [P, T])
        rot_c, rot_s = sb("rot_c", [P, 2, RC]), sb("rot_s", [P, 2, RC])
        rot, rest = sb("rot", [P, 2, RC]), sb("rest", [P, 2, RC])
        parts = sb("parts", [P, TILES, RC, 3], BF16)
        qt = sb("qt", [P, 3, T], BF16)
        kt = sb("kt", [3 * KC, T], BF16)
        q8 = [sb(f"q8_{i}", [P, H, T], BF16) for i in two]
        k8 = [sb(f"k8_{i}", [P, KVH, T], BF16) for i in two]
        vv = [sb(f"vv{i}", [P, TILES, KVH, 32]) for i in two]
        v_next = sb("v_next", [P, TILES, KC])
        late_tile = carve(q8[1][:].rearrange("p h t -> p (h t)").bitcast(F32))
        lane_tile = [splat_tile, splat_tile, late_tile, late_tile]
        a_xn = [lane_tile[i]([P, TILES, P]) for i in lanes]
        a_xt = [lane_tile[i]([P, T]) for i in lanes]
        a_et = [a_xt[i][0:NSPLAT] for i in lanes]
        a_d2 = [lane_tile[i]([P, TILES, NSPLAT]) for i in lanes]
        a_e = [lane_tile[i]([P, TILES, NSPLAT]) for i in lanes]
        a_gt = [lane_tile[i]([P, NSPLAT]) for i in lanes]
        a_m = [lane_tile[i]([NSPLAT, P + 1]) for i in lanes]
        negmax = [sb(f"negmax{i}", [P, TILES, GRP]) for i in two]
        shift = [sb(f"shift{i}", [P, TILES, 2, GRP], BF16) for i in two]
        shift_t = [sb(f"shift_t{i}", [2 * GRP, T], BF16) for i in two]
        w_ring = [mixer_tile([P, T]) for i in range(W_RING)]
        av_sb = [output_tile([P, T]) for i in two]
        rden = sb("rden", [P, TILES, GRP])
        o_tok = [output_tile([P, TILES, P]) for i in two]
        o_t = output_tile([P, T])
        st3, mv3, rs3 = sb("st3", [P, TILES, 6]), sb("mv3", [P, TILES, 2]), sb("rs3", [P, 2, TILES])
        xn3, xt3 = sb("xn3", [P, TILES, P]), sb("xt3", [P, T])
        lmax, score = sb("lmax", [P, TILES]), sb("score", [P, 2, TILES])
        top, pri, onehot_f = sb("top", [P, TILES, NE]), sb("pri", [P, TILES]), sb("onehot_f", [P, TILES, NE])
        onehot = sb("onehot", [P, TILES, NE], BF16)
        place, place_s = sb("place", [P, TILES, NE]), sb("place_s", [P, TILES])
        place_i = [sb(f"place_i{i}", [P, TILES], U32) for i in two]
        th, sg = sb("th", [P, T]), sb("sg", [P, T])
        hid = sb("hid", [P, 2, T])
        rows = [sb(f"rows{i}", [P, TILES, ROW]) for i in two]

        pad_rows = sb("pad_rows", [P, ROW])
        cnt, cnt_i, ntile_i = sb("cnt", [P, NE]), sb("cnt_i", [P, NE], I32), sb("ntile_i", [P, NE], I32)
        ntile, ends = sb("ntile", [P, NE]), sb("ends", [P, NE])
        slot_no = sb("slot_no", [P, 1])
        ended, s_tmp = sb("ended", [P, NE]), sb("s_tmp", [P, NE])
        s_val = sb("s_val", [P, 6])
        s_tab, s_row = sb("s_tab", [P, 2]), sb("s_row", [2, P], I32)
        base_i = sb("base_i", [1, NE], I32)
        slot = [expert_tile([P, ROW]) for i in range(OUT_R)]
        d_xt = [expert_tile([P, P]) for i in two]
        d_th = [expert_tile([P, FE]) for i in two]
        d_h = [expert_tile([P, FE]) for i in two]
        d_ht = [expert_tile([P, FE]) for i in two]
        d_out = [expert_tile([P, P]) for i in range(OUT_R)]

        bank = [ctx.enter_context(nc.psum_tensor(f"bank{i}", [P, T], F32)) for i in range(8)]
        MAXB, SCB, AVB, PREB, POSTB = bank[0:2], bank[2:5], bank[5], bank[6], bank[7]

        names = """w_p w_small w_ffn w_attn w_moe w_rope w_experts
            const_pool const_dve ident_ready s_dve s_act s_pe1 s_copy1 s_pe2 s_copy2 beta_part beta_sum wq_ready
            x_loaded0 x_loaded1 x_loaded2 x_loaded3
            a_stats a_rstd a_xn a_xt_ps a_xt a_d2_ps a_sq a_d2 a_e a_gt_ps a_et_ps a_gt a_et a_m_ps a_m a_o_ps a_den a_x1
            a_stats2 a_rstd2 a_zn a_zt_ps a_zt a_zmax zlim_part zlim_all zlim
            pre_full pre_free post_full post_free
            zclip x2 arg2 arg3 a_arg a_arg2 q8_clear xbias rstd2 xn2_ready rope_mul v_ready rope_add part_hi rest_lo part_mid part_lo
            parts_stored0 parts_stored1 parts_loaded0 parts_loaded1
            max_ps max_done shift_split shift_stored0 shift_stored1 shift_loaded0 shift_loaded1
            score_ps exp_done masked av_ps av_copied o_rden stats3 rstd3 xn3_ready
            route score_tanh expert_in tanh_g place_ready numbered
            rows_sent0 rows_sent1 pads_sent pad_ready table table_ps table_ready
            slot_in0 slot_in1 slot_in2 slot_in3 slot_in4 slot_in5 slot_in6 slot_in7 d_xt_ps d_xt_ready d_gu_ps d_tanh d_sg d_hid d_ht_ps d_ht_ready d_dn_ps
            d_out_ready scatter_turn out_sent0 out_sent1 out_sent2 out_sent3 out_sent4 out_sent5 out_sent6 out_sent7""".split()
        s = {n: sem(n) for n in names}

        block = ctx.enter_context(nc.Block())

        @block.sync
        def _(sp):
            load = lambda dst, src, sm: sp.dma_start(dst, src).then_inc(s[sm], 16)
            for q in lanes:
                load(xres[:, q], x_d[q], f"x_loaded{q}")
            load(w_in["p"][:], ins["p"], "w_p")
            with nc.allow_non_contiguous_dma(reason="columns of one value for each partition"):
                load(logs[:], ins["logs"].rearrange("(p a) -> p a", a=1), "w_small")
                load(amp[:], ins["amp"].rearrange("(p a) -> p a", a=1), "w_small")
                load(gamma_c[:], ins["gamma"].rearrange("(p a) -> p a", a=1), "w_small")
                load(beta_c[:], ins["beta"].rearrange("(p a) -> p a", a=1), "w_small")
            for n in ("wv", "wo"):
                load(w_in[n][:], ins[n], "w_attn")
            load(w_in["wffn"][:], ins["wffn"], "w_ffn")
            for n in ("wqa", "wqb", "wkva", "wkvb", "wout"):
                load(w_in[n][:], ins[n], "w_attn")
            load(w_in["bout"][:], ins["bout"].rearrange("(a f) -> a f", a=1), "w_attn")
            load(w_in["router"][:], ins["router"], "w_moe")
            load(w_in["wg"][:], ins["wg"].rearrange("(c p) f -> p c f", p=P), "w_moe")
            load(w_in["wu"][:], ins["wu"].rearrange("(c p) f -> p c f", p=P), "w_moe")
            load(w_in["wd"][:], ins["wd"], "w_moe")
            for q in lanes:
                sp.wait_ge(s[f"x_loaded{q}"], 16)
                load(xres[:, LANES + q], x_d[LANES + q], f"x_loaded{q}")
            load(rope_c[:], ins["rope_c"], "w_rope")
            load(rope_s[:], ins["rope_s"], "w_rope")
            sp.wait_ge(s["pad_ready"], 1)
            sp.dma_start(rows_d[NE * CAP:NE * CAP + P, :], pad_rows[:]).then_inc(s["pads_sent"], 16)
            load(gate_up[:], ins["gate_up"].rearrange("e p f -> p e f"), "w_experts")

            sp.wait_ge(s["const_dve"], 12)

            def parts_round_trip(b, par, past):
                sp.wait_ge(s["pre_free"], bank_uses("SPLITB", b))
                st, ld = s[f"parts_stored{par}"], s[f"parts_loaded{par}"]
                sp.wait_ge(ld, 12 * 16 * past)
                sp.dma_start(q_d[par].rearrange("c p t -> p c t"), qt[:]).then_inc(st, 16)
                sp.dma_start(k_d[par].rearrange("c p t -> (c p) t"), kt[:]).then_inc(st, 16)
                if not isinstance(b, int) or b >= 2:
                    sp.wait_ge(s["score_ps"], KVH * UNITS * (b - 1))
                if isinstance(b, int) and b == 1:
                    sp.wait_ge(s["q8_clear"], 1)
                sp.wait_ge(st, 32 * past + 32)
                for g, (qp, kp) in enumerate(((0, 0), (1, 0), (2, 0), (0, 1), (1, 1), (0, 2))):
                    r = slice(HD * g, HD * g + HD)
                    sp.dma_start(q8[par][r], q_d[par][qp].rearrange("(h d) t -> d h t", d=HD)).then_inc(ld, 16)
                    sp.dma_start(k8[par][r], k_d[par][:, kp].rearrange("(h d) t -> d h t", d=HD)).then_inc(ld, 16)

            def shift_round_trip(b, par, kv, groups):
                g = kv % 2
                sp.wait_ge(s["pre_free"], bank_uses("CT", b, kv))
                st, ld = s[f"shift_stored{g}"], s[f"shift_loaded{g}"]
                sp.wait_ge(ld, 16 * groups)
                sp.dma_start(c_d[g].rearrange("c h t -> (c h) t"), shift_t[g][:]).then_inc(st, 16)
                sp.wait_ge(st, 16 * groups + 16)
                if kv == 0 and not (isinstance(b, int) and b < 2):
                    sp.wait_ge(s["score_ps"], KVH * UNITS * (b - 1))
                sp.dma_start(q8[par][64:66, GRP * kv:GRP * kv + GRP, :], c_d[g]).then_inc(ld, 16)

            parts_round_trip(0, 0, 0)
            shift_round_trip(0, 0, 0, 0)

            def body(b, par, past, nxt=True):
                shift_round_trip(b, par, 1, 2 * b)
                if nxt:
                    parts_round_trip(b + 1, 1 - par, past + par)
                shift_round_trip(b, par, 2, 2 * b + 1)
                shift_round_trip(b, par, 3, 2 * b + 1)
                if nxt:
                    shift_round_trip(b + 1, 1 - par, 0, 2 * b + 2)

            body(0, 0, 0)
            with sp.Fori(0, B // 2 - 1) as i:
                body(i * 2 + 1, 1, i)
                body(i * 2 + 2, 0, i + 1)
            body(B - 1, 1, B // 2 - 1, nxt=False)

            sp.wait_ge(s["x2"], 8 * B)
            sp.dma_start(down[:], ins["down"].rearrange("e (c p) f -> p e c f", p=P)).then_inc(s["w_experts"], 16)

            sp.wait_ge(s["table"], 1)
            for e in range(NE):
                end = sp.value_load(base_i[0:1, e:e + 1], min_val=0, max_val=NE * CAP)
                sp.dma_start(rows_d[bass.ds(end, P), :], pad_rows[:]).then_inc(s["pads_sent"], 16)
            for i in two:
                sp.wait_ge(s[f"rows_sent{i}"], 16 * TILES * B // 2)
            sp.wait_ge(s["pads_sent"], 16 * (NE + 1))
            sp.wait_ge(s["table_ready"], 1)

            def load_slot(n, r, past, waits=True):
                at = sp.value_load(s_row[0:1, bass.ds(n, 1)], min_val=0, max_val=NE * CAP)
                if waits:
                    sp.wait_ge(s[f"out_sent{r}"], 16 * past)
                sp.dma_start(slot[r][:], rows_d[bass.ds(at, P), :]).then_inc(s[f"slot_in{r}"], 16)

            for n in range(OUT_R):
                load_slot(n, n, 0, waits=False)
            with sp.Fori(1, FULL) as i:
                for r in range(OUT_R):
                    load_slot(i * OUT_R + r, r, i)
            for n in range(FULL * OUT_R, SLOTS):
                load_slot(n, n % OUT_R, n // OUT_R)
            for r in range(OUT_R):
                sp.wait_ge(s[f"out_sent{r}"], 16 * len(range(r, SLOTS, OUT_R)))

        @block.gpsimd
        def _(pool):
            g = nc.gpsimd
            g.memset(ident[:], 0.0).then_inc(s["const_pool"], 1)
            g.memset(identb[:], 0.0).then_inc(s["const_pool"], 1)
            g.memset(causal[:], 0.0).then_inc(s["const_pool"], 1)
            g.memset(before[:], 0.0).then_inc(s["const_pool"], 1)
            g.memset(half[:], -0.5).then_inc(s["const_pool"], 1)
            g.memset(seen[:], 1.0).then_inc(s["const_pool"], 1)
            g.memset(idle_pool[:], 0.0).then_inc(s["const_pool"], 1)
            pool.wait_ge(s["const_pool"], 7)
            for m, op, fill, cm, step in ((ident, ALU.not_equal, 1.0, 1, -1), (identb, ALU.not_equal, 1.0, 1, -1),
                                          (causal, ALU.is_ge, MASKED, 1, -1), (before, ALU.is_ge, 1.0, 1, -1)):
                g.affine_select(out=m[:], in_=m[:], compare_op=op, fill=fill, base=0, pattern=[[step, P]],
                                channel_multiplier=cm).then_inc(s["ident_ready"], 1)
            g.affine_select(out=seen[:], in_=seen[:], compare_op=ALU.is_ge, fill=0.0, base=0, pattern=[[1, P]],
                            channel_multiplier=-1).then_inc(s["ident_ready"], 1)
            g.iota(token_no[:], pattern=[[T, B], [P, TILES]], base=0, channel_multiplier=1).then_inc(s["const_pool"], 1)
            g.iota(s_tmp[:].bitcast(I32), pattern=[[CAP, NE]], base=0, channel_multiplier=0).then_inc(s["const_pool"], 1)
            g.iota(ended[:].bitcast(I32), pattern=[[-1, NE]], base=NE, channel_multiplier=0).then_inc(s["const_pool"], 1)
            g.iota(s_val[:, 0:1].bitcast(I32), pattern=[[0, 1]], base=0, channel_multiplier=1).then_inc(s["const_pool"], 1)
            g.memset(pad_rows[:], 0.0).then_inc(s["const_pool"], 1)
            g.iota(s_val[:, 1:2].bitcast(I32), pattern=[[0, 1]], base=NOBODY, channel_multiplier=0).then_inc(s["const_pool"], 1)
            pool.wait_ge(s["beta_part"], 1)
            g.partition_all_reduce(small[:, 9:10], small[:, 8:9], P, REDUCE_ADD).then_inc(s["beta_sum"], 1)

            clear = lambda tile: g.memset(tile[:].bitcast(F32) if tile.dtype != F32 else tile[:], 0.0)
            for tile in (k8[0], k8[1], q8[0]):
                clear(tile).then_inc(s["const_pool"], 1)

            def root(dst, src, sm):
                g.tensor_tensor(dst, src, half[:], ALU.pow).then_inc(s[sm], 1)

            with pool.Fori(0, ROUNDS) as i:
                for q in lanes:
                    b = i * LANES + q
                    pool.wait_ge(s["a_arg"], b + 1)
                    root(a_rs[q][:, 1], a_rs[q][:, 0], "a_rstd")
                for q in lanes:
                    b = i * LANES + q
                    rs = a_rs[q]
                    pool.wait_ge(s["a_rstd"], b + 1)
                    g.tensor_tensor(rs[:, 2], rs[:, 1], rs[:, 1], ALU.mult).then_inc(s["a_sq"], 1)
                    pool.wait_ge(s["a_sq"], 2 * b + 1)
                    g.tensor_tensor(rs[:, 3], rs[:, 2], a_mv[q][:, :, 1], ALU.mult).then_inc(s["a_sq"], 1)
                for q in lanes:
                    b = i * LANES + q
                    pool.wait_ge(s["a_arg2"], b + 1)
                    root(a_rs[q][:, 1], a_rs[q][:, 0], "a_rstd2")
            pool.wait_ge(s["a_zt"], B)
            clear(q8[1]).then_inc(s["q8_clear"], 1)
            pool.wait_ge(s["zlim_part"], 1)
            g.partition_all_reduce(zlim[:, 1:2], zlim[:, 0:1], P, REDUCE_MAX).then_inc(s["zlim_all"], 1)

            def root2(b):
                pool.wait_ge(s["arg2"], b + 1)
                root(rs2[:, 1], rs2[:, 0], "rstd2")

            def xbias(b):
                pool.wait_ge(s["xn2_ready"], 4 * b + 4)
                xb = xres[:, b] if isinstance(b, int) else xres[:, bass.ds(b, 1)].rearrange("p a j f -> p (a j) f")
                g.tensor_tensor(xb, xb, bout_rows[:].unsqueeze(1).to_broadcast([P, TILES, P]), ALU.add)\
                 .then_inc(s["xbias"], 1)

            def add(b, hf):
                if not isinstance(b, int) or 2 * b + hf:
                    pool.wait_ge(s["rest_lo"], 2 * b + hf)
                pool.wait_ge(s["rope_mul"], 6 * b + 3 * hf + 3)
                g.tensor_tensor(rot[:], rot_c[:], rot_s[:], ALU.add).then_inc(s["rope_add"], 1)

            def part_rest(b, hf):
                if not isinstance(b, int) or 2 * b + hf:
                    pool.wait_ge(s["part_lo"], 2 * b + hf)
                pool.wait_ge(s["part_hi"], 2 * b + hf + 1)
                g.tensor_tensor(rest[:], rot[:], parts[:, 2 * hf:2 * hf + 2, :, 0], ALU.subtract).then_inc(s["rest_lo"], 1)

            def part_low(b, hf):
                pool.wait_ge(s["part_mid"], 2 * b + hf + 1)
                g.tensor_tensor(parts[:, 2 * hf:2 * hf + 2, :, 2], rest[:], parts[:, 2 * hf:2 * hf + 2, :, 1], ALU.subtract)\
                 .then_inc(s["part_lo"], 1)

            def outp(b, par):
                pool.wait_ge(s["arg3"], b + 1)
                root(rs3[:, 1], rs3[:, 0], "rstd3")

            def down_scatter(b, par, j):
                if j == 0:
                    pool.wait_ge(s["post_free"], bank_uses("DOWN", b))
                    pool.wait_ge(s["expert_in"], 4 * b + 4)
                    pool.wait_ge(s["numbered"], b + 1)
                    pool.wait_ge(s["place_ready"], 5 * b + 5)
                    g.tensor_tensor(idle_pool[:, 0:1], idle_pool[:, 1:2], idle_pool[:, 1:2], ALU.add)
                g.indirect_dma_start(rows_d, bass.IndirectOffsetOnAxis(place_i[par][:, j:j + 1], 0), rows[par][:, j, :],
                                     None, bounds_check=NE * CAP - 1, oob_is_err=False)\
                 .then_inc(s[f"rows_sent{par}"], 16)

            def select(b, kv, u):
                ktile, h0, nh = SCORE_UNITS[u]
                pool.wait_ge(s["exp_done"], KVH * UNITS * b + UNITS * kv + u + 1)
                n = T - P * ktile
                blk = w_ring[u % W_RING][:, 0:nh * n].rearrange("p (h n) -> p h n", h=nh)[:, :, 0:P]
                g.tensor_tensor(blk, blk, seen[:].unsqueeze(1).to_broadcast([P, nh, P]), ALU.mult).then_inc(s["masked"], 1)

            for b in two:
                root2(b)
                xbias(b)
                for hf in two:
                    add(b, hf)
                    part_rest(b, hf)
                    part_low(b, hf)

            def body(b, par, prev=True, nxt=True):
                steps = steps_of(plan(prev, nxt)[0], POOL_STEPS)
                for kv in range(KVH):
                    for u in range(UNITS):
                        for step, name, off, _ in steps.get((kv, u), ()):
                            if step == "ROOT3":
                                outp(b - 1, 1 - par)
                            elif step == "ROOT2":
                                root2(b + 2)
                            elif step == "XBIAS":
                                xbias(b + 2)
                            elif step.startswith("SCATTER"):
                                down_scatter(b - 1, 1 - par, int(step[7]))
                            else:
                                {"ADD": add, "REST": part_rest, "LOW": part_low}[step](b + 2, int(name[3]))
                        select(b, kv, u)

            body(0, 0, prev=False)
            with pool.Fori(0, B // 2 - 1) as i:
                body(i * 2 + 1, 1)
                body(i * 2 + 2, 0)
            body(B - 1, 1, nxt=False)
            outp(B - 1, 1)
            for j in range(TILES):
                down_scatter(B - 1, 1, j)

            def scatter(n, r, past):
                pool.wait_ge(s["d_out_ready"], n + 1)
                pool.wait_ge(s["scatter_turn"], n)
                g.tensor_tensor(idle_pool[:, 2:3], idle_pool[:, 1:2], idle_pool[:, 1:2], ALU.add).then_inc(s["scatter_turn"], 1)
                g.indirect_dma_start(out_rows, bass.IndirectOffsetOnAxis(slot[r][:, 2 * P:ROW].bitcast(U32), 0), d_out[r][:],
                                     None, bounds_check=B * T - 1, oob_is_err=False).then_inc(s[f"out_sent{r}"], 16)

            with pool.Fori(0, FULL) as i:
                for r in range(OUT_R):
                    scatter(i * OUT_R + r, r, i)
            for n in range(FULL * OUT_R, SLOTS):
                scatter(n, n % OUT_R, n // OUT_R)

        @block.scalar
        def _(act):
            a = nc.scalar
            act.wait_ge(s["w_small"], 64)
            act.wait_ge(s["const_dve"], 6)
            a.activation(small[0:NSPLAT, 0:1], logs[:], ACT.Exp, scale=-2.0).then_inc(s["s_act"], 1)
            act.wait_ge(s["s_pe1"], 11)
            for dst, src in ((wvt[:], bank[0][:, 0:128]), (splat_t[:], bank[0][:, 128:192]),
                             (wqat[:], bank[0][0:64, 192:320]), (wkvat[:], bank[0][0:32, 320:448]),
                             (router_t[:], bank[0][:, 448:464]), (gate_t[:], bank[1][:, 0:256]),
                             (up_t[:], bank[1][:, 256:512]), (down_t[:], bank[2][:, 0:256].rearrange("p (c f) -> p c f", c=2))):
                a.copy(dst, src).then_inc(s["s_copy1"], 1)
            act.wait_ge(s["s_pe2"], 6)
            for dst, src in ((wvo[:], bank[3][:, 0:128]), (wqkv[:], bank[3][:, 128:320]), (a_rows[:], bank[3][:, 320:384]),
                             (bout_rows[:], bank[3][:, 384:512])):
                a.copy(dst, src).then_inc(s["s_copy2"], 1)

            with act.Fori(0, ROUNDS) as i:
                for q in lanes:
                    b = i * LANES + q
                    act.wait_ge(s["a_xt_ps"], b + 1)
                    a.copy(a_xt[q][:], bank[2 * q][:]).then_inc(s["a_xt"], 1)
                for q in lanes:
                    b = i * LANES + q
                    act.wait_ge(s["a_d2"], 5 * b + 5)
                    a.activation(a_e[q][:], a_d2[q][:], ACT.Exp).then_inc(s["a_e"], 1)
                for q in lanes:
                    b = i * LANES + q
                    act.wait_ge(s["a_gt_ps"], b + 1)
                    a.copy(a_gt[q][:], bank[2 * q + 1][:, 0:NSPLAT]).then_inc(s["a_gt"], 1)
                for q in lanes:
                    b = i * LANES + q
                    act.wait_ge(s["a_et_ps"], b + 1)
                    a.copy(a_et[q], bank[2 * q][0:NSPLAT, :]).then_inc(s["a_et"], 1)
                for q in lanes:
                    b = i * LANES + q
                    act.wait_ge(s["a_zt_ps"], b + 1)
                    a.activation(zt[:, bass.ds(b, 1)].rearrange("p a t -> p (a t)"), bank[2 * q][:], ACT.Identity,
                                 bias=beta_c[:, 0:1], scale=gamma_c[:, 0:1]).then_inc(s["a_zt"], 1)

            def t2(b, n):
                act.wait_ge(s["pre_full"], n + 1)
                a.copy(xt2[:], PREB[:]).then_inc(s["pre_free"], 1)

            def high(b, hf):
                act.wait_ge(s["rope_add"], 2 * b + hf + 1)
                if hf == 0 and (not isinstance(b, int) or b > 0):
                    act.wait_ge(s["pre_full"], bank_uses("SPLITB", b - 1))
                a.copy(parts[:, 2 * hf:2 * hf + 2, :, 0], rot[:]).then_inc(s["part_hi"], 1)

            def mid(b, hf):
                act.wait_ge(s["rest_lo"], 2 * b + hf + 1)
                a.copy(parts[:, 2 * hf:2 * hf + 2, :, 1], rest[:]).then_inc(s["part_mid"], 1)

            def split_a(b, n, par, past):
                act.wait_ge(s["pre_full"], n + 1)
                if not isinstance(b, int) or b > 0:
                    act.wait_ge(s[f"parts_stored{1 - par}"], 32 * (past + par))
                a.copy(qt[:, 0:2], PREB[:].bitcast(BF16).rearrange("p (c t) -> p c t", c=2)).then_inc(s["pre_free"], 1)

            def split_b(b, n):
                act.wait_ge(s["pre_full"], n + 1)
                both = PREB[:].bitcast(BF16)
                a.copy(qt[:, 2], both[:, 0:T])
                a.copy(kt[:], both[0:3 * KC, T:2 * T]).then_inc(s["pre_free"], 1)

            def ct(gb, kv, n, groups):
                act.wait_ge(s["pre_full"], n + 1)
                act.wait_ge(s[f"shift_stored{kv % 2}"], 16 * groups)
                a.copy(shift_t[kv % 2][:], PREB[:].bitcast(BF16)[0:2 * GRP, 0:T]).then_inc(s["pre_free"], 1)

            def ot(b, n):
                act.wait_ge(s["post_full"], n + 1)
                a.copy(o_t[:], POSTB[:]).then_inc(s["post_free"], 1)

            def t3(b, n):
                act.wait_ge(s["post_full"], n + 1)
                a.copy(xt3[:], POSTB[:]).then_inc(s["post_free"], 1)

            def router(b):
                act.wait_ge(s["route"], 5 * b + 1)
                a.activation(score[:, 0], lmax[:], ACT.Tanh, scale=0.5).then_inc(s["score_tanh"], 1)

            def gate(b, n, hf):
                act.wait_ge(s["post_full"], n + 1)
                a.activation(th[:], POSTB[:], ACT.Tanh, scale=0.5).then_inc(s["tanh_g"], 1)

            def av_copy(b, kv):
                g = KVH * b + kv
                act.wait_ge(s["av_ps"], 4 * g + 4)
                a.copy(av_sb[kv % 2][:], AVB[:]).then_inc(s["av_copied"], 1)

            def exp(b, kv, u):
                ktile, h0, nh = SCORE_UNITS[u]
                g = KVH * b + kv
                act.wait_ge(s["score_ps"], UNITS * g + u + 1)
                back, v = prior(u, W_RING)
                if not (isinstance(b, int) and b == 0 and kv == 0) or back == 0:
                    done = next(k for k, last in enumerate(LAST_OF_TILE) if v <= last) + 1
                    act.wait_ge(s["av_ps"], 4 * (g - back) + done)
                cols = nh * (T - P * ktile)
                a.activation(w_ring[u % W_RING][:, 0:cols], SCB[u % SC_BANKS][:, 0:cols], ACT.Exp).then_inc(s["exp_done"], 1)

            for n, (name, b) in enumerate(HEAD):
                if name == "T2":
                    t2(b, n)
                elif name in ("QKV0", "QKV1"):
                    high(b, int(name[3]))
                    mid(b, int(name[3]))
                elif name == "SPLITA":
                    split_a(b, n, b % 2, 0)
                elif name == "SPLITB":
                    split_b(b, n)
            ct(0, 0, HEAD_USES - 1, 0)

            def body(b, par, past, prev=True, nxt=True):
                steps = steps_of(plan(prev, nxt)[0], ACT_STEPS)
                for kv in range(KVH):
                    for u in range(UNITS):
                        for step, name, off, n in steps.get((kv, u), ()):
                            pre, post = pre_use(b, n), post_use(b, n)
                            if step == "T2":
                                t2(b + 2, pre)
                            elif step == "HIGH":
                                high(b + 2, int(name[3]))
                            elif step == "MID":
                                mid(b + 2, int(name[3]))
                            elif step == "SPLITA":
                                split_a(b + 1, pre, 1 - par, past + par)
                            elif step == "SPLITB":
                                split_b(b + 1, pre)
                            elif step == "CT":
                                c = CT_OF[kv]
                                ct(b + off, c, pre, 2 * (b + off) + c // 2)
                            elif step == "OT":
                                ot(b - 1, post)
                            elif step == "T3":
                                t3(b - 1, post)
                            elif step == "ROUTER":
                                router(b - 1)
                            elif step in ("GATE0", "GATE1"):
                                gate(b - 1, post, int(name[4]))
                        exp(b, kv, u)
                        if u == AV_COPY_AT and (prev or kv):
                            av_copy(*((b, kv - 1) if kv else (b - 1, KVH - 1)))

            body(0, 0, 0, prev=False)
            with act.Fori(0, B // 2 - 1) as i:
                body(i * 2 + 1, 1, i)
                body(i * 2 + 2, 0, i + 1)
            body(B - 1, 1, B // 2 - 1, nxt=False)
            av_copy(B - 1, KVH - 1)
            last = post_use(B, 0) + 1
            for n, name in enumerate(TAIL):
                if name == "OT":
                    ot(B - 1, last + n)
                elif name == "T3":
                    t3(B - 1, last + n)
                elif name == "ROUTER":
                    router(B - 1)
                elif name in ("GATE0", "GATE1"):
                    gate(B - 1, last + n, int(name[4]))

            def d_xt_copy(n, r):
                act.wait_ge(s["d_xt_ps"], n + 1)
                a.copy(d_xt[r % 2][:], bank[r % 2][:, 0:P]).then_inc(s["d_xt_ready"], 1)

            def d_tanh(n, r):
                act.wait_ge(s["d_gu_ps"], n + 1)
                if not isinstance(n, int) or n >= 2:
                    act.wait_ge(s["d_hid"], n - 1)
                a.activation(d_th[r % 2][:], bank[2 + r % 2][:, 0:FE], ACT.Tanh, scale=0.5).then_inc(s["d_tanh"], 1)

            def d_slot(n, r, past):
                more = SLOTS - n if isinstance(n, int) else 3
                if more > 1:
                    d_tanh(n + 1, r + 1)
                if more > 2:
                    d_xt_copy(n + 2, r)
                act.wait_ge(s["d_ht_ps"], n + 1)
                a.copy(d_ht[r % 2][:], bank[4 + r % 2][:, 0:FE]).then_inc(s["d_ht_ready"], 1)

            d_xt_copy(0, 0)
            d_xt_copy(1, 1)
            d_tanh(0, 0)
            for n in range(OUT_R):
                d_slot(n, n, 0)
            with act.Fori(1, FULL) as i:
                for r in range(OUT_R):
                    d_slot(i * OUT_R + r, r, i)
            for n in range(FULL * OUT_R, SLOTS):
                d_slot(n, n % OUT_R, n // OUT_R)

        @block.vector
        def _(dve):
            v = nc.vector
            v.memset(ones[:], 1.0).then_inc(s["const_dve"], 1)
            v.memset(onesb[:], 1.0).then_inc(s["const_dve"], 1)
            for i in two:
                v.memset(vv[i][:], 0.0).then_inc(s["const_dve"], 1)
            v.memset(small[:], 0.0).then_inc(s["const_dve"], 1)
            v.memset(idle[:], 0.0).then_inc(s["const_dve"], 1)
            dve.wait_ge(s["const_dve"], 6)

            small_s = lambda c: small[0:NSPLAT, c:c + 1]
            dve.wait_ge(s["s_act"], 1)
            dve.wait_ge(s["w_p"], 16)
            dve.wait_ge(s["w_small"], 64)
            dve.wait_ge(s["ident_ready"], 5)
            v.tensor_tensor(squares[:], w_in["p"][:], w_in["p"][:], ALU.mult).then_inc(s["s_dve"], 1)
            v.tensor_scalar(small_s(1), small_s(0), -0.5, None, ALU.mult).then_inc(s["s_dve"], 1)
            v.tensor_scalar(small_s(2), small_s(0), -0.5 * P, None, ALU.mult).then_inc(s["s_dve"], 1)
            v.tensor_tensor(small_s(4), amp[:], amp[:], ALU.mult).then_inc(s["s_dve"], 1)
            dve.wait_ge(s["s_dve"], 4)
            v.tensor_reduce(small_s(3), squares[:], AX, ALU.add).then_inc(s["s_dve"], 1)
            v.tensor_scalar(scaled_p[:], w_in["p"][:], small_s(1), -2.0, ALU.mult, ALU.mult).then_inc(s["s_dve"], 1)
            v.tensor_scalar(diag_a[:], ident[0:NSPLAT, 0:NSPLAT], small_s(2), None, ALU.mult).then_inc(s["s_dve"], 1)
            dve.wait_ge(s["s_dve"], 7)
            v.tensor_scalar(diag_p[:], ident[0:NSPLAT, 0:NSPLAT], small_s(3), small_s(1), ALU.mult, ALU.mult)\
             .then_inc(s["s_dve"], 1)

            dve.wait_ge(s["w_ffn"], 16)
            v.tensor_reduce(small[:, 8:9], w_in["wffn"][:], AX, ALU.add, apply_absolute_value=True).then_inc(s["beta_part"], 1)
            dve.wait_ge(s["beta_sum"], 1)
            v.tensor_scalar(small[:, 10:11], small[:, 9:10], 1.0 / (P * P), EPS_BETA, ALU.mult, ALU.add).then_inc(s["wq_ready"], 1)
            v.tensor_scalar(small[:, 5:6], small[:, 9:10], 1.0 / (P * P), None, ALU.mult).then_inc(s["wq_ready"], 1)
            dve.wait_ge(s["wq_ready"], 2)
            v.reciprocal(small[:, 7:8], small[:, 10:11]).then_inc(s["wq_ready"], 1)
            dve.wait_ge(s["wq_ready"], 3)
            v.tensor_scalar(wq_pos[:], w_in["wffn"][:], small[:, 7:8], 0.5, ALU.mult, ALU.is_gt).then_inc(s["wq_ready"], 1)
            v.tensor_scalar(wq_neg[:], w_in["wffn"][:], small[:, 7:8], -0.5, ALU.mult, ALU.is_lt).then_inc(s["wq_ready"], 1)
            dve.wait_ge(s["wq_ready"], 5)
            v.tensor_tensor(wq[:], wq_pos[:], wq_neg[:], ALU.subtract).then_inc(s["wq_ready"], 1)
            for i in two:
                v.memset(vv[i][:, :, :, HD:HD + 1], 1.0).then_inc(s["const_dve"], 1)
            v.memset(xres[:, B], 1.0).then_inc(s["const_dve"], 1)
            v.memset(zt[:, B], 0.0).then_inc(s["const_dve"], 1)
            dve.wait_ge(s["const_pool"], 13)
            v.tensor_copy(e_start[:], s_tmp[:].bitcast(I32)).then_inc(s["s_dve"], 1)
            v.tensor_copy(priority[:], ended[:].bitcast(I32)).then_inc(s["s_dve"], 1)
            v.tensor_copy(slot_no[:], s_val[:, 0:1].bitcast(I32)).then_inc(s["s_dve"], 1)
            v.tensor_copy(pad_rows[:, 2 * P:ROW].bitcast(I32), s_val[:, 1:2].bitcast(I32)).then_inc(s["pad_ready"], 1)
            dve.wait_ge(s["const_pool"], 16)
            for i in two:
                v.memset(k8[i][64:66], 1.0).then_inc(s["const_dve"], 1)
            dve.wait_ge(s["s_dve"], 11)
            v.tensor_copy(e_base[:], e_start[:]).then_inc(s["s_dve"], 1)

            def statistics(src, st, mv, sm, at):
                for j in range(TILES):
                    v.bn_stats(st[:, j], src(j)).then_inc(s[sm], 1)
                dve.wait_ge(s[sm], at + TILES)
                v.tensor_copy(idle[:, 0:1], idle[:, 1:2])
                for j in range(TILES):
                    v.bn_aggr(mv[:, j], st[:, j]).then_inc(s[sm], 1)

            def normalise(dst, src, mv, rstd, sm):
                for j in range(TILES):
                    v.tensor_scalar(dst[:, j], src(j), mv[:, j, 0:1], rstd[:, j:j + 1], ALU.subtract, ALU.mult)\
                     .then_inc(s[sm], 1)

            def res(b):
                if isinstance(b, int):
                    return lambda j: xres[:, b, j]
                return lambda j: xres[:, bass.ds(b, 1), j].rearrange("p a f -> p (a f)")

            with dve.Fori(0, ROUNDS) as i:
                for q in lanes:
                    b = i * LANES + q
                    dve.wait_ge(s[f"x_loaded{q}"], i * 16 + 16)
                    statistics(res(b), a_st[q], a_mv[q], "a_stats", 8 * b)
                    dve.wait_ge(s["a_stats"], 8 * b + 8)
                    v.tensor_scalar(a_rs[q][:, 0], a_mv[q][:, :, 1], LN_EPS, None, ALU.add).then_inc(s["a_arg"], 1)
                for q in lanes:
                    b = i * LANES + q
                    dve.wait_ge(s["a_rstd"], b + 1)
                    normalise(a_xn[q], res(b), a_mv[q], a_rs[q][:, 1], "a_xn")
                dve.wait_ge(s["s_copy2"], 4)
                for q in lanes:
                    b = i * LANES + q
                    dve.wait_ge(s["a_sq"], 2 * b + 2)
                    dve.wait_ge(s["a_d2_ps"], b + 1)
                    for j in range(TILES):
                        c = slice(NSPLAT * j, NSPLAT * j + NSPLAT)
                        v.scalar_tensor_tensor(a_d2[q][:, j], a_rows[:], a_rs[q][:, 3, j:j + 1], bank[2 * q + 1][:, c],
                                               ALU.mult, ALU.add).then_inc(s["a_d2"], 1)
                    dve.wait_ge(s["a_d2"], 5 * b + 4)
                    v.tensor_scalar(a_d2[q][:], a_d2[q][:], 0.0, None, ALU.min).then_inc(s["a_d2"], 1)
                for q in lanes:
                    b = i * LANES + q
                    dve.wait_ge(s["a_gt"], b + 1)
                    dve.wait_ge(s["a_m_ps"], b + 1)
                    v.tensor_scalar(a_m[q][:], bank[2 * q + 1][0:NSPLAT, NSPLAT:NSPLAT + P + 1], small_s(4), None, ALU.mult)\
                     .then_inc(s["a_m"], 1)
                for q in lanes:
                    b = i * LANES + q
                    den = a_den[q]
                    for h in two:
                        dve.wait_ge(s["a_o_ps"], 2 * b + h + 1)
                        o = bank[2 * q + h][:, 0:2 * (P + 1)].rearrange("p (j f) -> p j f", j=2)
                        v.tensor_scalar(den[:, 0, 2 * h:2 * h + 2], o[:, :, P], EPS_SPLAT, None, ALU.add).then_inc(s["a_den"], 1)
                        dve.wait_ge(s["a_den"], 4 * b + 2 * h + 1)
                        v.reciprocal(den[:, 1, 2 * h:2 * h + 2], den[:, 0, 2 * h:2 * h + 2]).then_inc(s["a_den"], 1)
                        dve.wait_ge(s["a_den"], 4 * b + 2 * h + 2)
                        for j in two:
                            xb = res(b)(2 * h + j)
                            v.scalar_tensor_tensor(xb, o[:, j, 0:P], den[:, 1, 2 * h + j:2 * h + j + 1], xb, ALU.mult, ALU.add)\
                             .then_inc(s["a_x1"], 1)
                    dve.wait_ge(s["a_x1"], 4 * b + 4)
                    v.tensor_copy(idle[:, 0:1], idle[:, 1:2])
                    statistics(res(b), a_st[q], a_mv[q], "a_stats2", 8 * b)
                    dve.wait_ge(s["a_stats2"], 8 * b + 8)
                    v.tensor_scalar(a_rs[q][:, 0], a_mv[q][:, :, 1], 1.0 + FFN_LN_EPS, LN_EPS * FFN_LN_EPS, ALU.mult, ALU.add)\
                     .then_inc(s["a_arg2"], 1)
                for q in lanes:
                    b = i * LANES + q
                    dve.wait_ge(s["a_rstd2"], b + 1)
                    normalise(a_xn[q], res(b), a_mv[q], a_rs[q][:, 1], "a_zn")
                for q in lanes:
                    b = i * LANES + q
                    dve.wait_ge(s["a_zt"], b + 1)
                    v.tensor_reduce(zmax[:, bass.ds(b, 1)], zt[:, bass.ds(b, 1)].rearrange("p a t -> p (a t)"), AX, ALU.max,
                                    apply_absolute_value=True).then_inc(s["a_zmax"], 1)
            dve.wait_ge(s["a_zmax"], B)
            v.tensor_reduce(zlim[:, 0:1], zmax[:], AX, ALU.max).then_inc(s["zlim_part"], 1)
            dve.wait_ge(s["zlim_all"], 1)
            lim = float(np.float32(QB - EPS_BETA)) / QB
            v.tensor_scalar(zlim[:, 2:3], zlim[:, 1:2], lim, None, ALU.mult).then_inc(s["zlim"], 1)
            v.tensor_scalar(zlim[:, 3:4], zlim[:, 1:2], -lim, None, ALU.mult).then_inc(s["zlim"], 1)
            dve.wait_ge(s["zlim"], 2)

            def clip(b):
                if not isinstance(b, int) or b > 0:
                    dve.wait_ge(s["x2"], 8 * b - 7)
                z = zt[:, b] if isinstance(b, int) else zt[:, bass.ds(b, 1)].rearrange("p a t -> p (a t)")
                v.tensor_scalar(zc[:], z, zlim[:, 2:3], zlim[:, 3:4], ALU.min, ALU.max).then_inc(s["zclip"], 1)

            def y(b, n):
                dve.wait_ge(s["pre_full"], n + 1)
                xb = xres[:, b] if isinstance(b, int) else xres[:, bass.ds(b, 1)].rearrange("p a j f -> p (a j) f")
                v.scalar_tensor_tensor(xb, PREB[:].rearrange("p (j f) -> p j f", j=TILES), small[:, 5:6], xb, ALU.mult, ALU.add)\
                 .then_inc(s["pre_free"], 1)
                dve.wait_ge(s["pre_free"], n + 1)
                v.tensor_copy(idle[:, 0:1], idle[:, 1:2])
                statistics(res(b), st2, mv2, "x2", 8 * b)
                dve.wait_ge(s["x2"], 8 * b + 8)
                v.tensor_scalar(rs2[:, 0], mv2[:, :, 1], LN_EPS, None, ALU.add).then_inc(s["arg2"], 1)

            def norm2(b):
                dve.wait_ge(s["rstd2"], b + 1)
                normalise(xn2, res(b), mv2, rs2[:, 1], "xn2_ready")

            def qkv(b, par, n, hf):
                k = 2 * b + hf
                dve.wait_ge(s["pre_full"], n + 1)
                tiles = slice(2 * hf, 2 * hf + 2)
                o = PREB[:, 0:2 * (RC + KC)].rearrange("p (j f) -> p j f", j=2)
                if not isinstance(k, int) or k > 0:
                    dve.wait_ge(s["rope_add"], k)
                v.tensor_tensor(rot_c[:], o[:, :, 0:RC], rope_c[:, tiles], ALU.mult).then_inc(s["rope_mul"], 1)
                for odd in two:
                    pair = lambda t, w: t.rearrange("p j (n two) -> p j n two", two=2)[:, :, :, w]
                    v.tensor_tensor(pair(rot_s[:], odd), pair(o[:, :, 0:RC], 1 - odd), pair(rope_s[:, tiles], odd), ALU.mult)\
                     .then_inc(s["rope_mul"], 1)
                v.tensor_copy(v_next[:, tiles], o[:, :, RC:RC + KC]).then_inc(s["pre_free"], 1)

            def values(b, par, n):
                dve.wait_ge(s["pre_free"], n)
                if not isinstance(b, int) or b >= 2:
                    dve.wait_ge(s["av_ps"], 4 * KVH * (b - 1))
                v.tensor_copy(vv[par][:, :, :, 0:HD], v_next[:].rearrange("p j (h d) -> p j h d", h=KVH)).then_inc(s["v_ready"], 1)

            def row_max(b, kv, u):
                qtile, h0, nh = MAX_UNITS[u]
                k = UNITS * (KVH * b + kv) + u
                n = P * (qtile + 1)
                dve.wait_ge(s["max_ps"], k + 1)
                v.tensor_reduce(negmax[kv % 2][:, qtile, h0:h0 + nh],
                                MAXB[(kv * UNITS + u) % 2][:, 0:nh * n].rearrange("p (h n) -> p h n", h=nh),
                                AX, ALU.max, negate=True).then_inc(s["max_done"], 1)

            def shift_parts(b, kv):
                g = KVH * b + kv
                dve.wait_ge(s["max_done"], UNITS * (g + 1))
                nm, sh = negmax[kv % 2], shift[kv % 2]
                v.tensor_copy(sh[:, :, 0], nm[:]).then_inc(s["shift_split"], 1)
                dve.wait_ge(s["shift_split"], 2 * g + 1)
                v.tensor_tensor(sh[:, :, 1], nm[:], sh[:, :, 0], ALU.subtract).then_inc(s["shift_split"], 1)

            def avt(b, par, kv, n):
                g = KVH * b + kv
                dve.wait_ge(s["post_full"], n + 1)
                o = POSTB[:].rearrange("p (j h c) -> p j h c", j=TILES, h=GRP)
                v.reciprocal(rden[:], o[:, :, :, HD]).then_inc(s["o_rden"], 1)
                dve.wait_ge(s["o_rden"], g + 1)
                v.tensor_tensor(o_tok[par][:, :, KC * kv:KC * kv + KC].rearrange("p j (h d) -> p j h d", h=GRP),
                                o[:, :, :, 0:HD], rden[:].unsqueeze(3).to_broadcast([P, TILES, GRP, HD]), ALU.mult)\
                 .then_inc(s["post_free"], 1)

            def outp(b, n):
                dve.wait_ge(s["post_full"], n + 1)
                dve.wait_ge(s["xbias"], b + 1)
                xb = xres[:, b] if isinstance(b, int) else xres[:, bass.ds(b, 1)].rearrange("p a j f -> p (a j) f")
                v.tensor_tensor(xb, POSTB[:].rearrange("p (j f) -> p j f", j=TILES), xb, ALU.add).then_inc(s["post_free"], 1)
                dve.wait_ge(s["post_free"], n + 1)
                v.tensor_copy(idle[:, 0:1], idle[:, 1:2])
                statistics(res(b), st3, mv3, "stats3", 8 * b)
                dve.wait_ge(s["stats3"], 8 * b + 8)
                v.tensor_scalar(rs3[:, 0], mv3[:, :, 1], LN_EPS, None, ALU.add).then_inc(s["arg3"], 1)

            def norm3(b):
                dve.wait_ge(s["rstd3"], b + 1)
                normalise(xn3, res(b), mv3, rs3[:, 1], "xn3_ready")

            def router(b, n):
                dve.wait_ge(s["post_full"], n + 1)
                lg = POSTB[:, 0:TILES * NE].rearrange("p (j e) -> p j e", j=TILES)
                wide = lambda t: t.unsqueeze(2).to_broadcast([P, TILES, NE])
                v.tensor_reduce(lmax[:], lg, AX, ALU.max).then_inc(s["route"], 1)
                dve.wait_ge(s["route"], 5 * b + 1)
                v.tensor_tensor(top[:], lg, wide(lmax[:]), ALU.is_ge).then_inc(s["post_free"], 1)
                dve.wait_ge(s["post_free"], n + 1)
                v.tensor_tensor(top[:], top[:], priority[:].unsqueeze(1).to_broadcast([P, TILES, NE]), ALU.mult)\
                 .then_inc(s["route"], 1)
                dve.wait_ge(s["route"], 5 * b + 2)
                v.tensor_reduce(pri[:], top[:], AX, ALU.max).then_inc(s["route"], 1)
                dve.wait_ge(s["route"], 5 * b + 3)
                v.tensor_tensor(onehot[:], top[:], wide(pri[:]), ALU.is_equal).then_inc(s["route"], 1)

            def expert_in(b, par, past):
                dve.wait_ge(s["score_tanh"], b + 1)
                v.tensor_scalar(score[:, 1], score[:, 0], 0.5, 0.5, ALU.mult, ALU.add).then_inc(s["route"], 1)
                dve.wait_ge(s["route"], 5 * b + 5)
                dve.wait_ge(s[f"rows_sent{par}"], 16 * TILES * past)
                for j in range(TILES):
                    v.tensor_scalar(rows[par][:, j, 0:P], xn3[:, j], score[:, 1, j:j + 1], None, ALU.mult)\
                     .then_inc(s["expert_in"], 1)
                num = token_no[:, b] if isinstance(b, int) else token_no[:, bass.ds(b, 1)].rearrange("p a j -> p (a j)")
                v.tensor_copy(rows[par][:, :, 2 * P].bitcast(I32), num).then_inc(s["numbered"], 1)

            def gate(b, n, hf):
                dve.wait_ge(s["tanh_g"], 2 * b + hf + 1)
                v.scalar_tensor_tensor(sg[:], th[:], 1.0, POSTB[:], ALU.add, ALU.mult).then_inc(s["post_free"], 1)

            def up(b, n, hf, tail=False):
                dve.wait_ge(s["post_free"], bank_uses(f"GATE{hf}", b))
                dve.wait_ge(s["post_full" if tail else "pre_full"], n + 1)
                v.tensor_tensor(hid[:, hf], sg[:], (POSTB if tail else PREB)[:], ALU.mult)\
                 .then_inc(s["post_free" if tail else "pre_free"], 1)

            def rank(b, par, past, n):
                dve.wait_ge(s["post_full"], n + 1)
                r = POSTB[:, 0:TILES * NE].rearrange("p (j e) -> p j e", j=TILES)
                v.tensor_tensor(place[:], r, e_base[:].unsqueeze(1).to_broadcast([P, TILES, NE]), ALU.add)\
                 .then_inc(s["place_ready"], 1)
                v.tensor_copy(onehot_f[:], onehot[:]).then_inc(s["place_ready"], 1)
                dve.wait_ge(s["place_ready"], 5 * b + 2)
                v.tensor_tensor(place[:], place[:], onehot_f[:], ALU.mult).then_inc(s["place_ready"], 1)
                v.tensor_tensor(e_base[:], POSTB[:, TILES * NE:(TILES + 1) * NE], e_base[:], ALU.add)\
                 .then_inc(s["post_free"], 1)
                dve.wait_ge(s["place_ready"], 5 * b + 3)
                v.tensor_reduce(place_s[:], place[:], AX, ALU.add).then_inc(s["place_ready"], 1)
                dve.wait_ge(s["place_ready"], 5 * b + 4)
                v.tensor_copy(place_i[par][:], place_s[:]).then_inc(s["place_ready"], 1)

            def carry(b, par, n):
                dve.wait_ge(s["post_full"], n + 1)
                xb = xres[:, b] if isinstance(b, int) else xres[:, bass.ds(b, 1)].rearrange("p a j f -> p (a j) f")
                v.scalar_tensor_tensor(rows[par][:, :, P:2 * P], POSTB[:].rearrange("p (j f) -> p j f", j=TILES), 0.5, xb,
                                       ALU.mult, ALU.add).then_inc(s["post_free"], 1)

            for n, (name, b) in enumerate(HEAD):
                if name == "Y":
                    clip(b)
                    y(b, n)
                    norm2(b)
                elif name in ("QKV0", "QKV1"):
                    qkv(b, b % 2, n, int(name[3]))
                    if (name, b) == ("QKV1", 0):
                        values(0, 0, n + 1)
            for kv in range(2):
                for u in range(UNITS):
                    row_max(0, kv, u)
                if kv == 0:
                    shift_parts(0, 0)

            def body(b, par, past, prev=True, nxt=True):
                steps = steps_of(plan(prev, nxt)[0], DVE_STEPS)
                before_prev = past + par - 1 if not isinstance(past, int) or prev else 0
                for kv in range(KVH):
                    for u in range(UNITS):
                        m = (b, kv + 2) if kv < 2 else (b + 1, kv - 2)
                        if kv < 2 or nxt:
                            row_max(*m, u)
                        if u == 0 and (kv < 3 or nxt):
                            shift_parts(*((b, kv + 1) if kv < 3 else (b + 1, 0)))
                        for name, _, off, n in steps.get((kv, u), ()):
                            pre, post = pre_use(b, n), post_use(b, n)
                            if name == "Y":
                                y(b + 2, pre)
                            elif name in ("QKV0", "QKV1"):
                                qkv(b + 2, par, pre, int(name[3]))
                            elif name == "AVT":
                                avt(*((b, par, kv - 1) if off == 0 else (b - 1, 1 - par, KVH - 1)), post)
                            elif name == "OUTP":
                                outp(b - 1, post)
                            elif name == "ROUTER":
                                router(b - 1, post)
                            elif name == "EXPERT_IN":
                                expert_in(b - 1, 1 - par, before_prev)
                            elif name in ("GATE0", "GATE1"):
                                gate(b - 1, post, int(name[4]))
                            elif name in ("UP0", "UP1"):
                                up(b - 1, pre, int(name[2]))
                            elif name == "RANK":
                                rank(b - 1, 1 - par, before_prev, post)
                            elif name == "DOWN":
                                carry(b - 1, 1 - par, post)
                        if (kv, u) == NORM3_AT and prev:
                            norm3(b - 1)
                        if (kv, u) == VALUES_AT and nxt:
                            values(b + 1, 1 - par, bank_uses("QKV1", b + 1))
                        if (kv, u) == CLIP_AT and nxt:
                            clip(b + 2)
                        if (kv, u) == NORM2_AT and nxt:
                            norm2(b + 2)

            body(0, 0, 0, prev=False)
            with dve.Fori(0, B // 2 - 1) as i:
                body(i * 2 + 1, 1, i)
                body(i * 2 + 2, 0, i + 1)
            body(B - 1, 1, B // 2 - 1, nxt=False)
            last = post_use(B, 0)
            avt(B - 1, 1, KVH - 1, last)
            for n, name in enumerate(TAIL):
                n += last + 1
                if name == "OUTP":
                    outp(B - 1, n)
                    norm3(B - 1)
                elif name == "ROUTER":
                    router(B - 1, n)
                    expert_in(B - 1, 1, B // 2 - 1)
                elif name in ("GATE0", "GATE1"):
                    gate(B - 1, n, int(name[4]))
                elif name in ("UP0", "UP1"):
                    up(B - 1, n, int(name[2]), tail=True)
                    if name == "UP0":
                        dve.wait_ge(s["table_ps"], 1)
                        v.tensor_copy(s_row[:], bank[0][0:2, 0:P]).then_inc(s["table_ready"], 1)
                elif name == "RANK":
                    rank(B - 1, 1, B // 2 - 1, n)
                    dve.wait_ge(s["post_free"], n + 1)
                    v.tensor_copy(base_i[:], e_base[0:1, :]).then_inc(s["table"], 1)
                    v.tensor_tensor(cnt[:], e_base[:], e_start[:], ALU.subtract).then_inc(s["table"], 1)
                    dve.wait_ge(s["table"], 2)
                    v.tensor_scalar(cnt_i[:], cnt[:], float(P - 1), None, ALU.add).then_inc(s["table"], 1)
                    dve.wait_ge(s["table"], 3)
                    v.tensor_scalar(ntile_i[:], cnt_i[:], P.bit_length() - 1, None, ALU.logical_shift_right).then_inc(s["table"], 1)
                    dve.wait_ge(s["table"], 4)
                    v.tensor_copy(ntile[:], ntile_i[:]).then_inc(s["table"], 1)
                    dve.wait_ge(s["table"], 5)
                    v.tensor_tensor_scan(ends[:], ones[:, 0:NE], ntile[:], 0.0, ALU.mult, ALU.add).then_inc(s["table"], 1)
                    dve.wait_ge(s["table"], 6)
                    v.tensor_scalar(ended[:], ends[:], slot_no[:, 0:1], None, ALU.is_le).then_inc(s["table"], 1)
                    dve.wait_ge(s["table"], 7)
                    v.tensor_reduce(s_val[:, 0:1], ended[:], AX, ALU.add).then_inc(s["table"], 1)
                    v.tensor_tensor(s_tmp[:], ended[:], ntile[:], ALU.mult).then_inc(s["table"], 1)
                    dve.wait_ge(s["table"], 9)
                    v.tensor_reduce(s_val[:, 1:2], s_tmp[:], AX, ALU.add).then_inc(s["table"], 1)
                    v.tensor_scalar(s_tab[:, 1:2], s_val[:, 0:1], float(NE - 1), None, ALU.min).then_inc(s["table"], 1)
                    dve.wait_ge(s["table"], 11)
                    v.tensor_tensor(s_val[:, 2:3], slot_no[:], s_val[:, 1:2], ALU.subtract).then_inc(s["table"], 1)
                    v.tensor_scalar(s_val[:, 3:4], s_val[:, 0:1], float(CAP), None, ALU.mult).then_inc(s["table"], 1)
                    dve.wait_ge(s["table"], 13)
                    v.scalar_tensor_tensor(s_val[:, 4:5], s_val[:, 2:3], float(P), s_val[:, 3:4], ALU.mult, ALU.add)\
                     .then_inc(s["table"], 1)
                    dve.wait_ge(s["table"], 14)
                    v.tensor_scalar(s_tab[:, 0:1], s_val[:, 4:5], float(NE * CAP), None, ALU.min).then_inc(s["table"], 1)
                elif name == "DOWN":
                    carry(B - 1, 1, n)

            def d_step(n, r):
                p = r % 2
                dve.wait_ge(s["d_tanh"], n + 1)
                v.scalar_tensor_tensor(d_th[p][:], d_th[p][:], 1.0, bank[2 + p][:, 0:FE], ALU.add, ALU.mult)\
                 .then_inc(s["d_sg"], 1)
                dve.wait_ge(s["d_sg"], n + 1)
                if not isinstance(n, int) or n >= 2:
                    dve.wait_ge(s["d_ht_ps"], n - 1)
                v.tensor_tensor(d_h[p][:], d_th[p][:], bank[2 + p][:, FE:2 * FE], ALU.mult).then_inc(s["d_hid"], 1)

            def d_output(n, r, past):
                dve.wait_ge(s["d_dn_ps"], n + 1)
                dve.wait_ge(s[f"out_sent{r}"], 16 * past)
                dve.wait_ge(s[f"slot_in{r}"], 16 * past + 16)
                v.scalar_tensor_tensor(d_out[r][:], bank[6 + r % 2][:, 0:P], 0.5, slot[r][:, P:2 * P], ALU.mult, ALU.add)\
                 .then_inc(s["d_out_ready"], 1)

            def d_slot(n, r, past):
                if not isinstance(n, int) or n + 1 < SLOTS:
                    d_step(n + 1, r + 1)
                if not isinstance(n, int) or n > 0:
                    back = (r - 1) % OUT_R
                    d_output(n - 1, back, past - (r == 0))

            d_step(0, 0)
            for n in range(OUT_R):
                d_slot(n, n, 0)
            with dve.Fori(1, FULL) as i:
                for r in range(OUT_R):
                    d_slot(i * OUT_R + r, r, i)
            for n in range(FULL * OUT_R, SLOTS):
                d_slot(n, n % OUT_R, n // OUT_R)
            d_output(SLOTS - 1, (SLOTS - 1) % OUT_R, (SLOTS - 1) // OUT_R)

        @block.tensor
        def _(pe):
            t = nc.tensor
            mm = lambda o, l, r, start=True, stop=True: t.matmul(o, l, r, start=start, stop=stop)
            pe.wait_ge(s["ident_ready"], 5)
            pe.wait_ge(s["w_attn"], 16 * 8)
            pe.wait_ge(s["s_dve"], 8)
            pe.wait_ge(s["w_moe"], 64)
            turn = lambda o, i: t.transpose(o, i, ident[0:i.shape[0], 0:i.shape[0]]).then_inc(s["s_pe1"], 1)
            turn(bank[0][:, 0:128], w_in["wv"][:])
            turn(bank[0][:, 128:192], scaled_p[:])
            turn(bank[0][0:64, 192:320], w_in["wqa"][:])
            turn(bank[0][0:32, 320:448], w_in["wkva"][:])
            turn(bank[0][:, 448:464], w_in["router"][:])
            for c in two:
                turn(bank[1][:, P * c:P * c + P], w_in["wg"][:, c])
                turn(bank[1][:, 256 + P * c:256 + P * c + P], w_in["wu"][:, c])
                turn(bank[2][:, P * c:P * c + P], w_in["wd"][:, P * c:P * c + P])
            pe.wait_ge(s["s_copy1"], 8)
            pe.wait_ge(s["const_dve"], 6)
            kv_cols = w_in["wkvb"][:].rearrange("p (n two) -> p n two", two=2)
            mm(bank[3][:, 0:128], wvt[:], w_in["wo"][:]).then_inc(s["s_pe2"], 1)
            mm(bank[3][:, 128:256], wqat[:], w_in["wqb"][:]).then_inc(s["s_pe2"], 1)
            mm(bank[3][:, 256:288], wkvat[:], kv_cols[:, :, 0]).then_inc(s["s_pe2"], 1)
            mm(bank[3][:, 288:320], wkvat[:], kv_cols[:, :, 1]).then_inc(s["s_pe2"], 1)
            mm(bank[3][:, 320:384], ones[0:NSPLAT, :], diag_a[:]).then_inc(s["s_pe2"], 1)
            mm(bank[3][:, 384:512], ones[0:1, :], w_in["bout"][:]).then_inc(s["s_pe2"], 1)
            pe.wait_ge(s["s_copy2"], 4)

            def turn_tiles(dst, src, idn=None):
                for j in range(TILES):
                    last = t.transpose(dst[:, P * j:P * j + P], src(j), ident[:])
                return last

            with pe.Fori(0, ROUNDS) as i:
                for q in lanes:
                    b = i * LANES + q
                    pe.wait_ge(s["a_zt"], LANES * i)
                    pe.wait_ge(s["a_xn"], 4 * b + 4)
                    turn_tiles(bank[2 * q], lambda j: a_xn[q][:, j]).then_inc(s["a_xt_ps"], 1)
                for q in lanes:
                    b = i * LANES + q
                    pe.wait_ge(s["a_xt"], b + 1)
                    for j in range(TILES):
                        o = bank[2 * q + 1][:, NSPLAT * j:NSPLAT * j + NSPLAT]
                        mm(o, a_xt[q][:, P * j:P * j + P], splat_t[:], stop=False)
                        last = mm(o, ones[0:NSPLAT, :], diag_p[:], start=False)
                    last.then_inc(s["a_d2_ps"], 1)
                for q in lanes:
                    b = i * LANES + q
                    pe.wait_ge(s["a_e"], b + 1)
                    for j in range(TILES):
                        mm(bank[2 * q + 1][:, 0:NSPLAT], a_xn[q][:, j], a_e[q][:, j], j == 0, j == TILES - 1)
                    for j in range(TILES):
                        last = mm(bank[2 * q + 1][0:NSPLAT, NSPLAT + P:NSPLAT + P + 1], a_e[q][:, j], ones[:, 0:1], j == 0, j == TILES - 1)
                    last.then_inc(s["a_gt_ps"], 1)
                for q in lanes:
                    for j in range(TILES):
                        last = t.transpose(bank[2 * q][0:NSPLAT, P * j:P * j + P], a_e[q][:, j], ident[:])
                    last.then_inc(s["a_et_ps"], 1)
                for q in lanes:
                    b = i * LANES + q
                    pe.wait_ge(s["a_gt"], b + 1)
                    mm(bank[2 * q + 1][0:NSPLAT, NSPLAT:NSPLAT + P], a_gt[q][:], wvo[:]).then_inc(s["a_m_ps"], 1)
                for q in lanes:
                    b = i * LANES + q
                    pe.wait_ge(s["a_m"], b + 1)
                    pe.wait_ge(s["a_et"], b + 1)
                    for h in two:
                        for j in two:
                            tile = 2 * h + j
                            last = mm(bank[2 * q + h][:, (P + 1) * j:(P + 1) * (j + 1)], a_et[q][:, P * tile:P * tile + P], a_m[q][:])
                        last.then_inc(s["a_o_ps"], 1)
                for q in lanes:
                    b = i * LANES + q
                    pe.wait_ge(s["a_zn"], 4 * b + 4)
                    turn_tiles(bank[2 * q], lambda j: a_xn[q][:, j]).then_inc(s["a_zt_ps"], 1)
            pe.wait_ge(s["a_zt"], B)
            pe.wait_ge(s["w_rope"], 32)

            def pre_bank(n):
                if not isinstance(n, int) or n > 0:
                    pe.wait_ge(s["pre_free"], n)

            def post_bank(n):
                if not isinstance(n, int) or n > 0:
                    pe.wait_ge(s["post_free"], n)

            def y(b, n):
                pre_bank(n)
                pe.wait_ge(s["zclip"], b + 1)
                for j in range(TILES):
                    last = mm(PREB[:, P * j:P * j + P], zc[:, P * j:P * j + P], wq[:])
                last.then_inc(s["pre_full"], 1)

            def t2(b, n):
                pre_bank(n)
                pe.wait_ge(s["xn2_ready"], 4 * b + 4)
                turn_tiles(PREB, lambda j: xn2[:, j]).then_inc(s["pre_full"], 1)

            def qkv(b, n, hf):
                pre_bank(n)
                for j in two:
                    c = P * (2 * hf + j)
                    last = mm(PREB[:, (RC + KC) * j:(RC + KC) * (j + 1)], xt2[:, c:c + P], wqkv[:])
                last.then_inc(s["pre_full"], 1)

            def split_a(b, n):
                pre_bank(n)
                pe.wait_ge(s["part_lo"], 2 * b + 2)
                both = PREB[:].bitcast(BF16)
                for c in two:
                    for j in range(TILES):
                        last = t.transpose(both[:, T * c + P * j:T * c + P * j + P], parts[:, j, 0:QC, c], identb[:])
                last.then_inc(s["pre_full"], 1)

            def split_b(b, n):
                pre_bank(n)
                both = PREB[:].bitcast(BF16)
                for j in range(TILES):
                    t.transpose(both[:, P * j:P * j + P], parts[:, j, 0:QC, 2], identb[:])
                for j in range(TILES):
                    last = t.transpose(both[0:3 * KC, T + P * j:T + P * j + P], parts[:, j, QC:RC].rearrange("p k c -> p (k c)"), identb[:])
                last.then_inc(s["pre_full"], 1)

            def ct(gb, kv, n):
                pre_bank(n)
                pe.wait_ge(s["shift_split"], 2 * (KVH * gb + kv) + 2)
                both = PREB[:].bitcast(BF16)
                for j in range(TILES):
                    last = t.transpose(both[0:2 * GRP, P * j:P * j + P], shift[kv % 2][:, j], identb[:])
                last.then_inc(s["pre_full"], 1)

            def avt(b, kv, n):
                post_bank(n)
                pe.wait_ge(s["av_copied"], KVH * b + kv + 1)
                turn_tiles(POSTB, lambda j: av_sb[kv % 2][:, P * j:P * j + P]).then_inc(s["post_full"], 1)

            def ot(b, par, n):
                post_bank(n)
                turn_tiles(POSTB, lambda j: o_tok[par][:, j]).then_inc(s["post_full"], 1)

            def outp(b, n):
                post_bank(n)
                for j in range(TILES):
                    last = mm(POSTB[:, P * j:P * j + P], o_t[:, P * j:P * j + P], w_in["wout"][:])
                last.then_inc(s["post_full"], 1)

            def t3(b, n):
                post_bank(n)
                pe.wait_ge(s["xn3_ready"], 4 * b + 4)
                turn_tiles(POSTB, lambda j: xn3[:, j]).then_inc(s["post_full"], 1)

            def router(b, n):
                post_bank(n)
                for j in range(TILES):
                    last = mm(POSTB[:, NE * j:NE * j + NE], xt3[:, P * j:P * j + P], router_t[:])
                last.then_inc(s["post_full"], 1)

            def inner(b, n, w, hf, pre=False):
                (pre_bank if pre else post_bank)(n)
                mm((PREB if pre else POSTB)[:], w[:, P * hf:P * hf + P], xt3[:]).then_inc(s["pre_full" if pre else "post_full"], 1)

            def rank(b, n):
                post_bank(n)
                pe.wait_ge(s["route"], 5 * b + 4)
                for j in range(TILES):
                    o = POSTB[:, NE * j:NE * j + NE]
                    for k in range(j):
                        mm(o, onesb[:], onehot[:, k], k == 0, False)
                    mm(o, before[:], onehot[:, j], j == 0, True)
                for k in range(TILES):
                    last = mm(POSTB[:, TILES * NE:(TILES + 1) * NE], onesb[:], onehot[:, k], k == 0, k == TILES - 1)
                last.then_inc(s["post_full"], 1)

            def down_shared(b, n, tail=False):
                post_bank(n)
                if not tail:
                    pe.wait_ge(s["pre_free"], bank_uses("UP1", b))
                for j in range(TILES):
                    for c in two:
                        last = mm(POSTB[:, P * j:P * j + P], hid[:, c, P * j:P * j + P], down_t[:, c], c == 0, c == 1)
                last.then_inc(s["post_full"], 1)

            def max_unit(b, par, past, kv, u):
                qtile, h0, nh = MAX_UNITS[u]
                k = UNITS * (KVH * b + kv) + u
                if kv == 0 and u == 0:
                    pe.wait_ge(s[f"parts_loaded{par}"], 12 * 16 * past + 12 * 16)
                if not isinstance(k, int) or k >= 2:
                    pe.wait_ge(s["max_done"], k - 1)
                n = P * (qtile + 1)
                o = MAXB[(kv * UNITS + u) % 2]
                for h in range(nh):
                    q = q8[par][0:64, GRP * kv + h0 + h, P * qtile:P * qtile + P]
                    mm(o[:, n * h:n * h + n], q, k8[par][0:64, kv, 0:n], True, False)
                    last = mm(o[:, n * h + n - P:n * h + n], identb[:], causal[:], False, True)
                last.then_inc(s["max_ps"], 1)

            def score_unit(b, par, past, kv, u):
                ktile, h0, nh = SCORE_UNITS[u]
                g = KVH * b + kv
                if u == 0:
                    pe.wait_ge(s[f"shift_loaded{kv % 2}"], 16 * (2 * b + kv // 2) + 16)
                back, was = prior(u, SC_BANKS)
                if not (isinstance(b, int) and b == 0 and kv == 0) or back == 0:
                    pe.wait_ge(s["exp_done"], UNITS * (g - back) + was + 1)
                n = T - P * ktile
                for h in range(nh):
                    last = mm(SCB[u % SC_BANKS][:, n * h:n * h + n], k8[par][:, kv, P * ktile:P * ktile + P],
                              q8[par][:, GRP * kv + h0 + h, P * ktile:T])
                last.then_inc(s["score_ps"], 1)

            def av(b, par, kv, ktile):
                g = KVH * b + kv
                pe.wait_ge(s["masked"], UNITS * g + LAST_OF_TILE[ktile] + 1)
                if ktile == 0:
                    if kv == 0:
                        pe.wait_ge(s["v_ready"], b + 1)
                    if not (isinstance(b, int) and b == 0 and kv == 0):
                        pe.wait_ge(s["av_copied"], g)
                n = T - P * ktile
                for u, (kt_, h0, nh) in enumerate(SCORE_UNITS):
                    if kt_ != ktile:
                        continue
                    for h in range(nh):
                        c = 32 * (h0 + h)
                        last = t.matmul(AVB[c:c + 32, P * ktile:T], vv[par][:, ktile, kv], w_ring[u % W_RING][:, n * h:n * h + n],
                                        start=ktile == 0, stop=ktile == TILES - 1)
                last.then_inc(s["av_ps"], 1)

            for n, (name, b) in enumerate(HEAD):
                {"Y": y, "T2": t2, "SPLITA": split_a, "SPLITB": split_b}[name](b, n) if name[0] != "Q" else qkv(b, n, int(name[3]))
            for kv in range(2):
                for u in range(UNITS):
                    max_unit(0, 0, 0, kv, u)
            ct(0, 0, HEAD_USES - 1)

            def body(b, par, past, prev=True, nxt=True):
                order, _ = plan(prev, nxt)
                for kv in range(KVH):
                    for u in range(UNITS):
                        for name, off, n in order.get((kv, u), ()):
                            pre, post = pre_use(b, n), post_use(b, n)
                            if name == "Y":
                                y(b + 2, pre)
                            elif name == "T2":
                                t2(b + 2, pre)
                            elif name in ("QKV0", "QKV1"):
                                qkv(b + 2, pre, int(name[3]))
                            elif name == "SPLITA":
                                split_a(b + 1, pre)
                            elif name == "SPLITB":
                                split_b(b + 1, pre)
                            elif name == "CT":
                                ct(b + off, CT_OF[kv], pre)
                            elif name == "AVT":
                                avt(*((b, kv - 1) if off == 0 else (b - 1, KVH - 1)), post)
                            elif name == "OT":
                                ot(b - 1, 1 - par, post)
                            elif name == "OUTP":
                                outp(b - 1, post)
                            elif name == "T3":
                                t3(b - 1, post)
                            elif name == "ROUTER":
                                router(b - 1, post)
                            elif name in ("GATE0", "GATE1"):
                                inner(b - 1, post, gate_t, int(name[4]))
                            elif name in ("UP0", "UP1"):
                                inner(b - 1, pre, up_t, int(name[2]), pre=True)
                            elif name == "RANK":
                                rank(b - 1, post)
                            elif name == "DOWN":
                                down_shared(b - 1, post)
                        if kv < 2:
                            max_unit(b, par, past, kv + 2, u)
                        elif nxt:
                            max_unit(b + 1, 1 - par, past + par, kv - 2, u)
                        score_unit(b, par, past, kv, u)
                        if u in AV_AT:
                            before_this, ktile = AV_AT[u]
                            if not before_this:
                                av(b, par, kv, ktile)
                            elif prev or kv:
                                av(*((b, par, kv - 1) if kv else (b - 1, 1 - par, KVH - 1)), ktile)

            body(0, 0, 0, prev=False)
            with pe.Fori(0, B // 2 - 1) as i:
                body(i * 2 + 1, 1, i)
                body(i * 2 + 2, 0, i + 1)
            body(B - 1, 1, B // 2 - 1, nxt=False)
            for before_this, ktile in sorted(AV_AT.values()):
                if before_this:
                    av(B - 1, 1, KVH - 1, ktile)
            last_post = post_use(B, 0)
            avt(B - 1, KVH - 1, last_post)
            for n, name in enumerate(TAIL):
                n += last_post + 1
                if name == "OT":
                    ot(B - 1, 1, n)
                elif name == "OUTP":
                    outp(B - 1, n)
                elif name == "T3":
                    t3(B - 1, n)
                elif name == "ROUTER":
                    router(B - 1, n)
                elif name in ("GATE0", "GATE1"):
                    inner(B - 1, n, gate_t, int(name[4]))
                elif name in ("UP0", "UP1"):
                    inner(B - 1, n, up_t, int(name[2]))
                    if name == "UP0":
                        pe.wait_ge(s["table"], 15)
                        t.transpose(bank[0][0:2, 0:P], s_tab[:], ident[:]).then_inc(s["table_ps"], 1)
                elif name == "RANK":
                    rank(B - 1, n)
                elif name == "DOWN":
                    down_shared(B - 1, n, tail=True)
            pe.wait_ge(s["table_ready"], 1)
            pe.wait_ge(s["post_free"], last_post + 1 + len(TAIL))
            pe.wait_ge(s["w_experts"], 32)

            def d_turn(n, r, past):
                pe.wait_ge(s[f"slot_in{r % OUT_R}"], 16 * (past + r // OUT_R) + 16)
                if not isinstance(n, int) or n >= 2:
                    pe.wait_ge(s["d_xt_ready"], n - 1)
                t.transpose(bank[r % 2][:, 0:P], slot[r % OUT_R][:, 0:P], ident[:]).then_inc(s["d_xt_ps"], 1)

            def d_gate_up(n, r):
                e = pe.value_load(s_row[1:2, bass.ds(n, 1)], min_val=0, max_val=NE - 1)
                pe.wait_ge(s["d_xt_ready"], n + 1)
                if not isinstance(n, int) or n >= 2:
                    pe.wait_ge(s["d_hid"], n - 1)
                mm(bank[2 + r % 2][:], d_xt[r % 2][:], gate_up[:, bass.ds(e, 1)].rearrange("p a f -> p (a f)"))\
                  .then_inc(s["d_gu_ps"], 1)

            def d_turn_inner(n, r):
                pe.wait_ge(s["d_hid"], n + 1)
                if not isinstance(n, int) or n >= 2:
                    pe.wait_ge(s["d_ht_ready"], n - 1)
                for c in two:
                    last = t.transpose(bank[4 + r % 2][:, P * c:P * c + P], d_h[r % 2][:, P * c:P * c + P], ident[:])
                last.then_inc(s["d_ht_ps"], 1)

            def d_down(n, r):
                e = pe.value_load(s_row[1:2, bass.ds(n, 1)], min_val=0, max_val=NE - 1)
                pe.wait_ge(s["d_ht_ready"], n + 1)
                if not isinstance(n, int) or n >= 2:
                    pe.wait_ge(s["d_out_ready"], n - 1)
                for c in two:
                    last = mm(bank[6 + r % 2][:, 0:P], d_ht[r % 2][:, P * c:P * c + P],
                              down[:, bass.ds(e, 1), c].rearrange("p a f -> p (a f)"), c == 0, c == 1)
                last.then_inc(s["d_dn_ps"], 1)

            def d_slot(n, r, past):
                more = SLOTS - n if isinstance(n, int) else 3
                if more > 1:
                    d_gate_up(n + 1, r + 1)
                if more > 2:
                    d_turn(n + 2, r + 2, past)
                d_turn_inner(n, r)
                if not isinstance(n, int) or n > 0:
                    d_down(n - 1, r + 1)

            d_turn(0, 0, 0)
            d_turn(1, 1, 0)
            d_gate_up(0, 0)
            for n in range(OUT_R):
                d_slot(n, n, 0)
            with pe.Fori(1, FULL) as i:
                for r in range(OUT_R):
                    d_slot(i * OUT_R + r, r, i)
            for n in range(FULL * OUT_R, SLOTS):
                d_slot(n, n % OUT_R, n // OUT_R)
            d_down(SLOTS - 1, (SLOTS - 1) % OUT_R)


_NAMES = {"x": "L0_attn_token_embeddings", "p": "L0_attn_splat_positions", "logs": "L0_attn_splat_log_scales",
          "amp": "L0_attn_splat_amplitudes", "wv": "L0_attn_Wv", "wo": "L0_attn_Wo", "wffn": "L0_ffn_weight",
          "gamma": "L0_ffn_ln_gamma", "beta": "L0_ffn_ln_beta", "wqa": "L1_attn_Wqa", "wqb": "L1_attn_Wqb",
          "wkva": "L1_attn_Wkva", "wkvb": "L1_attn_Wkvb", "wout": "L1_attn_Wout", "bout": "L1_attn_bout",
          "router": "L1_ffn_w_router", "gate_up": "L1_ffn_gate_up_proj", "down": "L1_ffn_down_proj",
          "wg": "L1_ffn_w_gate", "wu": "L1_ffn_w_up", "wd": "L1_ffn_w_down"}


def rope_tables():
    inv = (1.0 / 10000.0 ** (np.arange(0, HD, 2, dtype=np.float32) / np.float32(HD))).astype(np.float32)
    ang = np.outer(np.arange(T, dtype=np.float32), inv).astype(np.float32)
    cos = np.repeat(np.cos(ang), 2, axis=1)
    sin = np.repeat(np.sin(ang), 2, axis=1) * np.tile([-1.0, 1.0], HD // 2)
    out = []
    for t in (cos, sin):
        full = np.concatenate([np.tile(t, (1, H)) * HD ** -0.5, np.tile(t, (1, KVH))], axis=1)
        out.append(np.ascontiguousarray(full.reshape(TILES, P, RC).transpose(1, 0, 2).astype(np.float32)))
    return out


def kernel(**inputs):
    import numpy as _np
    import concourse.bacc as _bacc
    from concourse.bass_utils import run_bass_kernel_spmd as _run

    nc = _bacc.Bacc("TRN2", target_bir_lowering=False, num_devices=1)
    rope_c, rope_s = rope_tables()
    arrays = {n: _np.ascontiguousarray(inputs[full]) for n, full in _NAMES.items()} | {"rope_c": rope_c, "rope_s": rope_s}
    ins = {n: nc.dram_tensor(f"in_{n}", a.shape, mybir.dt.from_np(a.dtype), kind="ExternalInput").ap()
           for n, a in arrays.items()}
    out = nc.dram_tensor("out_rows", (B, T, P), F32, kind="ExternalOutput").ap()
    build(nc, ins, out)
    r = _run(nc, [{f"in_{n}": a for n, a in arrays.items()}], core_ids=[0])
    return r.results[0]["out_rows"]
```

```python
from contextlib import ExitStack

import numpy as np
import concourse.bass as bass
from concourse import mybir

F32, BF16 = mybir.dt.float32, mybir.dt.bfloat16
I32, U32 = mybir.dt.int32, mybir.dt.uint32
ALU = mybir.AluOpType
ACT = mybir.ActivationFunctionType
AX = mybir.AxisListType.X
REDUCE_ADD, REDUCE_MAX = bass.bass_isa.ReduceOp.add, bass.bass_isa.ReduceOp.max

P = 128
B, T = 8, 512
TILES = T // P
NSPLAT = 64
H, KVH, HD = 16, 4, 8
GRP = H // KVH
QC, KC = H * HD, KVH * HD
RC = QC + KC
NE, FE = 16, 256
LN_EPS, FFN_LN_EPS, EPS_BETA, EPS_SPLAT = 1e-5, 1e-3, 1e-5, 1e-8
QB = 128.0
MASKED = -1e30
CAP = B * T + P
ROW = 2 * P + 1
NOBODY = B * T
SLOTS = B * T // P + NE - 1
OUT_R = 8
FULL = (SLOTS - 2) // OUT_R
LANES, ROUNDS = 4, B // 4

MAX_UNITS = [(0, 0, 4), (1, 0, 2), (1, 2, 2)] + [(2, h, 1) for h in range(4)] + [(3, h, 1) for h in range(4)]
SCORE_UNITS = [(0, h, 1) for h in range(4)] + [(1, h, 1) for h in range(4)] + [(2, 0, 2), (2, 2, 2), (3, 0, 4)]
UNITS = len(SCORE_UNITS)
LAST_OF_TILE = [3, 7, 9, 10]
W_RING = UNITS
AV_AT = {7: (0, 0), 10: (0, 1), 1: (1, 2), 2: (1, 3)}
AV_COPY_AT, CLIP_AT, VALUES_AT = 3, (1, 5), (0, 9)
SC_BANKS = 3

PLAN = {
    (0, 3): [("CT", 0)], (0, 5): [("SPLITA", 1)], (0, 6): [("AVT", -1)], (0, 8): [("SPLITB", 1), ("OT", -1)],
    (0, 10): [("OUTP", -1)],
    (1, 3): [("CT", 0)], (1, 6): [("AVT", 0)], (1, 7): [("Y", 2)], (1, 8): [("T3", -1)], (1, 10): [("ROUTER", -1)],
    (2, 1): [("GATE0", -1)], (2, 2): [("UP0", -1)], (2, 4): [("GATE1", -1)], (2, 5): [("CT", 0)], (2, 6): [("UP1", -1)],
    (2, 8): [("T2", 2)], (2, 9): [("AVT", 0)], (2, 10): [("QKV0", 2)],
    (3, 1): [("RANK", -1)], (3, 3): [("QKV1", 2)], (3, 4): [("DOWN", -1)], (3, 5): [("CT", 1)], (3, 7): [("AVT", 0)],
}
DVE_STEPS = {n: [(n, 0)] for n in ("QKV0", "QKV1", "AVT", "RANK", "DOWN")} | {
    "Y": [("Y", 0), ("STATS2A", 1), ("STATS2B", 2)], "OUTP": [("OUTP", 0), ("STATS3A", 1), ("STATS3B", 3)],
    "UP0": [("UP0", 1)], "UP1": [("UP1", 1)], "GATE0": [("GATE0", 1)], "GATE1": [("GATE1", 1)],
    "ROUTER": [("ROUTER", 0), ("EXPERT_IN", 2)]}
ACT_STEPS = {n: [(n, 0)] for n in ("T2", "SPLITA", "SPLITB", "CT", "OT", "T3", "GATE0", "GATE1")} | {
    "Y": [("NORM2", 5)], "OUTP": [("NORM3", 5)], "ROUTER": [("ROUTER", 1), ("EXPERT_IN", 3)],
    "QKV0": [("HIGH", 2), ("MID", 4)], "QKV1": [("HIGH", 2), ("MID", 4)]}
POOL_STEPS = {"Y": [("ROOT2", 3), ("XBIAS", 12)], "OUTP": [("ROOT3", 4)], "DOWN": [(f"SCATTER{j}", j + 2) for j in range(TILES)],
              "QKV0": [("ADD", 1), ("REST", 3), ("LOW", 5)], "QKV1": [("ADD", 1), ("REST", 3), ("LOW", 5)]}
PRE_PIECES = ("Y", "T2", "QKV0", "QKV1", "SPLITA", "SPLITB", "CT", "UP0", "UP1")
CT_OF = {0: 1, 1: 2, 2: 3, 3: 0}


def plan(prev, nxt):
    out, n = {}, {"pre": 0, "post": 0}
    for kv in range(KVH):
        for u in range(UNITS):
            for name, off in PLAN.get((kv, u), ()):
                if (off < 0 and not prev) or (off > 0 and not nxt):
                    continue
                bank = "pre" if name in PRE_PIECES else "post"
                out.setdefault((kv, u), []).append((name, off, n[bank]))
                n[bank] += 1
    return out, n


def steps_of(order, steps):
    out = {}
    for (kv, u), pieces in order.items():
        for name, off, n in pieces:
            for step, delay in steps.get(name, ()):
                out.setdefault(divmod(kv * UNITS + u + delay, UNITS), []).append((step, name, off, n))
    return out


PRE_USES, POST_USES = plan(True, True)[1]["pre"], plan(True, True)[1]["post"]
HEAD = [("Y", 0), ("T2", 0), ("QKV0", 0), ("QKV1", 0), ("Y", 1), ("SPLITA", 0), ("SPLITB", 0),
        ("T2", 1), ("QKV0", 1), ("QKV1", 1)]
HEAD_MAX = {("T2", 1): range(0, 4), ("QKV0", 1): range(4, UNITS)}
HEAD_USES = len(HEAD) + 1
FIRST_PRE, FIRST_POST = plan(False, True)[1]["pre"], plan(False, True)[1]["post"]
TAIL = ["OT", "OUTP", "T3", "ROUTER", "RANK", "GATE0", "UP0", "GATE1", "UP1", "DOWN"]


def pre_use(b, n):
    return HEAD_USES + (n if isinstance(b, int) and b == 0 else FIRST_PRE + PRE_USES * (b - 1) + n)


def post_use(b, n):
    return n if isinstance(b, int) and b == 0 else FIRST_POST + POST_USES * (b - 1) + n


def bank_uses(name, b, kv=None):
    if isinstance(b, int) and (name, b) in HEAD:
        return HEAD.index((name, b)) + 1
    if name == "CT" and kv == 0 and isinstance(b, int) and b == 0:
        return HEAD_USES
    if name in TAIL and isinstance(b, int) and b == B - 1:
        return post_use(B, 0) + 1 + TAIL.index(name) + 1
    off = {0: 1, None: None}.get(kv, 0) if name == "CT" else next(o for v in PLAN.values() for p, o in v if p == name)
    body = b - off
    order, _ = plan(not isinstance(body, int) or body > 0, not isinstance(body, int) or body < B - 1)
    n = next(n for (slot, u), v in order.items() for p, o, n in v if p == name and (kv is None or CT_OF[slot] == kv))
    return (pre_use if name in PRE_PIECES else post_use)(body, n) + 1


def prior(u, ring):
    if u >= ring:
        return 0, u - ring
    return 1, max(v for v in range(UNITS) if v % ring == u)


def carve(region):
    at = 0

    def tile(shape):
        nonlocal at
        n = int(np.prod(shape[1:]))
        view = region[0:shape[0], at:at + n]
        at += n
        assert at <= region.shape[1], (at, region.shape)
        if len(shape) == 3:
            view = view.rearrange("p (a b) -> p a b", a=shape[1])
        elif len(shape) == 4:
            view = view.rearrange("p (a b c) -> p a b c", a=shape[1], b=shape[2])
        return view
    return tile


def build(nc, ins, out):
    ctx = ExitStack()
    with ctx:
        def sb(name, shape, dt=F32):
            return ctx.enter_context(nc.sbuf_tensor(name, shape, dt))

        def sem(name):
            return ctx.enter_context(nc.semaphore(name))

        x_d = ins["x"].rearrange("b (j p) f -> b p j f", p=P)
        out_rows = out.rearrange("b t f -> (b t) f")
        rows_d = nc.dram_tensor("expert_rows", [NE * CAP + P, ROW], F32, kind="Internal").ap()
        q_d = [nc.dram_tensor(f"q_parts{i}", [3, QC, T], BF16, kind="Internal").ap() for i in range(2)]
        k_d = [nc.dram_tensor(f"k_parts{i}", [KC, 3, T], BF16, kind="Internal").ap() for i in range(2)]
        c_d = [nc.dram_tensor(f"shift_parts{i}", [2, GRP, T], BF16, kind="Internal").ap() for i in range(2)]

        xres = sb("xres", [P, B + 1, TILES, P])
        zt = sb("zt", [P, B + 1, T])
        gate_up = sb("gate_up", [P, NE, 2 * FE])
        down = zt[:, 0:B].rearrange("p b t -> p (b t)").rearrange("p (e c f) -> p e c f", e=NE, c=FE // P)
        stage = sb("stage", [P, W_RING * T])
        splat_tile, mixer_tile, expert_tile = carve(stage), carve(stage), carve(stage)
        turned = sb("turned", [P, 2800])
        setup_tile, output_tile = carve(turned), carve(turned)
        two = range(2)
        ident, identb = sb("ident", [P, P]), sb("identb", [P, P], BF16)
        causal = sb("causal", [P, P], BF16)
        before = sb("before", [P, P], BF16)
        onesb, ones = sb("onesb", [P, P], BF16), sb("ones", [P, P])
        half = sb("half", [P, TILES])
        causal_t = sb("causal_t", [P, P], BF16)
        idle, idle_pool = sb("idle", [P, 3]), sb("idle_pool", [P, 3])
        w_in = {n: setup_tile(s) for n, s in {
            "p": [NSPLAT, P], "wv": [P, P], "wo": [P, P], "wffn": [P, P], "wqa": [P, 64], "wqb": [64, P],
            "wkva": [P, 32], "wkvb": [32, 2 * KC], "router": [NE, P],
            "wg": [P, 2, P], "wu": [P, 2, P], "wd": [P, FE]}.items()} | {
            "wout": sb("w_wout", [P, P]), "bout": sb("w_bout", [1, P])}
        logs, amp = sb("logs", [NSPLAT, 1]), sb("amp", [NSPLAT, 1])
        gamma_c, beta_c = sb("gamma_c", [P, 1]), sb("beta_c", [P, 1])
        rope_c, rope_s = sb("rope_c", [P, TILES, RC]), sb("rope_s", [P, TILES, RC])
        small = sb("small", [P, 16])
        splat_t = sb("splat_t", [P, NSPLAT])
        scaled_p = setup_tile([NSPLAT, P])
        squares = setup_tile([NSPLAT, P])
        diag_a = sb("diag_a", [NSPLAT, NSPLAT])
        a_rows = sb("a_rows", [P, NSPLAT])
        wvt, wvo = setup_tile([P, P]), sb("wvo", [P, P])
        wqat, wkvat = setup_tile([64, P]), setup_tile([32, P])
        wqkv = sb("wqkv", [P, RC + KC])
        router_t = sb("router_t", [P, NE])
        gate_t, up_t = sb("gate_t", [P, FE]), sb("up_t", [P, FE])
        down_t = sb("down_t", [P, 2, P])
        wq_pos, wq_neg, wq = setup_tile([P, P]), setup_tile([P, P]), sb("wq", [P, P])
        bout_rows = sb("bout_rows", [P, P])
        e_base = sb("e_base", [P, NE])
        e_start = sb("e_start", [P, NE])
        priority = sb("priority", [P, NE])
        token_no = sb("token_no", [P, B, TILES], I32)

        lanes = range(LANES)
        a_st = [sb(f"a_st{i}", [P, TILES, 6]) for i in lanes]
        a_mv = [sb(f"a_mv{i}", [P, TILES, 2]) for i in lanes]
        a_rs = [sb(f"a_rs{i}", [P, 2, TILES]) for i in lanes]
        f_mv = [sb(f"f_mv{i}", [P, TILES, 2]) for i in lanes]
        f_rs = [sb(f"f_rs{i}", [P, 2, TILES]) for i in lanes]
        a_sum = [sb(f"a_sum{i}", [NSPLAT, 1]) for i in lanes]
        a_den = [sb(f"a_den{i}", [P, 2, TILES]) for i in lanes]
        zmax = sb("zmax", [P, B])
        zlim = sb("zlim", [P, 4])

        zc = sb("zc", [P, T])
        st2, mv2, rs2 = sb("st2", [P, TILES, 6]), sb("mv2", [P, TILES, 2]), sb("rs2", [P, 4, TILES])
        xn2, xt2 = sb("xn2", [P, TILES, P]), sb("xt2", [P, T])
        rot_c, rot_s = sb("rot_c", [P, 2, RC]), sb("rot_s", [P, 2, RC])
        rot, rest = sb("rot", [P, 2, RC]), sb("rest", [P, 2, RC])
        parts = sb("parts", [P, TILES, RC, 3], BF16)
        qt = sb("qt", [P, 3, T], BF16)
        kt = sb("kt", [3 * KC, T], BF16)
        q8 = [sb(f"q8_{i}", [P, H, T], BF16) for i in two]
        k8 = [sb(f"k8_{i}", [P, KVH, T], BF16) for i in two]
        vv = [sb(f"vv{i}", [P, TILES, KVH, 32]) for i in two]
        v_next = sb("v_next", [P, TILES, KC])
        late_tile = carve(q8[1][:].rearrange("p h t -> p (h t)").bitcast(F32))
        lane_tile = [splat_tile, splat_tile, late_tile, late_tile]
        a_xn = [lane_tile[i]([P, TILES, P]) for i in lanes]
        a_xt = [lane_tile[i]([P, T]) for i in lanes]
        a_sq = [lane_tile[i]([P, T]) for i in lanes]
        a_et = [a_xt[i][0:NSPLAT] for i in lanes]
        a_e = [lane_tile[i]([P, TILES, NSPLAT]) for i in lanes]
        a_gt = [lane_tile[i]([P, NSPLAT]) for i in lanes]
        a_m = [lane_tile[i]([NSPLAT, P + 1]) for i in lanes]
        negmax = [sb(f"negmax{i}", [P, TILES, GRP]) for i in two]
        shift = [sb(f"shift{i}", [P, TILES, 2, GRP], BF16) for i in two]
        shift_t = [sb(f"shift_t{i}", [2 * GRP, T], BF16) for i in two]
        w_ring = [mixer_tile([P, T]) for i in range(W_RING)]
        av_sb = [output_tile([P, T]) for i in two]
        rden = sb("rden", [P, TILES, GRP])
        o_tok = [output_tile([P, TILES, P]) for i in two]
        o_t = output_tile([P, T])
        st3, mv3, rs3 = sb("st3", [P, TILES, 6]), sb("mv3", [P, TILES, 2]), sb("rs3", [P, 4, TILES])
        xn3, xt3 = sb("xn3", [P, TILES, P]), sb("xt3", [P, T])
        lmax, score = sb("lmax", [P, TILES]), sb("score", [P, 2, TILES])
        top, pri, onehot_f = sb("top", [P, TILES, NE]), sb("pri", [P, TILES]), sb("onehot_f", [P, TILES, NE])
        onehot = sb("onehot", [P, TILES, NE], BF16)
        place, place_s = sb("place", [P, TILES, NE]), sb("place_s", [P, TILES])
        place_i = [sb(f"place_i{i}", [P, TILES], U32) for i in two]
        th, sg = sb("th", [P, T]), sb("sg", [P, T])
        hid = sb("hid", [P, 2, T])
        rows = [sb(f"rows{i}", [P, TILES, ROW]) for i in two]

        pad_rows = sb("pad_rows", [P, ROW])
        cnt, cnt_i, ntile_i = sb("cnt", [P, NE]), sb("cnt_i", [P, NE], I32), sb("ntile_i", [P, NE], I32)
        ntile, ends = sb("ntile", [P, NE]), sb("ends", [P, NE])
        slot_no = sb("slot_no", [P, 1])
        ended, s_tmp = sb("ended", [P, NE]), sb("s_tmp", [P, NE])
        s_val = sb("s_val", [P, 6])
        s_tab, s_row = sb("s_tab", [P, 2]), sb("s_row", [2, P], I32)
        base_i = sb("base_i", [1, NE], I32)
        slot = [expert_tile([P, ROW]) for i in range(OUT_R)]
        d_xt = [expert_tile([P, P]) for i in two]
        d_th = [expert_tile([P, FE]) for i in two]
        d_h = [expert_tile([P, FE]) for i in two]
        d_ht = [expert_tile([P, FE]) for i in two]
        d_out = [expert_tile([P, P]) for i in range(OUT_R)]

        bank = [ctx.enter_context(nc.psum_tensor(f"bank{i}", [P, T], F32)) for i in range(8)]
        MAXB, SCB, AVB, PREB, POSTB = bank[0:2], bank[2:5], bank[5], bank[6], bank[7]

        names = """w_p w_small w_ffn w_attn w_moe w_rope w_experts
            const_pool const_dve ident_ready s_dve s_act s_pe1 s_copy1 s_pe2 s_copy2 beta_part beta_sum wq_ready
            x_loaded0 x_loaded1 x_loaded2 x_loaded3
            a_stats a_rstd a_xn a_xt_ps a_xt a_d2_ps a_d2 a_e_ps a_e a_gt_ps a_gt a_et a_m_ps a_m a_o_ps a_den a_x1
            a_stats2 a_rstd2 a_zn a_zt_ps a_zt a_zmax zlim_part zlim_all zlim
            pre_full pre_free post_full post_free
            zclip x2 arg2 arg3 a_arg a_arg2 q8_clear xbias rstd2 xn2_ready rope_mul v_ready rope_add part_hi rest_lo part_mid part_lo
            parts_stored0 parts_stored1 parts_loaded0 parts_loaded1
            max_ps max_done shift_split shift_stored0 shift_stored1 shift_loaded0 shift_loaded1
            score_ps exp_done av_ps av_copied o_rden stats3 rstd3 xn3_ready
            route score_tanh expert_in tanh_g place_ready numbered
            rows_sent0 rows_sent1 pads_sent pad_ready table table_ps table_ready
            slot_in0 slot_in1 slot_in2 slot_in3 slot_in4 slot_in5 slot_in6 slot_in7 d_xt_ps d_xt_ready d_gu_ps d_tanh d_sg d_hid d_ht_ps d_ht_ready d_dn_ps
            d_out_ready scatter_turn out_sent0 out_sent1 out_sent2 out_sent3 out_sent4 out_sent5 out_sent6 out_sent7""".split()
        s = {n: sem(n) for n in names}

        block = ctx.enter_context(nc.Block())

        @block.sync
        def _(sp):
            load = lambda dst, src, sm: sp.dma_start(dst, src).then_inc(s[sm], 16)
            for q in lanes:
                load(xres[:, q], x_d[q], f"x_loaded{q}")
            load(w_in["p"][:], ins["p"], "w_p")
            with nc.allow_non_contiguous_dma(reason="columns of one value for each partition"):
                load(logs[:], ins["logs"].rearrange("(p a) -> p a", a=1), "w_small")
                load(amp[:], ins["amp"].rearrange("(p a) -> p a", a=1), "w_small")
                load(gamma_c[:], ins["gamma"].rearrange("(p a) -> p a", a=1), "w_small")
                load(beta_c[:], ins["beta"].rearrange("(p a) -> p a", a=1), "w_small")
            for n in ("wv", "wo"):
                load(w_in[n][:], ins[n], "w_attn")
            load(w_in["wffn"][:], ins["wffn"], "w_ffn")
            for n in ("wqa", "wqb", "wkva", "wkvb", "wout"):
                load(w_in[n][:], ins[n], "w_attn")
            load(w_in["bout"][:], ins["bout"].rearrange("(a f) -> a f", a=1), "w_attn")
            load(w_in["router"][:], ins["router"], "w_moe")
            load(w_in["wg"][:], ins["wg"].rearrange("(c p) f -> p c f", p=P), "w_moe")
            load(w_in["wu"][:], ins["wu"].rearrange("(c p) f -> p c f", p=P), "w_moe")
            load(w_in["wd"][:], ins["wd"], "w_moe")
            for q in lanes:
                sp.wait_ge(s[f"x_loaded{q}"], 16)
                load(xres[:, LANES + q], x_d[LANES + q], f"x_loaded{q}")
            load(rope_c[:], ins["rope_c"], "w_rope")
            load(rope_s[:], ins["rope_s"], "w_rope")
            load(gate_up[:], ins["gate_up"].rearrange("e p f -> p e f"), "w_experts")
            sp.wait_ge(s["pad_ready"], 1)
            sp.dma_start(rows_d[NE * CAP:NE * CAP + P, :], pad_rows[:]).then_inc(s["pads_sent"], 16)

            sp.wait_ge(s["const_dve"], 12)

            def parts_round_trip(b, par, past):
                sp.wait_ge(s["pre_free"], bank_uses("SPLITB", b))
                st, ld = s[f"parts_stored{par}"], s[f"parts_loaded{par}"]
                sp.wait_ge(ld, 12 * 16 * past)
                sp.dma_start(q_d[par].rearrange("c p t -> p c t"), qt[:]).then_inc(st, 16)
                sp.dma_start(k_d[par].rearrange("c p t -> (c p) t"), kt[:]).then_inc(st, 16)
                if not isinstance(b, int) or b >= 2:
                    sp.wait_ge(s["score_ps"], KVH * UNITS * (b - 1))
                if isinstance(b, int) and b == 1:
                    sp.wait_ge(s["q8_clear"], 1)
                sp.wait_ge(st, 32 * past + 32)
                for g, (qp, kp) in enumerate(((0, 0), (1, 0), (2, 0), (0, 1), (1, 1), (0, 2))):
                    r = slice(HD * g, HD * g + HD)
                    sp.dma_start(q8[par][r], q_d[par][qp].rearrange("(h d) t -> d h t", d=HD)).then_inc(ld, 16)
                    sp.dma_start(k8[par][r], k_d[par][:, kp].rearrange("(h d) t -> d h t", d=HD)).then_inc(ld, 16)

            def shift_round_trip(b, par, kv, groups):
                g = kv % 2
                sp.wait_ge(s["pre_free"], bank_uses("CT", b, kv))
                st, ld = s[f"shift_stored{g}"], s[f"shift_loaded{g}"]
                sp.wait_ge(ld, 16 * groups)
                sp.dma_start(c_d[g].rearrange("c h t -> (c h) t"), shift_t[g][:]).then_inc(st, 16)
                sp.wait_ge(st, 16 * groups + 16)
                if kv == 0 and not (isinstance(b, int) and b < 2):
                    sp.wait_ge(s["score_ps"], KVH * UNITS * (b - 1))
                sp.dma_start(q8[par][64:66, GRP * kv:GRP * kv + GRP, :], c_d[g]).then_inc(ld, 16)

            parts_round_trip(0, 0, 0)
            shift_round_trip(0, 0, 0, 0)

            def body(b, par, past, nxt=True):
                shift_round_trip(b, par, 1, 2 * b)
                if nxt:
                    parts_round_trip(b + 1, 1 - par, past + par)
                shift_round_trip(b, par, 2, 2 * b + 1)
                shift_round_trip(b, par, 3, 2 * b + 1)
                if nxt:
                    shift_round_trip(b + 1, 1 - par, 0, 2 * b + 2)

            body(0, 0, 0)
            with sp.Fori(0, B // 2 - 1) as i:
                body(i * 2 + 1, 1, i)
                body(i * 2 + 2, 0, i + 1)
            body(B - 1, 1, B // 2 - 1, nxt=False)

            sp.wait_ge(s["x2"], 8 * B)
            sp.dma_start(down[:], ins["down"].rearrange("e (c p) f -> p e c f", p=P)).then_inc(s["w_experts"], 16)

            sp.wait_ge(s["table"], 1)
            for e in range(NE):
                end = sp.value_load(base_i[0:1, e:e + 1], min_val=0, max_val=NE * CAP)
                sp.dma_start(rows_d[bass.ds(end, P), :], pad_rows[:]).then_inc(s["pads_sent"], 16)
            for i in two:
                sp.wait_ge(s[f"rows_sent{i}"], 16 * TILES * B // 2)
            sp.wait_ge(s["pads_sent"], 16 * (NE + 1))
            sp.wait_ge(s["table_ready"], 1)

            def load_slot(n, r, past, waits=True):
                at = sp.value_load(s_row[0:1, bass.ds(n, 1)], min_val=0, max_val=NE * CAP)
                if waits:
                    sp.wait_ge(s[f"out_sent{r}"], 16 * past)
                sp.dma_start(slot[r][:], rows_d[bass.ds(at, P), :]).then_inc(s[f"slot_in{r}"], 16)

            for n in range(OUT_R):
                load_slot(n, n, 0, waits=False)
            with sp.Fori(1, FULL) as i:
                for r in range(OUT_R):
                    load_slot(i * OUT_R + r, r, i)
            for n in range(FULL * OUT_R, SLOTS):
                load_slot(n, n % OUT_R, n // OUT_R)
            for r in range(OUT_R):
                sp.wait_ge(s[f"out_sent{r}"], 16 * len(range(r, SLOTS, OUT_R)))

        @block.gpsimd
        def _(pool):
            g = nc.gpsimd
            g.memset(ident[:], 0.0).then_inc(s["const_pool"], 1)
            g.memset(identb[:], 0.0).then_inc(s["const_pool"], 1)
            g.memset(causal[:], 0.0).then_inc(s["const_pool"], 1)
            g.memset(before[:], 0.0).then_inc(s["const_pool"], 1)
            g.memset(half[:], -0.5).then_inc(s["const_pool"], 1)
            g.memset(causal_t[:], 0.0).then_inc(s["const_pool"], 1)
            g.memset(idle_pool[:], 0.0).then_inc(s["const_pool"], 1)
            pool.wait_ge(s["const_pool"], 7)
            for m, op, fill, cm, step in ((ident, ALU.not_equal, 1.0, 1, -1), (identb, ALU.not_equal, 1.0, 1, -1),
                                          (causal, ALU.is_ge, MASKED, 1, -1), (before, ALU.is_ge, 1.0, 1, -1)):
                g.affine_select(out=m[:], in_=m[:], compare_op=op, fill=fill, base=0, pattern=[[step, P]],
                                channel_multiplier=cm).then_inc(s["ident_ready"], 1)
            g.affine_select(out=causal_t[:], in_=causal_t[:], compare_op=ALU.is_ge, fill=MASKED, base=0, pattern=[[1, P]],
                            channel_multiplier=-1).then_inc(s["ident_ready"], 1)
            g.iota(token_no[:], pattern=[[T, B], [P, TILES]], base=0, channel_multiplier=1).then_inc(s["const_pool"], 1)
            g.iota(s_tmp[:].bitcast(I32), pattern=[[CAP, NE]], base=0, channel_multiplier=0).then_inc(s["const_pool"], 1)
            g.iota(ended[:].bitcast(I32), pattern=[[-1, NE]], base=NE, channel_multiplier=0).then_inc(s["const_pool"], 1)
            g.iota(s_val[:, 0:1].bitcast(I32), pattern=[[0, 1]], base=0, channel_multiplier=1).then_inc(s["const_pool"], 1)
            g.memset(pad_rows[:], 0.0).then_inc(s["const_pool"], 1)
            g.iota(s_val[:, 1:2].bitcast(I32), pattern=[[0, 1]], base=NOBODY, channel_multiplier=0).then_inc(s["const_pool"], 1)
            pool.wait_ge(s["beta_part"], 1)
            g.partition_all_reduce(small[:, 9:10], small[:, 8:9], P, REDUCE_ADD).then_inc(s["beta_sum"], 1)

            clear = lambda tile: g.memset(tile[:].bitcast(F32) if tile.dtype != F32 else tile[:], 0.0)
            for tile in (k8[0], k8[1], q8[0]):
                clear(tile).then_inc(s["const_pool"], 1)

            def root(dst, src, sm):
                g.tensor_tensor(dst, src, half[:], ALU.pow).then_inc(s[sm], 1)

            def roots(i):
                for q in lanes:
                    b = i * LANES + q
                    pool.wait_ge(s["a_arg"], b + 1)
                    root(f_rs[q][:, 1], f_rs[q][:, 0], "a_rstd")

            roots(0)
            for i in range(ROUNDS):
                if i + 1 < ROUNDS:
                    roots(i + 1)
                for q in lanes:
                    b = i * LANES + q
                    pool.wait_ge(s["a_arg2"], b + 1)
                    root(a_rs[q][:, 1], a_rs[q][:, 0], "a_rstd2")
            pool.wait_ge(s["zlim_part"], 1)
            g.partition_all_reduce(zlim[:, 1:2], zlim[:, 0:1], P, REDUCE_MAX).then_inc(s["zlim_all"], 1)
            pool.wait_ge(s["a_zt"], B)
            clear(q8[1]).then_inc(s["q8_clear"], 1)

            def root2(b):
                pool.wait_ge(s["arg2"], 2 * b + 2)
                root(rs2[:, 1], rs2[:, 0], "rstd2")
                pool.wait_ge(s["rstd2"], 2 * b + 1)
                g.tensor_tensor(rs2[:, 3], rs2[:, 2], rs2[:, 1], ALU.mult).then_inc(s["rstd2"], 1)

            def xbias(b):
                pool.wait_ge(s["xn2_ready"], 4 * b + 4)
                xb = xres[:, b] if isinstance(b, int) else xres[:, bass.ds(b, 1)].rearrange("p a j f -> p (a j) f")
                g.tensor_tensor(xb, xb, bout_rows[:].unsqueeze(1).to_broadcast([P, TILES, P]), ALU.add)\
                 .then_inc(s["xbias"], 1)

            def add(b, hf):
                if not isinstance(b, int) or 2 * b + hf:
                    pool.wait_ge(s["rest_lo"], 2 * b + hf)
                pool.wait_ge(s["rope_mul"], 6 * b + 3 * hf + 3)
                g.tensor_tensor(rot[:], rot_c[:], rot_s[:], ALU.add).then_inc(s["rope_add"], 1)

            def part_rest(b, hf):
                if not isinstance(b, int) or 2 * b + hf:
                    pool.wait_ge(s["part_lo"], 2 * b + hf)
                pool.wait_ge(s["part_hi"], 2 * b + hf + 1)
                g.tensor_tensor(rest[:], rot[:], parts[:, 2 * hf:2 * hf + 2, :, 0], ALU.subtract).then_inc(s["rest_lo"], 1)

            def part_low(b, hf):
                pool.wait_ge(s["part_mid"], 2 * b + hf + 1)
                g.tensor_tensor(parts[:, 2 * hf:2 * hf + 2, :, 2], rest[:], parts[:, 2 * hf:2 * hf + 2, :, 1], ALU.subtract)\
                 .then_inc(s["part_lo"], 1)

            def outp(b, par):
                pool.wait_ge(s["arg3"], 2 * b + 2)
                root(rs3[:, 1], rs3[:, 0], "rstd3")
                pool.wait_ge(s["rstd3"], 2 * b + 1)
                g.tensor_tensor(rs3[:, 3], rs3[:, 2], rs3[:, 1], ALU.mult).then_inc(s["rstd3"], 1)

            def down_scatter(b, par, j):
                if j == 0:
                    pool.wait_ge(s["post_free"], bank_uses("DOWN", b))
                    pool.wait_ge(s["expert_in"], 4 * b + 4)
                    pool.wait_ge(s["numbered"], b + 1)
                    pool.wait_ge(s["place_ready"], 5 * b + 5)
                    g.tensor_tensor(idle_pool[:, 0:1], idle_pool[:, 1:2], idle_pool[:, 1:2], ALU.add)
                g.indirect_dma_start(rows_d, bass.IndirectOffsetOnAxis(place_i[par][:, j:j + 1], 0), rows[par][:, j, :],
                                     None, bounds_check=NE * CAP - 1, oob_is_err=False)\
                 .then_inc(s[f"rows_sent{par}"], 16)

            for b in two:
                root2(b)
                xbias(b)
                for hf in two:
                    add(b, hf)
                    part_rest(b, hf)
                    part_low(b, hf)

            def body(b, par, prev=True, nxt=True):
                steps = steps_of(plan(prev, nxt)[0], POOL_STEPS)
                for kv in range(KVH):
                    for u in range(UNITS):
                        for step, name, off, _ in steps.get((kv, u), ()):
                            if step == "ROOT3":
                                outp(b - 1, 1 - par)
                            elif step == "ROOT2":
                                root2(b + 2)
                            elif step == "XBIAS":
                                xbias(b + 2)
                            elif step.startswith("SCATTER"):
                                down_scatter(b - 1, 1 - par, int(step[7]))
                            else:
                                {"ADD": add, "REST": part_rest, "LOW": part_low}[step](b + 2, int(name[3]))

            body(0, 0, prev=False)
            with pool.Fori(0, B // 2 - 1) as i:
                body(i * 2 + 1, 1)
                body(i * 2 + 2, 0)
            body(B - 1, 1, nxt=False)
            outp(B - 1, 1)
            for j in range(TILES):
                down_scatter(B - 1, 1, j)

            def scatter(n, r, past):
                pool.wait_ge(s["d_out_ready"], n + 1)
                pool.wait_ge(s["scatter_turn"], n)
                g.tensor_tensor(idle_pool[:, 2:3], idle_pool[:, 1:2], idle_pool[:, 1:2], ALU.add).then_inc(s["scatter_turn"], 1)
                g.indirect_dma_start(out_rows, bass.IndirectOffsetOnAxis(slot[r][:, 2 * P:ROW].bitcast(U32), 0), d_out[r][:],
                                     None, bounds_check=B * T - 1, oob_is_err=False).then_inc(s[f"out_sent{r}"], 16)

            with pool.Fori(0, FULL) as i:
                for r in range(OUT_R):
                    scatter(i * OUT_R + r, r, i)
            for n in range(FULL * OUT_R, SLOTS):
                scatter(n, n % OUT_R, n // OUT_R)

        @block.scalar
        def _(act):
            a = nc.scalar
            act.wait_ge(s["w_small"], 64)
            act.wait_ge(s["const_dve"], 6)
            a.activation(small[0:NSPLAT, 0:1], logs[:], ACT.Exp, scale=-2.0).then_inc(s["s_act"], 1)
            act.wait_ge(s["s_pe1"], 11)
            for dst, src in ((wvt[:], bank[0][:, 0:128]), (splat_t[:], bank[0][:, 128:192]),
                             (wqat[:], bank[0][0:64, 192:320]), (wkvat[:], bank[0][0:32, 320:448]),
                             (router_t[:], bank[0][:, 448:464]), (gate_t[:], bank[1][:, 0:256]),
                             (up_t[:], bank[1][:, 256:512]), (down_t[:], bank[2][:, 0:256].rearrange("p (c f) -> p c f", c=2))):
                a.copy(dst, src).then_inc(s["s_copy1"], 1)
            act.wait_ge(s["s_pe2"], 6)
            for dst, src in ((wvo[:], bank[3][:, 0:128]), (wqkv[:], bank[3][:, 128:320]), (a_rows[:], bank[3][:, 320:384]),
                             (bout_rows[:], bank[3][:, 384:512])):
                a.copy(dst, src).then_inc(s["s_copy2"], 1)

            with act.Fori(0, ROUNDS) as i:
                for q in lanes:
                    b = i * LANES + q
                    act.wait_ge(s["a_xt_ps"], b + 1)
                    a.copy(a_xt[q][:], bank[2 * q][:]).then_inc(s["a_xt"], 1)
                    a.activation(a_sq[q][:], bank[2 * q][:], ACT.Square).then_inc(s["a_xt"], 1)
                for q in lanes:
                    b = i * LANES + q
                    act.wait_ge(s["a_d2"], b + 1)
                    a.activation(a_et[q], a_et[q], ACT.Exp, accum_out=a_sum[q][:]).then_inc(s["a_et"], 1)
                for q in lanes:
                    b = i * LANES + q
                    act.wait_ge(s["a_e_ps"], b + 1)
                    a.copy(a_e[q].rearrange("p j f -> p (j f)"), bank[2 * q][:, 0:TILES * NSPLAT]).then_inc(s["a_e"], 1)
                for q in lanes:
                    b = i * LANES + q
                    act.wait_ge(s["a_gt_ps"], b + 1)
                    a.copy(a_gt[q][:], bank[2 * q + 1][:, 0:NSPLAT]).then_inc(s["a_gt"], 1)
                for q in lanes:
                    b = i * LANES + q
                    act.wait_ge(s["a_zt_ps"], b + 1)
                    a.activation(zt[:, bass.ds(b, 1)].rearrange("p a t -> p (a t)"), bank[2 * q][:], ACT.Identity,
                                 bias=beta_c[:, 0:1], scale=gamma_c[:, 0:1]).then_inc(s["a_zt"], 1)

            def res(b):
                if isinstance(b, int):
                    return lambda j: xres[:, b, j]
                return lambda j: xres[:, bass.ds(b, 1), j].rearrange("p a f -> p (a f)")

            def normalise(dst, src, rs, sm):
                for j in range(TILES):
                    a.activation(dst[:, j], src(j), ACT.Identity, bias=rs[:, 3, j:j + 1], scale=rs[:, 1, j:j + 1])\
                     .then_inc(s[sm], 1)

            def norm2(b):
                act.wait_ge(s["rstd2"], 2 * b + 2)
                normalise(xn2, res(b), rs2, "xn2_ready")

            def norm3(b):
                act.wait_ge(s["rstd3"], 2 * b + 2)
                normalise(xn3, res(b), rs3, "xn3_ready")

            def expert_in(b, par, past):
                act.wait_ge(s["xn3_ready"], 4 * b + 4)
                act.wait_ge(s["route"], 5 * b + 5)
                act.wait_ge(s[f"rows_sent{par}"], 16 * TILES * past)
                for j in range(TILES):
                    a.mul(rows[par][:, j, 0:P], xn3[:, j], score[:, 1, j:j + 1]).then_inc(s["expert_in"], 1)

            def t2(b, n):
                act.wait_ge(s["pre_full"], n + 1)
                a.copy(xt2[:], PREB[:]).then_inc(s["pre_free"], 1)

            def high(b, hf):
                act.wait_ge(s["rope_add"], 2 * b + hf + 1)
                if hf == 0 and (not isinstance(b, int) or b > 0):
                    act.wait_ge(s["pre_full"], bank_uses("SPLITB", b - 1))
                a.copy(parts[:, 2 * hf:2 * hf + 2, :, 0], rot[:]).then_inc(s["part_hi"], 1)

            def mid(b, hf):
                act.wait_ge(s["rest_lo"], 2 * b + hf + 1)
                a.copy(parts[:, 2 * hf:2 * hf + 2, :, 1], rest[:]).then_inc(s["part_mid"], 1)

            def split_a(b, n, par, past):
                act.wait_ge(s["pre_full"], n + 1)
                if not isinstance(b, int) or b > 0:
                    act.wait_ge(s[f"parts_stored{1 - par}"], 32 * (past + par))
                a.copy(qt[:, 0:2], PREB[:].bitcast(BF16).rearrange("p (c t) -> p c t", c=2)).then_inc(s["pre_free"], 1)

            def split_b(b, n):
                act.wait_ge(s["pre_full"], n + 1)
                both = PREB[:].bitcast(BF16)
                a.copy(qt[:, 2], both[:, 0:T])
                a.copy(kt[:], both[0:3 * KC, T:2 * T]).then_inc(s["pre_free"], 1)

            def ct(gb, kv, n, groups):
                act.wait_ge(s["pre_full"], n + 1)
                act.wait_ge(s[f"shift_stored{kv % 2}"], 16 * groups)
                a.copy(shift_t[kv % 2][:], PREB[:].bitcast(BF16)[0:2 * GRP, 0:T]).then_inc(s["pre_free"], 1)

            def ot(b, n):
                act.wait_ge(s["post_full"], n + 1)
                a.copy(o_t[:], POSTB[:]).then_inc(s["post_free"], 1)

            def t3(b, n):
                act.wait_ge(s["post_full"], n + 1)
                a.copy(xt3[:], POSTB[:]).then_inc(s["post_free"], 1)

            def router(b):
                act.wait_ge(s["route"], 5 * b + 1)
                a.activation(score[:, 0], lmax[:], ACT.Tanh, scale=0.5).then_inc(s["score_tanh"], 1)

            def gate(b, n, hf):
                act.wait_ge(s["post_full"], n + 1)
                a.activation(th[:], POSTB[:], ACT.Tanh, scale=0.5).then_inc(s["tanh_g"], 1)

            def av_copy(b, kv):
                g = KVH * b + kv
                act.wait_ge(s["av_ps"], 4 * g + 4)
                a.copy(av_sb[kv % 2][:], AVB[:]).then_inc(s["av_copied"], 1)

            def exp(b, kv, u):
                ktile, h0, nh = SCORE_UNITS[u]
                g = KVH * b + kv
                act.wait_ge(s["score_ps"], UNITS * g + u + 1)
                back, v = prior(u, W_RING)
                if not (isinstance(b, int) and b == 0 and kv == 0) or back == 0:
                    done = next(k for k, last in enumerate(LAST_OF_TILE) if v <= last) + 1
                    act.wait_ge(s["av_ps"], 4 * (g - back) + done)
                cols = nh * (T - P * ktile)
                a.activation(w_ring[u % W_RING][:, 0:cols], SCB[u % SC_BANKS][:, 0:cols], ACT.Exp).then_inc(s["exp_done"], 1)

            for n, (name, b) in enumerate(HEAD):
                if name == "T2":
                    norm2(b)
                    t2(b, n)
                elif name in ("QKV0", "QKV1"):
                    high(b, int(name[3]))
                    mid(b, int(name[3]))
                elif name == "SPLITA":
                    split_a(b, n, b % 2, 0)
                elif name == "SPLITB":
                    split_b(b, n)
            ct(0, 0, HEAD_USES - 1, 0)

            def body(b, par, past, prev=True, nxt=True):
                steps = steps_of(plan(prev, nxt)[0], ACT_STEPS)
                before_prev = past + par - 1 if not isinstance(past, int) or prev else 0
                for kv in range(KVH):
                    for u in range(UNITS):
                        for step, name, off, n in steps.get((kv, u), ()):
                            pre, post = pre_use(b, n), post_use(b, n)
                            if step == "T2":
                                t2(b + 2, pre)
                            elif step == "NORM2":
                                norm2(b + 2)
                            elif step == "NORM3":
                                norm3(b - 1)
                            elif step == "EXPERT_IN":
                                expert_in(b - 1, 1 - par, before_prev)
                            elif step == "HIGH":
                                high(b + 2, int(name[3]))
                            elif step == "MID":
                                mid(b + 2, int(name[3]))
                            elif step == "SPLITA":
                                split_a(b + 1, pre, 1 - par, past + par)
                            elif step == "SPLITB":
                                split_b(b + 1, pre)
                            elif step == "CT":
                                c = CT_OF[kv]
                                ct(b + off, c, pre, 2 * (b + off) + c // 2)
                            elif step == "OT":
                                ot(b - 1, post)
                            elif step == "T3":
                                t3(b - 1, post)
                            elif step == "ROUTER":
                                router(b - 1)
                            elif step in ("GATE0", "GATE1"):
                                gate(b - 1, post, int(name[4]))
                        exp(b, kv, u)
                        if u == AV_COPY_AT and (prev or kv):
                            av_copy(*((b, kv - 1) if kv else (b - 1, KVH - 1)))

            body(0, 0, 0, prev=False)
            with act.Fori(0, B // 2 - 1) as i:
                body(i * 2 + 1, 1, i)
                body(i * 2 + 2, 0, i + 1)
            body(B - 1, 1, B // 2 - 1, nxt=False)
            av_copy(B - 1, KVH - 1)
            last = post_use(B, 0) + 1
            for n, name in enumerate(TAIL):
                if name == "OT":
                    ot(B - 1, last + n)
                elif name == "OUTP":
                    norm3(B - 1)
                elif name == "T3":
                    t3(B - 1, last + n)
                elif name == "ROUTER":
                    router(B - 1)
                    expert_in(B - 1, 1, B // 2 - 1)
                elif name in ("GATE0", "GATE1"):
                    gate(B - 1, last + n, int(name[4]))

            def d_xt_copy(n, r):
                act.wait_ge(s["d_xt_ps"], n + 1)
                a.copy(d_xt[r % 2][:], bank[r % 2][:, 0:P]).then_inc(s["d_xt_ready"], 1)

            def d_tanh(n, r):
                act.wait_ge(s["d_gu_ps"], n + 1)
                if not isinstance(n, int) or n >= 2:
                    act.wait_ge(s["d_hid"], n - 1)
                a.activation(d_th[r % 2][:], bank[2 + r % 2][:, 0:FE], ACT.Tanh, scale=0.5).then_inc(s["d_tanh"], 1)

            def d_slot(n, r, past):
                more = SLOTS - n if isinstance(n, int) else 3
                if more > 1:
                    d_tanh(n + 1, r + 1)
                if more > 2:
                    d_xt_copy(n + 2, r)
                act.wait_ge(s["d_ht_ps"], n + 1)
                a.copy(d_ht[r % 2][:], bank[4 + r % 2][:, 0:FE]).then_inc(s["d_ht_ready"], 1)

            d_xt_copy(0, 0)
            d_xt_copy(1, 1)
            d_tanh(0, 0)
            for n in range(OUT_R):
                d_slot(n, n, 0)
            with act.Fori(1, FULL) as i:
                for r in range(OUT_R):
                    d_slot(i * OUT_R + r, r, i)
            for n in range(FULL * OUT_R, SLOTS):
                d_slot(n, n % OUT_R, n // OUT_R)

        @block.vector
        def _(dve):
            v = nc.vector
            v.memset(ones[:], 1.0).then_inc(s["const_dve"], 1)
            v.memset(onesb[:], 1.0).then_inc(s["const_dve"], 1)
            for i in two:
                v.memset(vv[i][:], 0.0).then_inc(s["const_dve"], 1)
            v.memset(small[:], 0.0).then_inc(s["const_dve"], 1)
            v.memset(idle[:], 0.0).then_inc(s["const_dve"], 1)
            dve.wait_ge(s["const_dve"], 6)

            small_s = lambda c: small[0:NSPLAT, c:c + 1]
            dve.wait_ge(s["s_act"], 1)
            dve.wait_ge(s["w_p"], 16)
            dve.wait_ge(s["w_small"], 64)
            dve.wait_ge(s["ident_ready"], 5)
            v.tensor_tensor(squares[:], w_in["p"][:], w_in["p"][:], ALU.mult).then_inc(s["s_dve"], 1)
            v.tensor_scalar(small_s(1), small_s(0), -0.5, None, ALU.mult).then_inc(s["s_dve"], 1)
            v.tensor_tensor(small_s(4), amp[:], amp[:], ALU.mult).then_inc(s["s_dve"], 1)
            dve.wait_ge(s["s_dve"], 3)
            v.tensor_reduce(small_s(3), squares[:], AX, ALU.add).then_inc(s["s_dve"], 1)
            v.tensor_scalar(scaled_p[:], w_in["p"][:], small_s(1), -2.0, ALU.mult, ALU.mult).then_inc(s["s_dve"], 1)
            v.tensor_scalar(diag_a[:], ident[0:NSPLAT, 0:NSPLAT], small_s(1), None, ALU.mult).then_inc(s["s_dve"], 1)
            dve.wait_ge(s["s_dve"], 6)
            v.tensor_tensor(small_s(2), small_s(3), small_s(1), ALU.mult).then_inc(s["s_dve"], 1)

            dve.wait_ge(s["w_ffn"], 16)
            v.tensor_reduce(small[:, 8:9], w_in["wffn"][:], AX, ALU.add, apply_absolute_value=True).then_inc(s["beta_part"], 1)
            dve.wait_ge(s["beta_sum"], 1)
            v.tensor_scalar(small[:, 10:11], small[:, 9:10], 1.0 / (P * P), EPS_BETA, ALU.mult, ALU.add).then_inc(s["wq_ready"], 1)
            v.tensor_scalar(small[:, 5:6], small[:, 9:10], 1.0 / (P * P), None, ALU.mult).then_inc(s["wq_ready"], 1)
            dve.wait_ge(s["wq_ready"], 2)
            v.reciprocal(small[:, 7:8], small[:, 10:11]).then_inc(s["wq_ready"], 1)
            dve.wait_ge(s["wq_ready"], 3)
            v.tensor_scalar(wq_pos[:], w_in["wffn"][:], small[:, 7:8], 0.5, ALU.mult, ALU.is_gt).then_inc(s["wq_ready"], 1)
            v.tensor_scalar(wq_neg[:], w_in["wffn"][:], small[:, 7:8], -0.5, ALU.mult, ALU.is_lt).then_inc(s["wq_ready"], 1)
            dve.wait_ge(s["wq_ready"], 5)
            v.tensor_tensor(wq[:], wq_pos[:], wq_neg[:], ALU.subtract).then_inc(s["wq_ready"], 1)
            def statistics(src, st, mv, sm, at, tiles=range(TILES)):
                for j in tiles:
                    v.bn_stats(st[:, j], src(j)).then_inc(s[sm], 1)
                dve.wait_ge(s[sm], at + len(tiles))
                v.tensor_copy(idle[:, 2:3], idle[:, 1:2])
                for j in tiles:
                    v.bn_aggr(mv[:, j], st[:, j]).then_inc(s[sm], 1)

            def normalise(dst, src, mv, rstd, sm):
                for j in range(TILES):
                    v.tensor_scalar(dst[:, j], src(j), mv[:, j, 0:1], rstd[:, j:j + 1], ALU.subtract, ALU.mult)\
                     .then_inc(s[sm], 1)

            def res(b):
                if isinstance(b, int):
                    return lambda j: xres[:, b, j]
                return lambda j: xres[:, bass.ds(b, 1), j].rearrange("p a f -> p (a f)")

            def front(i):
                for q in lanes:
                    b = i * LANES + q
                    dve.wait_ge(s[f"x_loaded{q}"], i * 16 + 16)
                    statistics(res(b), a_st[q], f_mv[q], "a_stats", 8 * b)
                    dve.wait_ge(s["a_stats"], 8 * b + 8)
                    v.tensor_scalar(f_rs[q][:, 0], f_mv[q][:, :, 1], LN_EPS, None, ALU.add).then_inc(s["a_arg"], 1)

            def tables():
                for k in two:
                    v.memset(vv[k][:, :, :, HD:HD + 1], 1.0).then_inc(s["const_dve"], 1)
                v.memset(xres[:, B], 1.0).then_inc(s["const_dve"], 1)
                v.memset(zt[:, B], 0.0).then_inc(s["const_dve"], 1)
                dve.wait_ge(s["const_pool"], 13)
                v.tensor_copy(e_start[:], s_tmp[:].bitcast(I32)).then_inc(s["s_dve"], 1)
                v.tensor_copy(priority[:], ended[:].bitcast(I32)).then_inc(s["s_dve"], 1)
                v.tensor_copy(slot_no[:], s_val[:, 0:1].bitcast(I32)).then_inc(s["s_dve"], 1)
                v.tensor_copy(pad_rows[:, 2 * P:ROW].bitcast(I32), s_val[:, 1:2].bitcast(I32)).then_inc(s["pad_ready"], 1)
                dve.wait_ge(s["const_pool"], 16)
                for k in two:
                    v.memset(k8[k][64:66], 1.0).then_inc(s["const_dve"], 1)
                dve.wait_ge(s["s_dve"], 10)
                v.tensor_copy(e_base[:], e_start[:]).then_inc(s["s_dve"], 1)

            front(0)
            for i in range(ROUNDS):
                for q in lanes:
                    b = i * LANES + q
                    if i:
                        dve.wait_ge(s["a_zt_ps"], b - LANES + 1)
                    dve.wait_ge(s["a_rstd"], b + 1)
                    normalise(a_xn[q], res(b), f_mv[q], f_rs[q][:, 1], "a_xn")
                for q in lanes:
                    b = i * LANES + q
                    dve.wait_ge(s["a_d2_ps"], b + 1)
                    v.tensor_scalar(a_et[q], bank[2 * q + 1][0:NSPLAT, :], small_s(2), 0.0, ALU.add, ALU.min)\
                     .then_inc(s["a_d2"], 1)
                if i + 1 < ROUNDS:
                    front(i + 1)
                else:
                    tables()
                for q in lanes:
                    b = i * LANES + q
                    dve.wait_ge(s["a_et"], b + 1)
                    v.tensor_scalar(a_m[q][:, P:P + 1], a_sum[q][:], small_s(4), None, ALU.mult).then_inc(s["a_m"], 1)
                    dve.wait_ge(s["a_m_ps"], b + 1)
                    v.tensor_scalar(a_m[q][:, 0:P], bank[2 * q + 1][0:NSPLAT, NSPLAT:NSPLAT + P], small_s(4), None, ALU.mult)\
                     .then_inc(s["a_m"], 1)
                for q in lanes:
                    b = i * LANES + q
                    den = a_den[q]
                    for h in two:
                        dve.wait_ge(s["a_o_ps"], 2 * b + h + 1)
                        o = bank[2 * q + h][:, 0:2 * (P + 1)].rearrange("p (j f) -> p j f", j=2)
                        v.tensor_scalar(den[:, 0, 2 * h:2 * h + 2], o[:, :, P], EPS_SPLAT, None, ALU.add).then_inc(s["a_den"], 1)
                        dve.wait_ge(s["a_den"], 4 * b + 2 * h + 1)
                        v.reciprocal(den[:, 1, 2 * h:2 * h + 2], den[:, 0, 2 * h:2 * h + 2]).then_inc(s["a_den"], 1)
                        dve.wait_ge(s["a_den"], 4 * b + 2 * h + 2)
                        for j in two:
                            xb = res(b)(2 * h + j)
                            v.scalar_tensor_tensor(xb, o[:, j, 0:P], den[:, 1, 2 * h + j:2 * h + j + 1], xb, ALU.mult, ALU.add)\
                             .then_inc(s["a_x1"], 1)
                    dve.wait_ge(s["a_x1"], 4 * b + 4)
                    v.tensor_copy(idle[:, 0:1], idle[:, 1:2])
                    statistics(res(b), a_st[q], a_mv[q], "a_stats2", 8 * b)
                    dve.wait_ge(s["a_stats2"], 8 * b + 8)
                    v.tensor_scalar(a_rs[q][:, 0], a_mv[q][:, :, 1], 1.0 + FFN_LN_EPS, LN_EPS * FFN_LN_EPS, ALU.mult, ALU.add)\
                     .then_inc(s["a_arg2"], 1)
                for q in lanes:
                    b = i * LANES + q
                    dve.wait_ge(s["a_rstd2"], b + 1)
                    normalise(a_xn[q], res(b), a_mv[q], a_rs[q][:, 1], "a_zn")
                for q in lanes:
                    b = i * LANES + q
                    dve.wait_ge(s["a_zt"], b + 1)
                    v.tensor_reduce(zmax[:, b:b + 1], zt[:, b], AX, ALU.max,
                                    apply_absolute_value=True).then_inc(s["a_zmax"], 1)
            dve.wait_ge(s["a_zmax"], B)
            v.tensor_reduce(zlim[:, 0:1], zmax[:], AX, ALU.max).then_inc(s["zlim_part"], 1)
            dve.wait_ge(s["zlim_all"], 1)
            lim = float(np.float32(QB - EPS_BETA)) / QB
            v.tensor_scalar(zlim[:, 2:3], zlim[:, 1:2], lim, None, ALU.mult).then_inc(s["zlim"], 1)
            v.tensor_scalar(zlim[:, 3:4], zlim[:, 1:2], -lim, None, ALU.mult).then_inc(s["zlim"], 1)
            dve.wait_ge(s["zlim"], 2)

            def clip(b):
                if not isinstance(b, int) or b > 0:
                    dve.wait_ge(s["x2"], 8 * b - 7)
                z = zt[:, b] if isinstance(b, int) else zt[:, bass.ds(b, 1)].rearrange("p a t -> p (a t)")
                v.tensor_scalar(zc[:], z, zlim[:, 2:3], zlim[:, 3:4], ALU.min, ALU.max).then_inc(s["zclip"], 1)

            def y(b, n):
                dve.wait_ge(s["pre_full"], n + 1)
                xb = xres[:, b] if isinstance(b, int) else xres[:, bass.ds(b, 1)].rearrange("p a j f -> p (a j) f")
                v.scalar_tensor_tensor(xb, PREB[:].rearrange("p (j f) -> p j f", j=TILES), small[:, 5:6], xb, ALU.mult, ALU.add)\
                 .then_inc(s["pre_free"], 1)

            def stats2(b, half):
                if half == 0:
                    dve.wait_ge(s["pre_free"], bank_uses("Y", b))
                    v.tensor_copy(idle[:, 0:1], idle[:, 1:2])
                statistics(res(b), st2, mv2, "x2", 8 * b + 4 * half, range(2 * half, 2 * half + 2))
                if half == 0:
                    return
                dve.wait_ge(s["x2"], 8 * b + 8)
                v.tensor_scalar(rs2[:, 0], mv2[:, :, 1], LN_EPS, None, ALU.add).then_inc(s["arg2"], 1)
                v.tensor_scalar(rs2[:, 2], mv2[:, :, 0], -1.0, None, ALU.mult).then_inc(s["arg2"], 1)

            def qkv(b, par, n, hf):
                k = 2 * b + hf
                dve.wait_ge(s["pre_full"], n + 1)
                tiles = slice(2 * hf, 2 * hf + 2)
                o = PREB[:, 0:2 * (RC + KC)].rearrange("p (j f) -> p j f", j=2)
                if not isinstance(k, int) or k > 0:
                    dve.wait_ge(s["rope_add"], k)
                v.tensor_tensor(rot_c[:], o[:, :, 0:RC], rope_c[:, tiles], ALU.mult).then_inc(s["rope_mul"], 1)
                for odd in two:
                    pair = lambda t, w: t.rearrange("p j (n two) -> p j n two", two=2)[:, :, :, w]
                    v.tensor_tensor(pair(rot_s[:], odd), pair(o[:, :, 0:RC], 1 - odd), pair(rope_s[:, tiles], odd), ALU.mult)\
                     .then_inc(s["rope_mul"], 1)
                v.tensor_copy(v_next[:, tiles], o[:, :, RC:RC + KC]).then_inc(s["pre_free"], 1)

            def values(b, par, n):
                dve.wait_ge(s["pre_free"], n)
                if not isinstance(b, int) or b >= 2:
                    dve.wait_ge(s["av_ps"], 4 * KVH * (b - 1))
                v.tensor_copy(vv[par][:, :, :, 0:HD], v_next[:].rearrange("p j (h d) -> p j h d", h=KVH)).then_inc(s["v_ready"], 1)

            def row_max(b, kv, u):
                qtile, h0, nh = MAX_UNITS[u]
                k = UNITS * (KVH * b + kv) + u
                n = P * (qtile + 1)
                dve.wait_ge(s["max_ps"], k + 1)
                v.tensor_reduce(negmax[kv % 2][:, qtile, h0:h0 + nh],
                                MAXB[(kv * UNITS + u) % 2][:, 0:nh * n].rearrange("p (h n) -> p h n", h=nh),
                                AX, ALU.max, negate=True).then_inc(s["max_done"], 1)

            def shift_parts(b, kv):
                g = KVH * b + kv
                dve.wait_ge(s["max_done"], UNITS * (g + 1))
                nm, sh = negmax[kv % 2], shift[kv % 2]
                v.tensor_copy(sh[:, :, 0], nm[:]).then_inc(s["shift_split"], 1)
                dve.wait_ge(s["shift_split"], 2 * g + 1)
                v.tensor_tensor(sh[:, :, 1], nm[:], sh[:, :, 0], ALU.subtract).then_inc(s["shift_split"], 1)

            def avt(b, par, kv, n):
                g = KVH * b + kv
                dve.wait_ge(s["post_full"], n + 1)
                o = POSTB[:].rearrange("p (j h c) -> p j h c", j=TILES, h=GRP)
                v.reciprocal(rden[:], o[:, :, :, HD]).then_inc(s["o_rden"], 1)
                dve.wait_ge(s["o_rden"], g + 1)
                v.tensor_tensor(o_tok[par][:, :, KC * kv:KC * kv + KC].rearrange("p j (h d) -> p j h d", h=GRP),
                                o[:, :, :, 0:HD], rden[:].unsqueeze(3).to_broadcast([P, TILES, GRP, HD]), ALU.mult)\
                 .then_inc(s["post_free"], 1)

            def outp(b, n):
                dve.wait_ge(s["post_full"], n + 1)
                dve.wait_ge(s["xbias"], b + 1)
                xb = xres[:, b] if isinstance(b, int) else xres[:, bass.ds(b, 1)].rearrange("p a j f -> p (a j) f")
                v.tensor_tensor(xb, POSTB[:].rearrange("p (j f) -> p j f", j=TILES), xb, ALU.add).then_inc(s["post_free"], 1)

            def stats3(b, half):
                if half == 0:
                    dve.wait_ge(s["post_free"], bank_uses("OUTP", b))
                    v.tensor_copy(idle[:, 0:1], idle[:, 1:2])
                statistics(res(b), st3, mv3, "stats3", 8 * b + 4 * half, range(2 * half, 2 * half + 2))
                if half == 0:
                    return
                dve.wait_ge(s["stats3"], 8 * b + 8)
                v.tensor_scalar(rs3[:, 0], mv3[:, :, 1], LN_EPS, None, ALU.add).then_inc(s["arg3"], 1)
                v.tensor_scalar(rs3[:, 2], mv3[:, :, 0], -1.0, None, ALU.mult).then_inc(s["arg3"], 1)

            def router(b, n):
                dve.wait_ge(s["post_full"], n + 1)
                lg = POSTB[:, 0:TILES * NE].rearrange("p (j e) -> p j e", j=TILES)
                wide = lambda t: t.unsqueeze(2).to_broadcast([P, TILES, NE])
                v.tensor_reduce(lmax[:], lg, AX, ALU.max).then_inc(s["route"], 1)
                dve.wait_ge(s["route"], 5 * b + 1)
                v.tensor_tensor(top[:], lg, wide(lmax[:]), ALU.is_ge).then_inc(s["post_free"], 1)
                dve.wait_ge(s["post_free"], n + 1)
                v.tensor_tensor(top[:], top[:], priority[:].unsqueeze(1).to_broadcast([P, TILES, NE]), ALU.mult)\
                 .then_inc(s["route"], 1)
                dve.wait_ge(s["route"], 5 * b + 2)
                v.tensor_reduce(pri[:], top[:], AX, ALU.max).then_inc(s["route"], 1)
                dve.wait_ge(s["route"], 5 * b + 3)
                v.tensor_tensor(onehot[:], top[:], wide(pri[:]), ALU.is_equal).then_inc(s["route"], 1)

            def expert_in(b, par, past):
                dve.wait_ge(s["score_tanh"], b + 1)
                v.tensor_scalar(score[:, 1], score[:, 0], 0.5, 0.5, ALU.mult, ALU.add).then_inc(s["route"], 1)
                dve.wait_ge(s[f"rows_sent{par}"], 16 * TILES * past)
                num = token_no[:, b] if isinstance(b, int) else token_no[:, bass.ds(b, 1)].rearrange("p a j -> p (a j)")
                v.tensor_copy(rows[par][:, :, 2 * P].bitcast(I32), num).then_inc(s["numbered"], 1)

            def gate(b, n, hf, tail=False):
                if hf and not tail:
                    dve.wait_ge(s["pre_free"], bank_uses("UP0", b))
                dve.wait_ge(s["tanh_g"], 2 * b + hf + 1)
                v.scalar_tensor_tensor(sg[:], th[:], 1.0, POSTB[:], ALU.add, ALU.mult).then_inc(s["post_free"], 1)

            def up(b, n, hf, tail=False):
                dve.wait_ge(s["post_free"], bank_uses(f"GATE{hf}", b))
                dve.wait_ge(s["post_full" if tail else "pre_full"], n + 1)
                v.tensor_tensor(hid[:, hf], sg[:], (POSTB if tail else PREB)[:], ALU.mult)\
                 .then_inc(s["post_free" if tail else "pre_free"], 1)

            def rank(b, par, past, n):
                dve.wait_ge(s["post_full"], n + 1)
                r = POSTB[:, 0:TILES * NE].rearrange("p (j e) -> p j e", j=TILES)
                v.tensor_tensor(place[:], r, e_base[:].unsqueeze(1).to_broadcast([P, TILES, NE]), ALU.add)\
                 .then_inc(s["place_ready"], 1)
                v.tensor_copy(onehot_f[:], onehot[:]).then_inc(s["place_ready"], 1)
                dve.wait_ge(s["place_ready"], 5 * b + 2)
                v.tensor_tensor(place[:], place[:], onehot_f[:], ALU.mult).then_inc(s["place_ready"], 1)
                v.tensor_tensor(e_base[:], POSTB[:, TILES * NE:(TILES + 1) * NE], e_base[:], ALU.add)\
                 .then_inc(s["post_free"], 1)
                dve.wait_ge(s["place_ready"], 5 * b + 3)
                v.tensor_reduce(place_s[:], place[:], AX, ALU.add).then_inc(s["place_ready"], 1)
                dve.wait_ge(s["place_ready"], 5 * b + 4)
                v.tensor_copy(place_i[par][:], place_s[:]).then_inc(s["place_ready"], 1)

            def carry(b, par, n):
                dve.wait_ge(s["post_full"], n + 1)
                xb = xres[:, b] if isinstance(b, int) else xres[:, bass.ds(b, 1)].rearrange("p a j f -> p (a j) f")
                v.scalar_tensor_tensor(rows[par][:, :, P:2 * P], POSTB[:].rearrange("p (j f) -> p j f", j=TILES), 0.5, xb,
                                       ALU.mult, ALU.add).then_inc(s["post_free"], 1)

            for n, (name, b) in enumerate(HEAD):
                if name == "Y":
                    clip(b)
                    y(b, n)
                    stats2(b, 0)
                    stats2(b, 1)
                elif name in ("QKV0", "QKV1"):
                    qkv(b, b % 2, n, int(name[3]))
                    if (name, b) == ("QKV1", 0):
                        values(0, 0, n + 1)
                for u in HEAD_MAX.get((name, b), ()):
                    row_max(0, 0, u)
            shift_parts(0, 0)
            for u in range(UNITS):
                row_max(0, 1, u)

            def body(b, par, past, prev=True, nxt=True):
                steps = steps_of(plan(prev, nxt)[0], DVE_STEPS)
                before_prev = past + par - 1 if not isinstance(past, int) or prev else 0
                for kv in range(KVH):
                    for u in range(UNITS):
                        m = (b, kv + 2) if kv < 2 else (b + 1, kv - 2)
                        if kv < 2 or nxt:
                            row_max(*m, u)
                        if u == 0 and (kv < 3 or nxt):
                            shift_parts(*((b, kv + 1) if kv < 3 else (b + 1, 0)))
                        for name, _, off, n in steps.get((kv, u), ()):
                            pre, post = pre_use(b, n), post_use(b, n)
                            if name == "Y":
                                y(b + 2, pre)
                            elif name in ("QKV0", "QKV1"):
                                qkv(b + 2, par, pre, int(name[3]))
                            elif name == "AVT":
                                avt(*((b, par, kv - 1) if off == 0 else (b - 1, 1 - par, KVH - 1)), post)
                            elif name == "OUTP":
                                outp(b - 1, post)
                            elif name in ("STATS2A", "STATS2B"):
                                stats2(b + 2, "AB".index(name[6]))
                            elif name in ("STATS3A", "STATS3B"):
                                stats3(b - 1, "AB".index(name[6]))
                            elif name == "ROUTER":
                                router(b - 1, post)
                            elif name == "EXPERT_IN":
                                expert_in(b - 1, 1 - par, before_prev)
                            elif name in ("GATE0", "GATE1"):
                                gate(b - 1, post, int(name[4]))
                            elif name in ("UP0", "UP1"):
                                up(b - 1, pre, int(name[2]))
                            elif name == "RANK":
                                rank(b - 1, 1 - par, before_prev, post)
                            elif name == "DOWN":
                                carry(b - 1, 1 - par, post)
                        if (kv, u) == VALUES_AT and nxt:
                            values(b + 1, 1 - par, bank_uses("QKV1", b + 1))
                        if (kv, u) == CLIP_AT and nxt:
                            clip(b + 2)

            body(0, 0, 0, prev=False)
            with dve.Fori(0, B // 2 - 1) as i:
                body(i * 2 + 1, 1, i)
                body(i * 2 + 2, 0, i + 1)
            body(B - 1, 1, B // 2 - 1, nxt=False)
            last = post_use(B, 0)
            avt(B - 1, 1, KVH - 1, last)
            for n, name in enumerate(TAIL):
                n += last + 1
                if name == "OUTP":
                    outp(B - 1, n)
                    stats3(B - 1, 0)
                    stats3(B - 1, 1)
                elif name == "ROUTER":
                    router(B - 1, n)
                    expert_in(B - 1, 1, B // 2 - 1)
                elif name in ("GATE0", "GATE1"):
                    gate(B - 1, n, int(name[4]), tail=True)
                elif name in ("UP0", "UP1"):
                    up(B - 1, n, int(name[2]), tail=True)
                    if name == "UP0":
                        dve.wait_ge(s["table_ps"], 1)
                        v.tensor_copy(s_row[:], bank[0][0:2, 0:P]).then_inc(s["table_ready"], 1)
                elif name == "RANK":
                    rank(B - 1, 1, B // 2 - 1, n)
                    dve.wait_ge(s["post_free"], n + 1)
                    v.tensor_copy(base_i[:], e_base[0:1, :]).then_inc(s["table"], 1)
                    v.tensor_tensor(cnt[:], e_base[:], e_start[:], ALU.subtract).then_inc(s["table"], 1)
                    dve.wait_ge(s["table"], 2)
                    v.tensor_scalar(cnt_i[:], cnt[:], float(P - 1), None, ALU.add).then_inc(s["table"], 1)
                    dve.wait_ge(s["table"], 3)
                    v.tensor_scalar(ntile_i[:], cnt_i[:], P.bit_length() - 1, None, ALU.logical_shift_right).then_inc(s["table"], 1)
                    dve.wait_ge(s["table"], 4)
                    v.tensor_copy(ntile[:], ntile_i[:]).then_inc(s["table"], 1)
                    dve.wait_ge(s["table"], 5)
                    v.tensor_tensor_scan(ends[:], ones[:, 0:NE], ntile[:], 0.0, ALU.mult, ALU.add).then_inc(s["table"], 1)
                    dve.wait_ge(s["table"], 6)
                    v.tensor_scalar(ended[:], ends[:], slot_no[:, 0:1], None, ALU.is_le).then_inc(s["table"], 1)
                    dve.wait_ge(s["table"], 7)
                    v.tensor_reduce(s_val[:, 0:1], ended[:], AX, ALU.add).then_inc(s["table"], 1)
                    v.tensor_tensor(s_tmp[:], ended[:], ntile[:], ALU.mult).then_inc(s["table"], 1)
                    dve.wait_ge(s["table"], 9)
                    v.tensor_reduce(s_val[:, 1:2], s_tmp[:], AX, ALU.add).then_inc(s["table"], 1)
                    v.tensor_scalar(s_tab[:, 1:2], s_val[:, 0:1], float(NE - 1), None, ALU.min).then_inc(s["table"], 1)
                    dve.wait_ge(s["table"], 11)
                    v.tensor_tensor(s_val[:, 2:3], slot_no[:], s_val[:, 1:2], ALU.subtract).then_inc(s["table"], 1)
                    v.tensor_scalar(s_val[:, 3:4], s_val[:, 0:1], float(CAP), None, ALU.mult).then_inc(s["table"], 1)
                    dve.wait_ge(s["table"], 13)
                    v.scalar_tensor_tensor(s_val[:, 4:5], s_val[:, 2:3], float(P), s_val[:, 3:4], ALU.mult, ALU.add)\
                     .then_inc(s["table"], 1)
                    dve.wait_ge(s["table"], 14)
                    v.tensor_scalar(s_tab[:, 0:1], s_val[:, 4:5], float(NE * CAP), None, ALU.min).then_inc(s["table"], 1)
                elif name == "DOWN":
                    carry(B - 1, 1, n)

            def d_step(n, r):
                p = r % 2
                dve.wait_ge(s["d_tanh"], n + 1)
                v.scalar_tensor_tensor(d_th[p][:], d_th[p][:], 1.0, bank[2 + p][:, 0:FE], ALU.add, ALU.mult)\
                 .then_inc(s["d_sg"], 1)
                dve.wait_ge(s["d_sg"], n + 1)
                if not isinstance(n, int) or n >= 2:
                    dve.wait_ge(s["d_ht_ps"], n - 1)
                v.tensor_tensor(d_h[p][:], d_th[p][:], bank[2 + p][:, FE:2 * FE], ALU.mult).then_inc(s["d_hid"], 1)

            def d_output(n, r, past):
                dve.wait_ge(s["d_dn_ps"], n + 1)
                dve.wait_ge(s[f"out_sent{r}"], 16 * past)
                dve.wait_ge(s[f"slot_in{r}"], 16 * past + 16)
                v.scalar_tensor_tensor(d_out[r][:], bank[6 + r % 2][:, 0:P], 0.5, slot[r][:, P:2 * P], ALU.mult, ALU.add)\
                 .then_inc(s["d_out_ready"], 1)

            def d_slot(n, r, past):
                if not isinstance(n, int) or n + 1 < SLOTS:
                    d_step(n + 1, r + 1)
                if not isinstance(n, int) or n > 0:
                    back = (r - 1) % OUT_R
                    d_output(n - 1, back, past - (r == 0))

            d_step(0, 0)
            for n in range(OUT_R):
                d_slot(n, n, 0)
            with dve.Fori(1, FULL) as i:
                for r in range(OUT_R):
                    d_slot(i * OUT_R + r, r, i)
            for n in range(FULL * OUT_R, SLOTS):
                d_slot(n, n % OUT_R, n // OUT_R)
            d_output(SLOTS - 1, (SLOTS - 1) % OUT_R, (SLOTS - 1) // OUT_R)

        @block.tensor
        def _(pe):
            t = nc.tensor
            mm = lambda o, l, r, start=True, stop=True: t.matmul(o, l, r, start=start, stop=stop)
            pe.wait_ge(s["ident_ready"], 5)
            pe.wait_ge(s["w_attn"], 16 * 8)
            pe.wait_ge(s["s_dve"], 7)
            pe.wait_ge(s["w_moe"], 64)
            turn = lambda o, i: t.transpose(o, i, ident[0:i.shape[0], 0:i.shape[0]]).then_inc(s["s_pe1"], 1)
            turn(bank[0][:, 0:128], w_in["wv"][:])
            turn(bank[0][:, 128:192], scaled_p[:])
            turn(bank[0][0:64, 192:320], w_in["wqa"][:])
            turn(bank[0][0:32, 320:448], w_in["wkva"][:])
            turn(bank[0][:, 448:464], w_in["router"][:])
            for c in two:
                turn(bank[1][:, P * c:P * c + P], w_in["wg"][:, c])
                turn(bank[1][:, 256 + P * c:256 + P * c + P], w_in["wu"][:, c])
                turn(bank[2][:, P * c:P * c + P], w_in["wd"][:, P * c:P * c + P])
            pe.wait_ge(s["s_copy1"], 8)
            pe.wait_ge(s["const_dve"], 6)
            kv_cols = w_in["wkvb"][:].rearrange("p (n two) -> p n two", two=2)
            mm(bank[3][:, 0:128], wvt[:], w_in["wo"][:]).then_inc(s["s_pe2"], 1)
            mm(bank[3][:, 128:256], wqat[:], w_in["wqb"][:]).then_inc(s["s_pe2"], 1)
            mm(bank[3][:, 256:288], wkvat[:], kv_cols[:, :, 0]).then_inc(s["s_pe2"], 1)
            mm(bank[3][:, 288:320], wkvat[:], kv_cols[:, :, 1]).then_inc(s["s_pe2"], 1)
            mm(bank[3][:, 320:384], ones[0:NSPLAT, :], diag_a[:]).then_inc(s["s_pe2"], 1)
            mm(bank[3][:, 384:512], ones[0:1, :], w_in["bout"][:]).then_inc(s["s_pe2"], 1)
            pe.wait_ge(s["s_copy2"], 4)

            def turn_tiles(dst, src, idn=None):
                for j in range(TILES):
                    last = t.transpose(dst[:, P * j:P * j + P], src(j), ident[:])
                return last

            with pe.Fori(0, ROUNDS) as i:
                for q in lanes:
                    b = i * LANES + q
                    pe.wait_ge(s["a_zt"], LANES * i)
                    pe.wait_ge(s["a_xn"], 4 * b + 4)
                    turn_tiles(bank[2 * q], lambda j: a_xn[q][:, j]).then_inc(s["a_xt_ps"], 1)
                for q in lanes:
                    b = i * LANES + q
                    pe.wait_ge(s["a_xt"], 2 * b + 1)
                    mm(bank[2 * q + 1][0:NSPLAT, :], splat_t[:], a_xt[q][:], stop=False)
                    pe.wait_ge(s["a_xt"], 2 * b + 2)
                    mm(bank[2 * q + 1][0:NSPLAT, :], a_rows[:], a_sq[q][:], start=False).then_inc(s["a_d2_ps"], 1)
                for q in lanes:
                    b = i * LANES + q
                    pe.wait_ge(s["a_et"], b + 1)
                    mm(bank[2 * q][:, 0:NSPLAT], a_et[q][:, 0:P], ident[0:NSPLAT, 0:NSPLAT])
                    for j in range(1, TILES):
                        last = t.transpose(bank[2 * q][:, NSPLAT * j:NSPLAT * j + NSPLAT], a_et[q][:, P * j:P * j + P],
                                           ident[0:NSPLAT, 0:NSPLAT])
                    last.then_inc(s["a_e_ps"], 1)
                for q in lanes:
                    b = i * LANES + q
                    pe.wait_ge(s["a_e"], b + 1)
                    for j in range(TILES):
                        last = mm(bank[2 * q + 1][:, 0:NSPLAT], a_xn[q][:, j], a_e[q][:, j], j == 0, j == TILES - 1)
                    last.then_inc(s["a_gt_ps"], 1)
                for q in lanes:
                    b = i * LANES + q
                    pe.wait_ge(s["a_gt"], b + 1)
                    mm(bank[2 * q + 1][0:NSPLAT, NSPLAT:NSPLAT + P], a_gt[q][:], wvo[:]).then_inc(s["a_m_ps"], 1)
                for q in lanes:
                    b = i * LANES + q
                    pe.wait_ge(s["a_m"], 2 * b + 2)
                    for h in two:
                        for j in two:
                            tile = 2 * h + j
                            last = mm(bank[2 * q + h][:, (P + 1) * j:(P + 1) * (j + 1)], a_et[q][:, P * tile:P * tile + P], a_m[q][:])
                        last.then_inc(s["a_o_ps"], 1)
                for q in lanes:
                    b = i * LANES + q
                    pe.wait_ge(s["a_zn"], 4 * b + 4)
                    turn_tiles(bank[2 * q], lambda j: a_xn[q][:, j]).then_inc(s["a_zt_ps"], 1)
            pe.wait_ge(s["a_zt"], B)
            pe.wait_ge(s["w_rope"], 32)

            def pre_bank(n):
                if not isinstance(n, int) or n > 0:
                    pe.wait_ge(s["pre_free"], n)

            def post_bank(n):
                if not isinstance(n, int) or n > 0:
                    pe.wait_ge(s["post_free"], n)

            def y(b, n):
                pre_bank(n)
                pe.wait_ge(s["zclip"], b + 1)
                for j in range(TILES):
                    last = mm(PREB[:, P * j:P * j + P], zc[:, P * j:P * j + P], wq[:])
                last.then_inc(s["pre_full"], 1)

            def t2(b, n):
                pre_bank(n)
                pe.wait_ge(s["xn2_ready"], 4 * b + 4)
                turn_tiles(PREB, lambda j: xn2[:, j]).then_inc(s["pre_full"], 1)

            def qkv(b, n, hf):
                pre_bank(n)
                for j in two:
                    c = P * (2 * hf + j)
                    last = mm(PREB[:, (RC + KC) * j:(RC + KC) * (j + 1)], xt2[:, c:c + P], wqkv[:])
                last.then_inc(s["pre_full"], 1)

            def split_a(b, n):
                pre_bank(n)
                pe.wait_ge(s["part_lo"], 2 * b + 2)
                both = PREB[:].bitcast(BF16)
                for c in two:
                    for j in range(TILES):
                        last = t.transpose(both[:, T * c + P * j:T * c + P * j + P], parts[:, j, 0:QC, c], identb[:])
                last.then_inc(s["pre_full"], 1)

            def split_b(b, n):
                pre_bank(n)
                both = PREB[:].bitcast(BF16)
                for j in range(TILES):
                    t.transpose(both[:, P * j:P * j + P], parts[:, j, 0:QC, 2], identb[:])
                for j in range(TILES):
                    last = t.transpose(both[0:3 * KC, T + P * j:T + P * j + P], parts[:, j, QC:RC].rearrange("p k c -> p (k c)"), identb[:])
                last.then_inc(s["pre_full"], 1)

            def ct(gb, kv, n):
                pre_bank(n)
                pe.wait_ge(s["shift_split"], 2 * (KVH * gb + kv) + 2)
                both = PREB[:].bitcast(BF16)
                for j in range(TILES):
                    last = t.transpose(both[0:2 * GRP, P * j:P * j + P], shift[kv % 2][:, j], identb[:])
                last.then_inc(s["pre_full"], 1)

            def avt(b, kv, n):
                post_bank(n)
                pe.wait_ge(s["av_copied"], KVH * b + kv + 1)
                turn_tiles(POSTB, lambda j: av_sb[kv % 2][:, P * j:P * j + P]).then_inc(s["post_full"], 1)

            def ot(b, par, n):
                post_bank(n)
                turn_tiles(POSTB, lambda j: o_tok[par][:, j]).then_inc(s["post_full"], 1)

            def outp(b, n):
                post_bank(n)
                for j in range(TILES):
                    last = mm(POSTB[:, P * j:P * j + P], o_t[:, P * j:P * j + P], w_in["wout"][:])
                last.then_inc(s["post_full"], 1)

            def t3(b, n):
                post_bank(n)
                pe.wait_ge(s["xn3_ready"], 4 * b + 4)
                turn_tiles(POSTB, lambda j: xn3[:, j]).then_inc(s["post_full"], 1)

            def router(b, n):
                post_bank(n)
                for j in range(TILES):
                    last = mm(POSTB[:, NE * j:NE * j + NE], xt3[:, P * j:P * j + P], router_t[:])
                last.then_inc(s["post_full"], 1)

            def inner(b, n, w, hf, pre=False):
                (pre_bank if pre else post_bank)(n)
                mm((PREB if pre else POSTB)[:], w[:, P * hf:P * hf + P], xt3[:]).then_inc(s["pre_full" if pre else "post_full"], 1)

            def rank(b, n):
                post_bank(n)
                pe.wait_ge(s["route"], 5 * b + 4)
                for j in range(TILES):
                    o = POSTB[:, NE * j:NE * j + NE]
                    for k in range(j):
                        mm(o, onesb[:], onehot[:, k], k == 0, False)
                    mm(o, before[:], onehot[:, j], j == 0, True)
                for k in range(TILES):
                    last = mm(POSTB[:, TILES * NE:(TILES + 1) * NE], onesb[:], onehot[:, k], k == 0, k == TILES - 1)
                last.then_inc(s["post_full"], 1)

            def down_shared(b, n, tail=False):
                post_bank(n)
                if not tail:
                    pe.wait_ge(s["pre_free"], bank_uses("UP1", b))
                for j in range(TILES):
                    for c in two:
                        last = mm(POSTB[:, P * j:P * j + P], hid[:, c, P * j:P * j + P], down_t[:, c], c == 0, c == 1)
                last.then_inc(s["post_full"], 1)

            def max_unit(b, par, past, kv, u):
                qtile, h0, nh = MAX_UNITS[u]
                k = UNITS * (KVH * b + kv) + u
                if kv == 0 and u == 0:
                    pe.wait_ge(s[f"parts_loaded{par}"], 12 * 16 * past + 12 * 16)
                if not isinstance(k, int) or k >= 2:
                    pe.wait_ge(s["max_done"], k - 1)
                n = P * (qtile + 1)
                o = MAXB[(kv * UNITS + u) % 2]
                for h in range(nh):
                    q = q8[par][0:64, GRP * kv + h0 + h, P * qtile:P * qtile + P]
                    mm(o[:, n * h:n * h + n], q, k8[par][0:64, kv, 0:n], True, False)
                    last = mm(o[:, n * h + n - P:n * h + n], identb[:], causal[:], False, True)
                last.then_inc(s["max_ps"], 1)

            def score_unit(b, par, past, kv, u):
                ktile, h0, nh = SCORE_UNITS[u]
                g = KVH * b + kv
                if u == 0:
                    pe.wait_ge(s[f"shift_loaded{kv % 2}"], 16 * (2 * b + kv // 2) + 16)
                back, was = prior(u, SC_BANKS)
                if not (isinstance(b, int) and b == 0 and kv == 0) or back == 0:
                    pe.wait_ge(s["exp_done"], UNITS * (g - back) + was + 1)
                n = T - P * ktile
                o = SCB[u % SC_BANKS]
                for h in range(nh):
                    mm(o[:, n * h:n * h + n], k8[par][:, kv, P * ktile:P * ktile + P],
                       q8[par][:, GRP * kv + h0 + h, P * ktile:T], True, False)
                    last = mm(o[:, n * h:n * h + P], identb[:], causal_t[:], False, True)
                last.then_inc(s["score_ps"], 1)

            def av(b, par, kv, ktile):
                g = KVH * b + kv
                pe.wait_ge(s["exp_done"], UNITS * g + LAST_OF_TILE[ktile] + 1)
                if ktile == 0:
                    if kv == 0:
                        pe.wait_ge(s["v_ready"], b + 1)
                    if not (isinstance(b, int) and b == 0 and kv == 0):
                        pe.wait_ge(s["av_copied"], g)
                n = T - P * ktile
                for u, (kt_, h0, nh) in enumerate(SCORE_UNITS):
                    if kt_ != ktile:
                        continue
                    for h in range(nh):
                        c = 32 * (h0 + h)
                        last = t.matmul(AVB[c:c + 32, P * ktile:T], vv[par][:, ktile, kv], w_ring[u % W_RING][:, n * h:n * h + n],
                                        start=ktile == 0, stop=ktile == TILES - 1)
                last.then_inc(s["av_ps"], 1)

            for n, (name, b) in enumerate(HEAD):
                {"Y": y, "T2": t2, "SPLITA": split_a, "SPLITB": split_b}[name](b, n) if name[0] != "Q" else qkv(b, n, int(name[3]))
                for u in HEAD_MAX.get((name, b), ()):
                    max_unit(0, 0, 0, 0, u)
            ct(0, 0, HEAD_USES - 1)
            for u in range(UNITS):
                max_unit(0, 0, 0, 1, u)

            def body(b, par, past, prev=True, nxt=True):
                order, _ = plan(prev, nxt)
                for kv in range(KVH):
                    for u in range(UNITS):
                        for name, off, n in order.get((kv, u), ()):
                            pre, post = pre_use(b, n), post_use(b, n)
                            if name == "Y":
                                y(b + 2, pre)
                            elif name == "T2":
                                t2(b + 2, pre)
                            elif name in ("QKV0", "QKV1"):
                                qkv(b + 2, pre, int(name[3]))
                            elif name == "SPLITA":
                                split_a(b + 1, pre)
                            elif name == "SPLITB":
                                split_b(b + 1, pre)
                            elif name == "CT":
                                ct(b + off, CT_OF[kv], pre)
                            elif name == "AVT":
                                avt(*((b, kv - 1) if off == 0 else (b - 1, KVH - 1)), post)
                            elif name == "OT":
                                ot(b - 1, 1 - par, post)
                            elif name == "OUTP":
                                outp(b - 1, post)
                            elif name == "T3":
                                t3(b - 1, post)
                            elif name == "ROUTER":
                                router(b - 1, post)
                            elif name in ("GATE0", "GATE1"):
                                inner(b - 1, post, gate_t, int(name[4]))
                            elif name in ("UP0", "UP1"):
                                inner(b - 1, pre, up_t, int(name[2]), pre=True)
                            elif name == "RANK":
                                rank(b - 1, post)
                            elif name == "DOWN":
                                down_shared(b - 1, post)
                        if kv < 2:
                            max_unit(b, par, past, kv + 2, u)
                        elif nxt:
                            max_unit(b + 1, 1 - par, past + par, kv - 2, u)
                        score_unit(b, par, past, kv, u)
                        if u in AV_AT:
                            before_this, ktile = AV_AT[u]
                            if not before_this:
                                av(b, par, kv, ktile)
                            elif prev or kv:
                                av(*((b, par, kv - 1) if kv else (b - 1, 1 - par, KVH - 1)), ktile)

            body(0, 0, 0, prev=False)
            with pe.Fori(0, B // 2 - 1) as i:
                body(i * 2 + 1, 1, i)
                body(i * 2 + 2, 0, i + 1)
            body(B - 1, 1, B // 2 - 1, nxt=False)
            for before_this, ktile in sorted(AV_AT.values()):
                if before_this:
                    av(B - 1, 1, KVH - 1, ktile)
            last_post = post_use(B, 0)
            avt(B - 1, KVH - 1, last_post)
            for n, name in enumerate(TAIL):
                n += last_post + 1
                if name == "OT":
                    ot(B - 1, 1, n)
                elif name == "OUTP":
                    outp(B - 1, n)
                elif name == "T3":
                    t3(B - 1, n)
                elif name == "ROUTER":
                    router(B - 1, n)
                elif name in ("GATE0", "GATE1"):
                    inner(B - 1, n, gate_t, int(name[4]))
                elif name in ("UP0", "UP1"):
                    inner(B - 1, n, up_t, int(name[2]))
                    if name == "UP0":
                        pe.wait_ge(s["table"], 15)
                        t.transpose(bank[0][0:2, 0:P], s_tab[:], ident[:]).then_inc(s["table_ps"], 1)
                elif name == "RANK":
                    rank(B - 1, n)
                elif name == "DOWN":
                    down_shared(B - 1, n, tail=True)
            pe.wait_ge(s["table_ready"], 1)
            pe.wait_ge(s["post_free"], last_post + 1 + len(TAIL))
            pe.wait_ge(s["w_experts"], 32)

            def d_turn(n, r, past):
                pe.wait_ge(s[f"slot_in{r % OUT_R}"], 16 * (past + r // OUT_R) + 16)
                if not isinstance(n, int) or n >= 2:
                    pe.wait_ge(s["d_xt_ready"], n - 1)
                t.transpose(bank[r % 2][:, 0:P], slot[r % OUT_R][:, 0:P], ident[:]).then_inc(s["d_xt_ps"], 1)

            def d_gate_up(n, r, e):
                pe.wait_ge(s["d_xt_ready"], n + 1)
                if not isinstance(n, int) or n >= 2:
                    pe.wait_ge(s["d_hid"], n - 1)
                mm(bank[2 + r % 2][:], d_xt[r % 2][:], gate_up[:, bass.ds(e, 1)].rearrange("p a f -> p (a f)"))\
                  .then_inc(s["d_gu_ps"], 1)

            def d_turn_inner(n, r):
                pe.wait_ge(s["d_hid"], n + 1)
                if not isinstance(n, int) or n >= 2:
                    pe.wait_ge(s["d_ht_ready"], n - 1)
                for c in two:
                    last = t.transpose(bank[4 + r % 2][:, P * c:P * c + P], d_h[r % 2][:, P * c:P * c + P], ident[:])
                last.then_inc(s["d_ht_ps"], 1)

            def d_down(n, r, e):
                pe.wait_ge(s["d_ht_ready"], n + 1)
                if not isinstance(n, int) or n >= 2:
                    pe.wait_ge(s["d_out_ready"], n - 1)
                for c in two:
                    last = mm(bank[6 + r % 2][:, 0:P], d_ht[r % 2][:, P * c:P * c + P],
                              down[:, bass.ds(e, 1), c].rearrange("p a f -> p (a f)"), c == 0, c == 1)
                last.then_inc(s["d_dn_ps"], 1)

            def d_slots(i, count=OUT_R):
                numbers = {}

                def expert(k):
                    if k not in numbers:
                        numbers[k] = pe.value_load(s_row[1:2, bass.ds(i * OUT_R + k, 1)], min_val=0, max_val=NE - 1)
                    return numbers[k]

                for r in range(count):
                    n = i * OUT_R + r
                    more = SLOTS - n if isinstance(n, int) else 3
                    if more > 1:
                        d_gate_up(n + 1, r + 1, expert(r + 1))
                    if more > 2:
                        expert(r + 2)
                        d_turn(n + 2, r + 2, i)
                    if not isinstance(n, int) or n > 0:
                        expert(r - 1)
                    d_turn_inner(n, r)
                    if not isinstance(n, int) or n > 0:
                        d_down(n - 1, r + 1, expert(r - 1))

            d_turn(0, 0, 0)
            d_turn(1, 1, 0)
            d_gate_up(0, 0, pe.value_load(s_row[1:2, 0:1], min_val=0, max_val=NE - 1))
            d_slots(0)
            with pe.Fori(1, FULL) as i:
                d_slots(i)
            d_slots(FULL, SLOTS - FULL * OUT_R)
            d_down(SLOTS - 1, (SLOTS - 1) % OUT_R, pe.value_load(s_row[1:2, SLOTS - 1:SLOTS], min_val=0, max_val=NE - 1))


_NAMES = {"x": "L0_attn_token_embeddings", "p": "L0_attn_splat_positions", "logs": "L0_attn_splat_log_scales",
          "amp": "L0_attn_splat_amplitudes", "wv": "L0_attn_Wv", "wo": "L0_attn_Wo", "wffn": "L0_ffn_weight",
          "gamma": "L0_ffn_ln_gamma", "beta": "L0_ffn_ln_beta", "wqa": "L1_attn_Wqa", "wqb": "L1_attn_Wqb",
          "wkva": "L1_attn_Wkva", "wkvb": "L1_attn_Wkvb", "wout": "L1_attn_Wout", "bout": "L1_attn_bout",
          "router": "L1_ffn_w_router", "gate_up": "L1_ffn_gate_up_proj", "down": "L1_ffn_down_proj",
          "wg": "L1_ffn_w_gate", "wu": "L1_ffn_w_up", "wd": "L1_ffn_w_down"}


def rope_tables():
    inv = (1.0 / 10000.0 ** (np.arange(0, HD, 2, dtype=np.float32) / np.float32(HD))).astype(np.float32)
    ang = np.outer(np.arange(T, dtype=np.float32), inv).astype(np.float32)
    cos = np.repeat(np.cos(ang), 2, axis=1)
    sin = np.repeat(np.sin(ang), 2, axis=1) * np.tile([-1.0, 1.0], HD // 2)
    out = []
    for t in (cos, sin):
        full = np.concatenate([np.tile(t, (1, H)) * HD ** -0.5, np.tile(t, (1, KVH))], axis=1)
        out.append(np.ascontiguousarray(full.reshape(TILES, P, RC).transpose(1, 0, 2).astype(np.float32)))
    return out


def kernel(**inputs):
    import numpy as _np
    import concourse.bacc as _bacc
    from concourse.bass_utils import run_bass_kernel_spmd as _run

    nc = _bacc.Bacc("TRN2", target_bir_lowering=False, num_devices=1)
    rope_c, rope_s = rope_tables()
    arrays = {n: _np.ascontiguousarray(inputs[full]) for n, full in _NAMES.items()} | {"rope_c": rope_c, "rope_s": rope_s}
    ins = {n: nc.dram_tensor(f"in_{n}", a.shape, mybir.dt.from_np(a.dtype), kind="ExternalInput").ap()
           for n, a in arrays.items()}
    out = nc.dram_tensor("out_rows", (B, T, P), F32, kind="ExternalOutput").ap()
    build(nc, ins, out)
    r = _run(nc, [{f"in_{n}": a for n, a in arrays.items()}], core_ids=[0])
    return r.results[0]["out_rows"]
```
